# Optimizing a Trainium2 kernel written in Bass

```python
import numpy as np
import jax
import jax.numpy as jnp

def _softmax(x, axis=-1):
    return jax.nn.softmax(x, axis=axis)

def _gelu(x):
    return jax.nn.gelu(x, approximate=True)

def _silu(x):
    return jax.nn.silu(x)

def _sigmoid(x):
    return jax.nn.sigmoid(x)

def _layernorm(x, axis=-1, eps=1e-05):
    m = jnp.mean(x, axis=axis, keepdims=True)
    v = jnp.var(x, axis=axis, keepdims=True)
    return (x - m) / jnp.sqrt(v + eps)

def _scatter_add(tgt, idx, src, axis=0):
    return tgt.at[idx].add(src)

def _segment_sum(src, seg, n):
    return jax.ops.segment_sum(src, seg, n)
kernel_name = 'mk_gnn_preln_d4_gnn_r16_deaa73'

def setup_inputs(seed: int=0):
    np.random.seed(seed)
    _w = jnp.asarray

    def _rec_inputs():
        import jax
        import jax.numpy as jnp
        _gk = jax.random.key(seed)
        x = -0.0005121 + 1.001 * jax.random.normal(jax.random.fold_in(_gk, 1), (6250, 64), jnp.float32)
        _s = jax.random.randint(jax.random.fold_in(_gk, 2), (100000,), 0, 6250, jnp.int32)
        _d = jax.random.randint(jax.random.fold_in(_gk, 3), (100000,), 0, 6250, jnp.int32)
        _loop = jnp.arange(6250, dtype=jnp.int32)
        src = jnp.concatenate([_s, _d, _loop])
        dst = jnp.concatenate([_d, _s, _loop])
        _o = jnp.argsort(dst, stable=True)
        src = src[_o]
        dst = dst[_o]
        edge_attr_32 = 0.000196303 + 1.00016 * jax.random.normal(jax.random.fold_in(_gk, 12), (206250, 32), jnp.float32)
        return (x, src, dst, edge_attr_32)
    x, src, dst, edge_attr_32 = _rec_inputs()

    def _L0_gnn_setup():
        import jax, jax.numpy as jnp
        import numpy as np
        N_NODES = 3125
        N_EDGES = 50000
        F_NODE = 64
        F_EDGE = 32
        F_GLOBAL = 32
        OUT_DIM = 64
        N_GRAPHS = 256
        key = jax.random.key(seed)
        ks = jax.random.split(key, 8)
        x = jax.random.normal(ks[0], (N_NODES, F_NODE), dtype=jnp.float32)
        edge_index = jax.random.randint(ks[1], (2, N_EDGES), 0, N_NODES, dtype=jnp.int64)
        edge_attr = jax.random.normal(ks[2], (N_EDGES, F_EDGE), dtype=jnp.float32)
        u = jax.random.normal(ks[3], (N_GRAPHS, F_GLOBAL), dtype=jnp.float32)
        batch = jnp.sort(jax.random.randint(ks[4], (N_NODES,), 0, N_GRAPHS, dtype=jnp.int64))
        W1 = jax.random.normal(ks[5], (F_NODE + F_EDGE, OUT_DIM), dtype=jnp.float32) / np.sqrt(F_NODE + F_EDGE)
        b1 = jnp.zeros((OUT_DIM,), dtype=jnp.float32)
        W2 = jax.random.normal(ks[6], (F_NODE + OUT_DIM + F_GLOBAL, OUT_DIM), dtype=jnp.float32) / np.sqrt(F_NODE + OUT_DIM + F_GLOBAL)
        b2 = jnp.zeros((OUT_DIM,), dtype=jnp.float32)
        return {'x': x, 'edge_index': edge_index, 'edge_attr': edge_attr, 'u': u, 'batch': batch, 'W1': W1, 'b1': b1, 'W2': W2, 'b2': b2}
    _L0_gnn_all = _L0_gnn_setup()
    _L0_gnn_in = {k: v for k, v in _L0_gnn_all.items() if k in ('u', 'W1', 'b1', 'W2', 'b2')}
    del _L0_gnn_all

    def _L1_gnn_setup():
        import jax, jax.numpy as jnp
        import numpy as np
        N_NODES = 6250
        HIDDEN = 64
        NUM_LAYERS = 3

        def _gcn_norm(edge_index, num_nodes):
            row, col = (edge_index[0], edge_index[1])
            deg = jax.ops.segment_sum(jnp.ones(row.shape[0], jnp.float32), col, num_segments=num_nodes)
            dinv = jnp.where(deg > 0, jax.lax.rsqrt(jnp.maximum(deg, 1.0)), 0.0)
            return dinv[row] * dinv[col]
        key = jax.random.key(seed)
        ks = jax.random.split(key, 2 + 2 * NUM_LAYERS)
        x = jax.random.normal(ks[0], (N_NODES, HIDDEN), dtype=jnp.float32)
        edge_index = jax.random.randint(ks[1], (2, 100000), 0, N_NODES, dtype=jnp.int64)
        inp = {'x': x, 'edge_index': edge_index}
        scale = 1.0 / np.sqrt(HIDDEN)
        for i in range(NUM_LAYERS):
            inp[f'W{i}'] = jax.random.normal(ks[2 + 2 * i], (HIDDEN, HIDDEN), dtype=jnp.float32) * scale
            inp[f'b{i}'] = jnp.zeros((HIDDEN,), dtype=jnp.float32)
        return inp
    _L1_gnn_all = _L1_gnn_setup()
    _L1_gnn_in = {k: v for k, v in _L1_gnn_all.items() if k in ('W0', 'b0', 'W1', 'b1', 'W2', 'b2')}
    del _L1_gnn_all

    def _L2_gnn_setup():
        import jax, jax.numpy as jnp
        import numpy as np
        N_NODES = 6250
        N_EDGES = 78125
        D_FEAT = 64
        key = jax.random.key(seed)
        k1, k2 = jax.random.split(key)
        edge_index = jax.random.randint(k1, (2, N_EDGES), 0, N_NODES, dtype=jnp.int64)
        x = jax.random.normal(k2, (N_NODES, D_FEAT), dtype=jnp.float32)
        return {'edge_index': edge_index, 'x': x}
    _L2_gnn_all = _L2_gnn_setup()
    _L2_gnn_in = {k: v for k, v in _L2_gnn_all.items() if k in ()}
    del _L2_gnn_all

    def _L3_gnn_setup():
        import jax, jax.numpy as jnp
        import numpy as np
        N = 3125
        E = 50000
        D = 64

        def _gcn_layer(h, src, dst, coef, W, b, n):
            h = h @ W
            msg = h[src] * coef[:, None]
            return jax.ops.segment_sum(msg, dst, num_segments=n) + b
        key = jax.random.key(seed)
        ks = jax.random.split(key, 8)
        x = jax.random.normal(ks[0], (N, D), dtype=jnp.float32)
        edge_index = jax.random.randint(ks[1], (2, E), 0, N)
        s = 1.0 / np.sqrt(D)
        W1 = jax.random.normal(ks[2], (D, D), dtype=jnp.float32) * s
        W2 = jax.random.normal(ks[3], (D, D), dtype=jnp.float32) * s
        W3 = jax.random.normal(ks[4], (D, D), dtype=jnp.float32) * s
        b1 = jnp.zeros((D,), jnp.float32)
        b2 = jnp.zeros((D,), jnp.float32)
        b3 = jnp.zeros((D,), jnp.float32)
        return {'x': x, 'edge_index': edge_index, 'W1': W1, 'b1': b1, 'W2': W2, 'b2': b2, 'W3': W3, 'b3': b3}
    _L3_gnn_all = _L3_gnn_setup()
    _L3_gnn_in = {k: v for k, v in _L3_gnn_all.items() if k in ('W1', 'b1', 'W2', 'b2', 'W3', 'b3')}
    del _L3_gnn_all
    return {'x': x, 'src': src, 'dst': dst, 'edge_attr_32': edge_attr_32, 'L0_gnn_u': _L0_gnn_in['u'], 'L0_gnn_W1': _L0_gnn_in['W1'], 'L0_gnn_b1': _L0_gnn_in['b1'], 'L0_gnn_W2': _L0_gnn_in['W2'], 'L0_gnn_b2': _L0_gnn_in['b2'], 'L1_gnn_W0': _L1_gnn_in['W0'], 'L1_gnn_b0': _L1_gnn_in['b0'], 'L1_gnn_W1': _L1_gnn_in['W1'], 'L1_gnn_b1': _L1_gnn_in['b1'], 'L1_gnn_W2': _L1_gnn_in['W2'], 'L1_gnn_b2': _L1_gnn_in['b2'], 'L3_gnn_W1': _L3_gnn_in['W1'], 'L3_gnn_b1': _L3_gnn_in['b1'], 'L3_gnn_W2': _L3_gnn_in['W2'], 'L3_gnn_b2': _L3_gnn_in['b2'], 'L3_gnn_W3': _L3_gnn_in['W3'], 'L3_gnn_b3': _L3_gnn_in['b3']}

def reference(x, src, dst, edge_attr_32, L0_gnn_u, L0_gnn_W1, L0_gnn_b1, L0_gnn_W2, L0_gnn_b2, L1_gnn_W0, L1_gnn_b0, L1_gnn_W1, L1_gnn_b1, L1_gnn_W2, L1_gnn_b2, L3_gnn_W1, L3_gnn_b1, L3_gnn_W2, L3_gnn_b2, L3_gnn_W3, L3_gnn_b3):
    import jax
    import jax.numpy as jnp

    def _L0_gnn_ref(x, edge_index, edge_attr, u, batch, W1, b1, W2, b2):
        import jax, jax.numpy as jnp
        import numpy as np
        N_NODES = 3125
        N_EDGES = 50000
        F_NODE = 64
        F_EDGE = 32
        F_GLOBAL = 32
        OUT_DIM = 64
        N_GRAPHS = 256
        dest, src = (edge_index[0], edge_index[1])
        edge_info = jnp.concatenate([x[src], edge_attr], axis=1)
        edge_messages = jax.nn.relu(edge_info @ W1 + b1)
        aggregated = jax.ops.segment_sum(edge_messages, dest, num_segments=x.shape[0])
        node_info = jnp.concatenate([x, aggregated, u[batch]], axis=1)
        return jax.nn.relu(node_info @ W2 + b2)

    def _L1_gnn_ref(x, edge_index, W0, b0, W1, b1, W2, b2):
        import jax, jax.numpy as jnp
        import numpy as np
        N_NODES = 6250
        HIDDEN = 64
        NUM_LAYERS = 3

        def _gcn_norm(edge_index, num_nodes):
            row, col = (edge_index[0], edge_index[1])
            deg = jax.ops.segment_sum(jnp.ones(row.shape[0], jnp.float32), col, num_segments=num_nodes)
            dinv = jnp.where(deg > 0, jax.lax.rsqrt(jnp.maximum(deg, 1.0)), 0.0)
            return dinv[row] * dinv[col]
        row, col = (edge_index[0], edge_index[1])
        n = x.shape[0]
        norm = _gcn_norm(edge_index, n)
        for W, b in ((W0, b0), (W1, b1), (W2, b2)):
            h = x @ W
            msg = h[row] * norm[:, None]
            agg = jax.ops.segment_sum(msg, col, num_segments=n)
            x = jax.nn.relu(agg + b)
        return x

    def _L2_gnn_ref(edge_index, x):
        import jax, jax.numpy as jnp
        import numpy as np
        N_NODES = 6250
        N_EDGES = 78125
        D_FEAT = 64
        row, col = (edge_index[0], edge_index[1])
        messages = x[col]
        aggr_out = jax.ops.segment_sum(messages, row, num_segments=x.shape[0])
        return aggr_out

    def _L3_gnn_ref(x, edge_index, W1, b1, W2, b2, W3, b3):
        import jax, jax.numpy as jnp
        import numpy as np
        N = 3125
        E = 50000
        D = 64

        def _gcn_layer(h, src, dst, coef, W, b, n):
            h = h @ W
            msg = h[src] * coef[:, None]
            return jax.ops.segment_sum(msg, dst, num_segments=n) + b
        n = x.shape[0]
        loop = jnp.arange(n, dtype=edge_index.dtype)
        src = jnp.concatenate([edge_index[0], loop])
        dst = jnp.concatenate([edge_index[1], loop])
        deg = jax.ops.segment_sum(jnp.ones_like(dst, dtype=x.dtype), dst, num_segments=n)
        dinv = jnp.where(deg > 0, jax.lax.rsqrt(deg), 0.0)
        coef = dinv[src] * dinv[dst]
        h = jax.nn.relu(_gcn_layer(x, src, dst, coef, W1, b1, n))
        h = jax.nn.relu(_gcn_layer(h, src, dst, coef, W2, b2, n))
        return _gcn_layer(h, src, dst, coef, W3, b3, n)
    edge_index = jnp.stack([src, dst])
    batch0 = jnp.zeros((6250,), jnp.int32)
    h = jnp.maximum(_layernorm(x, axis=-1), 0.0)
    x = x + _L0_gnn_ref(h, edge_index, edge_attr_32, L0_gnn_u, batch0, L0_gnn_W1, L0_gnn_b1, L0_gnn_W2, L0_gnn_b2)
    h = jnp.maximum(_layernorm(x, axis=-1), 0.0)
    x = x + _L1_gnn_ref(h, edge_index, L1_gnn_W0, L1_gnn_b0, L1_gnn_W1, L1_gnn_b1, L1_gnn_W2, L1_gnn_b2)
    h = jnp.maximum(_layernorm(x, axis=-1), 0.0)
    x = x + _L2_gnn_ref(edge_index, h)
    h = jnp.maximum(_layernorm(x, axis=-1), 0.0)
    x = x + _L3_gnn_ref(h, edge_index, L3_gnn_W1, L3_gnn_b1, L3_gnn_W2, L3_gnn_b2, L3_gnn_W3, L3_gnn_b3)
    return x

_drawn_inputs = setup_inputs


def setup_inputs(seed=0):
    import zlib

    import numpy as np

    out = dict(_drawn_inputs(seed))
    spreads = {'L0_gnn_b1': (0.0, 0.1),
     'L0_gnn_b2': (0.0, 0.464),
     'L1_gnn_b0': (0.0, 0.8),
     'L1_gnn_b1': (0.0, 0.8),
     'L1_gnn_b2': (0.0, 0.529),
     'L3_gnn_b1': (0.0, 0.8),
     'L3_gnn_b2': (0.0, 0.8),
     'L3_gnn_b3': (0.0, 2.0)}
    factors = {'L3_gnn_W1': 5.872, 'L3_gnn_W2': 5.257, 'L3_gnn_W3': 4.087}
    for name, (base, spread) in spreads.items():
        noise = np.random.default_rng([zlib.crc32(name.encode()), seed]).standard_normal(out[name].shape)
        drawn = base * np.exp(spread * noise) if base else spread * noise
        out[name] = jnp.asarray(drawn.astype(out[name].dtype))
    for name, factor in factors.items():
        out[name] = (out[name] * factor).astype(out[name].dtype)
    return out
```

```python
from contextlib import ExitStack

import concourse.bass as bass
from concourse import mybir

P = 128
N = 6250
E = 206250
D = 64
FE = 32
FG = 32
NB = -(-N // P)
NP = NB * P
LAST = N - (NB - 1) * P
GT = 4
UN = 4
T = -(-E // (P * GT * UN)) * GT * UN
NG = T // GT
EP = P * T
PADNODE = 8191
ROW = FE + 4
C_SLO, C_DLO, C_SRC, C_DST = FE, FE + 1, FE + 2, FE + 3
CAP = P
J = NB + 1
SLOTS = NP * J
OVB = SLOTS
ROWS = SLOTS + EP
BIG = 1.0e6
PARTS = 3
ZW = PARTS * D
SG = -(-J // GT)
NS = 4
EPS = 1e-5

F32 = mybir.dt.float32
BF16 = mybir.dt.bfloat16
I32 = mybir.dt.int32
ALU = mybir.AluOpType
ACT = mybir.ActivationFunctionType
AX = mybir.AxisListType.X


class Names:
    pass


class Chain:

    def __init__(self, eng, sem, base):
        self.eng, self.sem, self.base, self.n = eng, sem, base, 0

    def __call__(self, ins, apart=False):
        self.n += 1
        ins.then_inc(self.sem, 1)
        (wait_apart if apart else wait)(self.eng, self.sem, self.base + self.n)


def looped(eng, count, unroll, body):
    for n in range(min(unroll, count)):
        body(n, n)
    rounds = count // unroll
    if rounds > 2:
        with eng.Fori(1, rounds) as i:
            for q in range(unroll):
                body(i * unroll + q, q)
    else:
        for n in range(unroll, rounds * unroll):
            body(n, n % unroll)
    for n in range(max(rounds, 1) * unroll, count):
        body(n, n % unroll)


def wait(eng, sem, value):
    if isinstance(value, int) and value <= 0:
        return
    eng.wait_ge(sem, value)


def wait_apart(eng, sem, value):
    if isinstance(value, int):
        return wait(eng, sem, value)
    value = eng.to_reg(value)
    eng.wait_ge(sem, 1)
    eng.wait_ge(sem, value)


def build(nc, t):
    with ExitStack() as ctx:
        k = Names()
        k.inp = t

        def sb(name, shape, dt=F32):
            return ctx.enter_context(nc.sbuf_tensor(name, shape, dt))

        k.sem = lambda name: ctx.enter_context(nc.semaphore(name))
        k.bank = [ctx.enter_context(nc.psum_tensor(f"bank{i}", [P, 512], F32)) for i in range(8)]

        k.rows_d = nc.dram_tensor("rows_d", (ROWS, ROW), F32, kind="Internal").ap()
        k.a_d = nc.dram_tensor("a_d", (NB, P, J * P), BF16, kind="Internal").ap()
        k.at_d = nc.dram_tensor("at_d", (NB, P, J * P), BF16, kind="Internal").ap()
        k.z_d = nc.dram_tensor("z_d", (NP, D), F32, kind="Internal").ap()
        k.ov_d = nc.dram_tensor("ov_d", (NP, D), F32, kind="Internal").ap()
        k.degov_d = nc.dram_tensor("degov_d", (NP, 1), F32, kind="Internal").ap()

        k.xres = sb("xres", [P, NB, D])
        k.h0 = sb("h0", [P, NB, D])
        k.agg0 = sb("agg0", [P, NB, D])
        k.zf = sb("zf", [P, NB, D])
        k.ovf = sb("ovf", [P, NB, D])
        k.z3a = sb("z3a", [P, NB, PARTS, D], BF16)
        k.z3b = sb("z3b", [P, NB, PARTS, D], BF16)
        k.deg = sb("deg", [P, NB])
        k.degov = sb("degov", [P, NB])
        k.degp = sb("degp", [P, SG, NB])
        k.dinv1 = sb("dinv1", [P, NB])
        k.dinv3 = sb("dinv3", [P, NB])
        k.dtmp = sb("dtmp", [P, NB])
        k.iota = sb("iota", [P, P])
        k.ident = sb("ident", [P, P])
        k.identb = sb("identb", [P, P], BF16)
        k.notbefore = sb("notbefore", [P, P], BF16)
        k.negfrom = sb("negfrom", [P, P], BF16)
        k.onesb = sb("onesb", [P, P], BF16)
        k.ones4 = sb("ones4", [P, GT])
        k.epsc = sb("epsc", [P, 1])
        k.minus1 = sb("minus1", [P, 1])
        k.w1n = sb("w1n", [D, D])
        k.w1e4 = sb("w1e4", [P, GT, D])
        k.w2na = sb("w2na", [P, D])
        k.w2u = sb("w2u", [FG, D])
        k.u0 = sb("u0", [FG, 1])
        k.u0b = sb("u0b", [FG, P])
        k.c2 = sb("c2", [P, D])
        k.wl = sb("wl", [D, 5, D])
        k.w3 = sb("w3", [D, D])
        k.bias = sb("bias", [P, 8, D])
        k.cat = sb("cat", [P, 2, P])
        k.catT = sb("catT", [P, P])
        k.lin_in = sb("lin_in", [P, 2, D])
        k.linT = sb("linT", [D, P])
        k.aggt = sb("aggt", [P, 2, D])
        k.st6 = sb("st6", [P, 6])
        k.mv = sb("mv", [P, 2])
        k.std = sb("std", [P, 1])
        k.rstd = sb("rstd", [P, 1])
        k.rem = sb("rem", [P, D])
        k.outb = sb("outb", [P, 2, D])
        k.nov = sb("nov", [P, 1], I32)
        k.ovmeta = sb("ovmeta", [1, 2], I32)
        k.ovrow = sb("ovrow", [1, FE])
        k.ovmsg = sb("ovmsg", [1, D])
        k.ovp = sb("ovp", [1, D])
        k.one1 = sb("one1", [1, 1])
        words = max(12 * T + 80, NS * J * P // 2)
        k.arena = sb("arena", [P, words])
        k.rowbuf = sb("rowbuf", [P, UN, GT, ROW])
        k.ab = sb("ab", [P, 2, GT, P], BF16)
        k.abT = sb("abT", [P, 2, GT, P], BF16)
        k.run = sb("run", [P, D], BF16)
        k.intra = sb("intra", [P, 2, GT])
        k.junk = sb("junk", [P, GT * P], BF16)
        k.pick = sb("pick", [P, GT, D])
        k.sel = sb("sel", [P, GT])
        k.rank = sb("rank", [P, GT])
        k.over = sb("over", [P, 2, GT], BF16)
        k.second = sb("second", [P, GT])
        k.pos = sb("pos", [P, GT])
        k.ovseen = sb("ovseen", [P, 2, GT])
        k.ovpos = sb("ovpos", [P, GT])
        k.posi = sb("posi", [P, UN, GT], I32)
        prologue(nc, k)
        bucket_stage(nc, k)
        edge_stage(nc, k)
        first_overflow(nc, k)
        node_stage(nc, k)
        layers(nc, k)



def layer_norm(dve, act_sem, std_sem, count, link, k, src, dst):
    link(dve.bn_stats(k.st6[:, :], src), apart=True)
    dve.bn_aggr(k.mv[:, :], k.st6[:, :]).then_inc(act_sem, 1)
    dve.wait_ge(std_sem, count)
    link(dve.reciprocal(k.rstd[:, :], k.std[:, :]))
    link(dve.tensor_scalar(dst, src, k.mv[:, 0:1], k.rstd[:, 0:1], ALU.subtract, ALU.mult))
    return dve.tensor_scalar(dst, dst, 0.0, None, ALU.max)


def split3(pool, link, z, rem, parts):
    link(pool.tensor_copy(parts[0], z), apart=True)
    link(pool.tensor_tensor(rem, z, parts[0], ALU.subtract), apart=True)
    link(pool.tensor_copy(parts[1], rem), apart=True)
    return pool.tensor_tensor(parts[2], rem, parts[1], ALU.subtract)


def block_of(tile, b):
    return tile[:, bass.ds(b, 1), :].rearrange("p o f -> p (o f)")


def parts_of(tile, b):
    return [tile[:, bass.ds(b, 1), i, :].rearrange("p o f -> p (o f)") for i in range(PARTS)]


def node_rows(dram):
    return dram.rearrange("(b p) f -> p b f", p=P)



def prologue(nc, k):
    words = k.arena[:, :]
    k.ab_val = words[:, 0:2 * (T + GT)]
    o = 2 * (T + GT)
    k.meta = words[:, o:o + 4 * T]
    o += 4 * T
    k.pos0 = words[:, o:o + T]
    k.cap = words[:, o + T:o + 2 * T]
    k.hop = words[:, o + 2 * T:o + 3 * T]
    k.srci = words[:, o + 3 * T:o + 4 * T].bitcast(I32)
    k.dsti = words[:, o + 4 * T:o + 5 * T].bitcast(I32)

    k.slotrow = k.z3b[:, :, :, :].rearrange("p b i f -> p (b i f)").bitcast(F32)[:, 0:J * ROW]
    s = {n: k.sem(n) for n in ("p_x", "p_idx", "p_w", "p_clear", "p_const", "p_c", "p_k", "p_slot", "p_zero",
                               "p_ln", "p_std", "p_in", "p_tr", "p_trs", "p_mm", "p_z", "p_split", "p_u", "p_c2")}
    tr, mm, cps = k.bank[0], k.bank[1:3], k.bank[3]
    meta = k.meta.rearrange("p (t c) -> p t c", c=4)
    metai = meta.bitcast(I32)
    abv = k.ab_val.rearrange("p (t c) -> p t c", c=2)

    with nc.Block() as block:

        @block.sync
        def _(sp):
            x = k.inp["x"]
            sp.wait_ge(s["p_zero"], 1)
            sp.dma_start(k.xres[:, 0:NB - 1, :], x[0:(NB - 1) * P].rearrange("(b p) f -> p b f", p=P)
                         ).then_inc(s["p_x"], 16)
            sp.dma_start(k.xres[0:LAST, NB - 1, :], x[(NB - 1) * P:N]).then_inc(s["p_x"], 16)
            sp.dma_start(k.srci, k.inp["src"]).then_inc(s["p_idx"], 16)
            sp.dma_start(k.dsti, k.inp["dst"]).then_inc(s["p_idx"], 16)
            sp.dma_start(k.w1n[:, :], k.inp["L0_gnn_W1"][0:D]).then_inc(s["p_w"], 16)
            for j in range(GT):
                sp.dma_start(k.w1e4[FE * j:FE * (j + 1), j, :], k.inp["L0_gnn_W1"][D:D + FE]).then_inc(s["p_w"], 16)
            sp.dma_start(k.w2na[:, :], k.inp["L0_gnn_W2"][0:P]).then_inc(s["p_w"], 16)
            sp.dma_start(k.w2u[:, :], k.inp["L0_gnn_W2"][P:P + FG]).then_inc(s["p_w"], 16)
            sp.dma_start(k.u0[:, :], k.inp["u0_in"]).then_inc(s["p_w"], 16)
            for i, w in enumerate((k.inp["L1_gnn_W0"], k.inp["L1_gnn_W1"], k.inp["L1_gnn_W2"], k.inp["L3_gnn_W1"], k.inp["L3_gnn_W2"])):
                sp.dma_start(k.wl[:, i, :], w).then_inc(s["p_w"], 16)
            for i, b in enumerate((k.inp["L0_gnn_b1"], k.inp["L0_gnn_b2"], k.inp["L1_gnn_b0"], k.inp["L1_gnn_b1"], k.inp["L1_gnn_b2"],
                                   k.inp["L3_gnn_b1"], k.inp["L3_gnn_b2"], k.inp["L3_gnn_b3"])):
                sp.dma_start(k.bias[:, i, :], b.partition_broadcast(P)).then_inc(s["p_w"], 16)
            sp.dma_start(k.w3[:, :], k.inp["L3_gnn_W3"]).then_inc(s["p_w"], 16)
            sp.wait_ge(s["p_slot"], 2)
            for b in range(NB):
                sp.dma_start(k.rows_d[b * P * J:(b + 1) * P * J].rearrange("(p j) c -> p (j c)", p=P),
                             k.slotrow).then_inc(s["p_clear"], 16)
            sp.dma_start(node_rows(k.ov_d), k.ovf[:, :, :]).then_inc(s["p_clear"], 16)
            with nc.allow_non_contiguous_dma(reason="one word per node"):
                sp.dma_start(k.degov_d.rearrange("(b p) f -> p (b f)", p=P), k.degov[:, :]).then_inc(s["p_clear"], 16)
            sp.wait_ge(s["p_clear"], 16 * (NB + 2))

        @block.gpsimd
        def _(pool):
            link = Chain(pool, s["p_k"], 0)
            link(pool.iota(k.iota[:, :], [[1, P]], base=0, channel_multiplier=0, allow_small_or_imprecise_dtypes=True))
            link(pool.memset(k.ident[:, :], 0.0))
            link(pool.affine_select(out=k.ident[:, :], in_=k.ident[:, :], compare_op=ALU.not_equal, fill=1.0, base=0,
                                    pattern=[[-1, P]], channel_multiplier=1))
            pool.tensor_copy(k.identb[:, :], k.ident[:, :])
            link(pool.memset(k.notbefore[:, :], -2.0))
            link(pool.affine_select(out=k.notbefore[:, :], in_=k.notbefore[:, :], compare_op=ALU.is_ge, fill=0.0,
                                    base=0, pattern=[[1, P]], channel_multiplier=-1))
            link(pool.memset(k.negfrom[:, :], -1.0))
            link(pool.affine_select(out=k.negfrom[:, :], in_=k.negfrom[:, :], compare_op=ALU.is_ge, fill=0.0,
                                    base=0, pattern=[[-1, P]], channel_multiplier=1))
            pool.memset(k.one1[:, :], 1.0)
            pool.memset(k.onesb[:, :], 1.0).then_inc(s["p_const"], 1)

            def split(b, q):
                wait_apart(pool, s["p_z"], b + 1)
                sub = Chain(pool, s["p_split"], 4 * b)
                sub(split3(pool, sub, block_of(k.zf, b), k.rem[:, :], parts_of(k.z3a, b)))

            looped(pool, NB, 2, split)

        @block.tensor
        def _(pe):
            pe.wait_ge(s["p_const"], 1)
            pe.wait_ge(s["p_w"], 16 * WLOADS)
            pe.wait_ge(s["p_u"], 1)
            pe.matmul(cps[:, 0:D], k.u0b[:, :], k.w2u[:, :], start=True, stop=True).then_inc(s["p_c2"], 1)

            def step(b, q):
                wait_apart(pe, s["p_in"], b + 1)
                pe.transpose(tr[0:D, 0:P], k.lin_in[:, q, :], k.ident[:, :]).then_inc(s["p_tr"], 1)
                pe.wait_ge(s["p_trs"], b + 1)
                pe.matmul(mm[q][:, 0:D], k.linT[:, :], k.w1n[:, :], start=True, stop=True
                          ).then_inc(s["p_mm"], 1)

            looped(pe, NB, 2, step)

        @block.scalar
        def _(act):
            act.wait_ge(s["p_slot"], 2)
            def step(b, q):
                act.wait_ge(s["p_ln"], b + 1)
                act.activation(k.std[:, :], k.mv[:, 1:2], ACT.Sqrt, bias=k.epsc[:, :]).then_inc(s["p_std"], 1)
                act.wait_ge(s["p_tr"], b + 1)
                act.copy(k.linT[:, :], tr[0:D, 0:P]).then_inc(s["p_trs"], 1)

            looped(act, NB, 2, step)

        @block.vector
        def _(dve):
            link = Chain(dve, s["p_c"], 0)
            link(dve.memset(k.w1e4[:, :, :], 0.0))
            dve.memset(k.xres[:, NB - 1, :], 0.0).then_inc(s["p_zero"], 1)
            link(dve.memset(k.slotrow, 0.0))
            dve.memset(k.slotrow.rearrange("p (j c) -> p j c", c=ROW)[:, :, C_SLO:C_DLO + 1], -1.0
                       ).then_inc(s["p_slot"], 1)
            dve.memset(k.ovf[:, :, :], 0.0)
            dve.memset(k.epsc[:, :], EPS)
            dve.memset(k.minus1[:, :], -1.0)
            dve.memset(k.run[:, :], 0.0)
            dve.memset(k.ones4[:, :], 1.0)
            dve.memset(k.ovseen[:, :, :], 0.0)
            dve.memset(k.agg0[:, :, :], 0.0)
            dve.memset(k.degov[:, :], 0.0).then_inc(s["p_slot"], 1)
            dve.wait_ge(s["p_idx"], 32)
            link(dve.memset(k.ab_val[:, 2 * T:], 0.0))
            for c, v in ((0, k.srci), (1, k.dsti)):
                tmp = k.pos0.bitcast(I32)
                link(dve.tensor_copy(metai[:, :, 2 + c], v))
                link(dve.tensor_scalar(tmp, v, 7, None, ALU.logical_shift_right))
                link(dve.tensor_copy(abv[:, 0:T, c], tmp))
                link(dve.tensor_scalar(tmp, v, P - 1, None, ALU.bitwise_and))
                link(dve.tensor_copy(meta[:, :, c], tmp))
            a, b = abv[:, 0:T, 0], abv[:, 0:T, 1]
            link(dve.tensor_tensor(k.cap, a, b, ALU.is_equal))
            link(dve.tensor_scalar(k.cap, k.cap, float(CAPD - CAPO), float(CAPO), ALU.mult, ALU.add))
            link(dve.tensor_scalar(k.hop, a, float(NB), BIG, ALU.is_ge, ALU.mult))
            link(dve.tensor_tensor(k.cap, k.cap, k.hop, ALU.add))
            link(dve.scalar_tensor_tensor(k.pos0, b, float(P * J), k.hop, ALU.mult, ALU.add))
            link(dve.tensor_tensor(k.pos0, k.pos0, a, ALU.add))
            link(dve.tensor_scalar(k.hop, a, -1.0, float(NB - P * J), ALU.mult, ALU.add))
            dve.wait_ge(s["p_w"], 16 * WLOADS)
            dve.tensor_copy(k.u0b[:, :], k.u0[:, 0:1].to_broadcast([FG, P])).then_inc(s["p_u"], 1)
            dve.wait_ge(s["p_c2"], 1)
            link(dve.tensor_tensor(k.c2[:, :], cps[:, 0:D], k.bias[:, 1, :], ALU.add))
            dve.wait_ge(s["p_x"], 32)
            first = link.n

            def norm(b, q):
                sub = Chain(dve, s["p_c"], first + 4 * b)
                ins = layer_norm(dve, s["p_ln"], s["p_std"], b + 1, sub, k, block_of(k.xres, b), block_of(k.h0, b))
                sub(ins, apart=True)
                wait_apart(dve, s["p_tr"], b - 1)
                dve.tensor_copy(k.lin_in[:, q, :], block_of(k.h0, b)).then_inc(s["p_in"], 1)

            def table(b, q):
                dve.wait_ge(s["p_mm"], b + 1)
                dve.tensor_tensor(block_of(k.zf, b), mm[q][:, 0:D], k.bias[:, 0, :], ALU.add
                                  ).then_inc(s["p_z"], 1)

            def step(b, q):
                norm(b, q)
                if not (isinstance(b, int) and b == 0):
                    table(b - 1, 1 - q)

            looped(dve, NB, 2, step)
            table(NB - 1, (NB - 1) % 2)



def bucket_stage(nc, k):
    loaded = [k.sem(f"row_loaded{q}") for q in range(UN)]
    scattered = [k.sem(f"row_scattered{q}") for q in range(UN)]
    s = {n: k.sem(n) for n in ("onehot", "onehot_t", "onehot_ts", "same", "intra", "counted", "run", "over", "ovcount",
                               "pos", "b_c")}
    abv = k.ab_val.rearrange("p (t c) -> p t c", c=2)
    meta = k.meta.rearrange("p (t c) -> p t c", c=4).bitcast(I32)
    LINKS = 10

    turned = k.bank[0][:, 0:256].bitcast(BF16).rearrange("p (j e) -> p j e", j=GT)
    same = [k.bank[1][:, 0:P], k.bank[1][:, P:3 * P], k.bank[2][:, 0:3 * P], k.bank[3][:, 0:4 * P]]
    shared = 2
    ovbefore, ovtotal = k.bank[6][:, 0:GT], k.bank[6][:, GT:2 * GT]

    def picked(q):
        return k.bank[4 + q][:, 0:GT * D].rearrange("p (j f) -> p j f", j=GT)

    def counts(q):
        return k.bank[4 + q][:, GT * D:(GT + 1) * D]

    with nc.Block() as block:

        @block.sync
        def _(sp):
            def load(n, q):
                wait(sp, scattered[q], 16 * GT * (n // UN) if isinstance(n, int) else (n - q) * 16)
                sp.dma_start(k.rowbuf[:, q, :, :], k.inp["edge_rows"][:, bass.ds(n * GT, GT), :]).then_inc(loaded[q], 16)

            looped(sp, NG, UN, load)
            for q in range(UN):
                sp.wait_ge(scattered[q], 16 * GT * (NG // UN))

        @block.gpsimd
        def _(pool):
            limit = pool.to_reg(ROWS - 1)

            def scatter(n, q):
                wait_apart(pool, s["pos"], n + 1)
                for j in range(GT):
                    pool.indirect_dma_start(k.rows_d, bass.IndirectOffsetOnAxis(ap=k.posi[:, q, j:j + 1], axis=0),
                                            k.rowbuf[:, q, j, :], None, bounds_check=limit, oob_is_err=False
                                            ).then_inc(scattered[q], 16)

            looped(pool, NG, UN, scatter)

        @block.tensor
        def _(pe):
            def turn(n, q):
                pe.wait_ge(s["onehot"], n + 1)
                wait(pe, s["onehot_ts"], n)
                for j in range(GT):
                    ins = pe.transpose(turned[:, j, :], k.ab[:, q, j, :], k.identb[:, :])
                ins.then_inc(s["onehot_t"], 1)

            def step(n, u):
                q = u % 2
                pe.wait_ge(s["onehot_ts"], n + 1)
                for j in range(GT):
                    if j != shared - 1:
                        last = max(j + 1, shared) - GT
                        wait(pe, s["intra"], GT * n + last)
                    out = same[j]
                    pe.matmul(out, k.abT[:, q, j, :], k.abT[:, q, 0:j + 1, :].rearrange("p j e -> p (j e)"),
                              start=True, stop=False)
                    pe.matmul(out[:, j * P:(j + 1) * P], k.identb[:, :], k.notbefore[:, :], start=False, stop=True
                              ).then_inc(s["same"], 1)
                turn(n + 1, 1 - q)
                wait(pe, s["over"], n - 1)
                wait(pe, s["run"], n)
                for j in range(GT):
                    pe.matmul(picked(q)[:, j, :], k.abT[:, q, j, :], k.run[:, :], start=True, stop=True)
                for j in range(GT):
                    ins = pe.matmul(counts(q), k.ab[:, q, j, :], k.ab[:, q, j, D:2 * D],
                                    start=(j == 0), stop=(j == GT - 1))
                ins.then_inc(s["counted"], 1)
                pe.wait_ge(s["over"], n + 1)
                wait(pe, s["pos"], n)
                pe.matmul(ovbefore, k.negfrom[:, :], k.over[:, q, :], start=True, stop=True)
                pe.matmul(ovtotal, k.onesb[:, :], k.over[:, q, :], start=True, stop=True).then_inc(s["ovcount"], 1)

            turn(0, 0)
            looped(pe, NG, UN, step)

        @block.scalar
        def _(act):
            def keep(n, q):
                wait(act, s["counted"], n - 1)
                act.wait_ge(s["onehot_t"], n + 1)
                act.copy(k.abT[:, q, :, :], turned).then_inc(s["onehot_ts"], 1)

            def step(n, u):
                q = u % 2
                wait(act, s["over"], n - 1)
                for j in range(GT):
                    if j:
                        act.wait_ge(s["intra"], GT * n + j)
                    act.wait_ge(s["same"], GT * n + max(j + 1, shared))
                    act.activation(k.junk[:, 0:(j + 1) * P], same[j], ACT.Relu, bias=k.minus1[:, :],
                                   accum_out=k.intra[:, q, j:j + 1]).then_inc(s["intra"], 1)
                keep(n + 1, 1 - q)

            keep(0, 0)
            looped(act, NG, UN, step)

        @block.vector
        def _(dve):
            def onehot(n, q):
                wait(dve, s["counted"], n - 1)
                val = k.ab_val[:, bass.ds(n * 2 * GT, 2 * GT)]
                dve.tensor_tensor(k.ab[:, q, :, :].rearrange("p j (c e) -> p (j c) e", c=2),
                                  k.iota[:, 0:D].unsqueeze(1).to_broadcast([P, 2 * GT, D]),
                                  val.unsqueeze(2).to_broadcast([P, 2 * GT, D]), ALU.is_equal
                                  ).then_inc(s["onehot"], 1)

            def step(n, u):
                q = u % 2
                link = Chain(dve, s["b_c"], n * LINKS)
                tiles = bass.ds(n * GT, GT)
                onehot(n + 1, 1 - q)
                dve.wait_ge(s["counted"], n + 1)
                dve.tensor_tensor(k.run[0:D, :], counts(q)[0:D, :], k.run[0:D, :], ALU.add).then_inc(s["run"], 1)
                link(dve.tensor_tensor(k.pick[:, :, :], picked(q), k.ab[:, q, :, D:2 * D], ALU.mult))
                link(dve.tensor_reduce(k.sel[:, :], k.pick[:, :, :], AX, ALU.add))
                dve.wait_ge(s["intra"], GT * n + GT)
                link(dve.tensor_tensor(k.rank[:, :], k.sel[:, :], k.intra[:, q, :], ALU.add))
                dve.tensor_tensor(k.over[:, q, :], k.rank[:, :], k.cap[:, tiles], ALU.is_ge).then_inc(s["over"], 1)
                link(dve.scalar_tensor_tensor(k.second[:, :], k.rank[:, :], float(P), k.hop[:, tiles],
                                              ALU.is_ge, ALU.mult))
                link(dve.scalar_tensor_tensor(k.pos[:, :], k.rank[:, :], float(J), k.pos0[:, tiles],
                                              ALU.mult, ALU.add))
                link(dve.tensor_tensor(k.pos[:, :], k.pos[:, :], k.second[:, :], ALU.add))
                dve.wait_ge(loaded[u], 16 * (n // UN) + 16 if isinstance(n, int) else (n - u) * (16 // UN) + 16)
                dve.tensor_copy(k.rowbuf[:, u, :, :].bitcast(I32)[:, :, C_SLO:ROW], meta[:, tiles, :])
                dve.wait_ge(s["ovcount"], n + 1)
                link(dve.tensor_tensor_scan(k.ovseen[:, q, :], k.ones4[:, :], ovtotal, k.ovseen[:, 1 - q, GT - 1:GT],
                                            ALU.mult, ALU.add))
                link(dve.scalar_tensor_tensor(k.ovpos[:, :], ovbefore, float(OVB), k.ovseen[:, q, :],
                                              ALU.add, ALU.add))
                link(dve.tensor_tensor(k.ovpos[:, :], k.ovpos[:, :], k.pos[:, :], ALU.subtract))
                link(dve.tensor_tensor(k.ovpos[:, :], k.ovpos[:, :], k.over[:, q, :], ALU.mult))
                dve.tensor_tensor(k.posi[:, u, :], k.pos[:, :], k.ovpos[:, :], ALU.add).then_inc(s["pos"], 1)
                assert link.n == LINKS

            onehot(0, 0)
            looped(dve, NG, UN, step)
            dve.tensor_copy(k.nov[:, :], k.ovseen[:, (NG - 1) % 2, GT - 1:GT])



def edge_buffers(k):
    at = [0]

    def take(shape, dt):
        n = 1
        for d in shape:
            n *= d
        words = n if dt == F32 else n // 2
        part = k.arena[:, at[0]:at[0] + words]
        at[0] += words
        names = "abcd"[:len(shape)]
        return (part if dt == F32 else part.bitcast(dt)).rearrange(
            f"p ({' '.join(names)}) -> p {' '.join(names)}", **dict(zip(names, shape)))

    k.strip = take((2, J, ROW), F32)
    k.oh = take((SG, GT * 2, P), BF16).rearrange("p g (j e) c -> p g j e c", e=2)
    k.attr = take((2, GT * FE), F32)
    k.dT = take((2, GT, P), BF16)
    k.eT = take((2, P), F32)
    k.atile = take((SG, GT, P), BF16)
    k.attile = take((SG, GT, P), BF16)
    k.msg = take((2, GT, D), F32)
    k.msgrem = take((GT, D), F32)
    k.msg3 = take((2, GT, PARTS, D), BF16)


class Group:

    def __init__(self, b, r, g):
        self.b, self.r, self.g = b, r, g
        self.n, self.q, self.m = SG * b + g, (SG * r + g) % 2, min(GT, J - GT * g)


def edge_stage(nc, k):
    edge_buffers(k)
    strip = [k.sem(f"strip{q}") for q in range(2)]
    a_out = [k.sem(f"a_out{g}") for g in range(SG)]
    at_out = [k.sem(f"at_out{g}") for g in range(SG)]
    s = {n: k.sem(n) for n in ("lanes", "packed", "turned", "a_sum", "at_sum", "e_t", "d_t", "a_kept", "at_kept", "gathered",
                               "message", "parts", "summed", "added", "e_k", "e_c")}

    def group(b, r, g, back=0):
        if g - back < 0:
            b, r, g = b - 1, 1 - r, g + SG
        g -= back
        if isinstance(b, int) and not 0 <= b < NB:
            return None
        return Group(b, r, g)

    a_ps, at_ps, e_t = k.bank[0], k.bank[1], k.bank[3][:, 0:P]
    d_t = k.bank[2][:, 0:256].bitcast(BF16).rearrange("p (j e) -> p j e", j=GT)

    def gat(q):
        return k.bank[4 + q][:, 0:GT * D]

    def tot(q):
        return k.bank[6 + q][:, 0:GT * D].rearrange("p (j f) -> p j f", j=GT)

    def strip_loaded(b, r):
        return 16 * (b // 2) + 16 if isinstance(b, int) else (b - r) * 8 + 16

    with nc.Block() as block:

        @block.sync
        def _(sp):
            def load(b, r):
                src = k.rows_d[bass.ds(b * (P * J), P * J), :] if not isinstance(b, int) else \
                    k.rows_d[b * P * J:(b + 1) * P * J]
                sp.dma_start(k.strip[:, r, :, :], src.rearrange("(p j) c -> p j c", p=P)).then_inc(strip[r], 16)

            def step(b, r, more=True):
                for g in range(SG):
                    t = group(b, r, g)
                    sp.wait_ge(s["a_kept"], t.n + 1)
                    sp.dma_start(k.a_d[bass.ds(b, 1), :, GT * P * g:GT * P * g + t.m * P].rearrange("o p c -> p (o c)"),
                                 k.atile[:, g, 0:t.m, :].rearrange("p j c -> p (j c)")).then_inc(a_out[g], 16)
                    sp.wait_ge(s["at_kept"], t.n + 1)
                    cols = bass.ds(b * P, P)
                    own = t.m if g < SG - 1 else t.m - 1
                    sp.dma_start(k.at_d[GT * g:GT * g + own, :, cols].rearrange("a p c -> p a c"),
                                 k.attile[:, g, 0:own, :]).then_inc(at_out[g], 16)
                    if g == SG - 1:
                        sp.dma_start(k.at_d[bass.ds(b, 1), :, NB * P:J * P].rearrange("o p c -> p (o c)"),
                                     k.attile[:, g, t.m - 1, :]).then_inc(at_out[g], 16)
                if more:
                    sp.wait_ge(s["packed"], SG * b + SG)
                    sp.wait_ge(s["lanes"], SG * b + SG)
                    load(b + 2, r)

            load(0, 0)
            load(1, 1)
            looped(sp, NB - 2, 2, step)
            for b in (NB - 2, NB - 1):
                step(b, b % 2, more=False)
            for g in range(SG):
                sp.wait_ge(a_out[g], 16 * NB)
                sp.wait_ge(at_out[g], 16 * NB * (2 if g == SG - 1 else 1))

        @block.tensor
        def _(pe):
            def front(t):
                wait_apart(pe, s["lanes"], t.n + 1)
                wait(pe, s["e_t"], t.n)
                wait(pe, s["d_t"], t.n)
                pe.wait_ge(s["packed"], t.n + 1)
                pe.transpose(e_t[0:t.m * FE, :], k.attr[:, t.q, 0:t.m * FE], k.ident[:, :])
                for j in range(t.m):
                    ins = pe.transpose(d_t[:, j, :], k.oh[:, t.g, j, 1, :], k.identb[:, :])
                ins.then_inc(s["turned"], 1)
                wait(pe, s["a_kept"], t.n)
                for j in range(t.m):
                    ins = pe.matmul(a_ps[:, j * P:(j + 1) * P], k.oh[:, t.g, j, 0, :], k.oh[:, t.g, j, 1, :],
                                    start=True, stop=True)
                ins.then_inc(s["a_sum"], 1)
                wait(pe, s["at_kept"], t.n)
                for j in range(t.m):
                    ins = pe.matmul(at_ps[:, j * P:(j + 1) * P], k.oh[:, t.g, j, 1, :], k.oh[:, t.g, j, 0, :],
                                    start=True, stop=True)
                ins.then_inc(s["at_sum"], 1)

            def gather(t):
                if t is None:
                    return
                table = parts_of(k.z3a, t.b)
                pe.wait_ge(s["e_t"], t.n + 1)
                pe.wait_ge(s["d_t"], t.n + 1)
                wait(pe, s["message"], t.n - 1)
                for j in range(t.m):
                    out = gat(t.q)[:, j * D:(j + 1) * D]
                    for i in range(PARTS):
                        pe.matmul(out, k.dT[:, t.q, j, :], table[i], start=(i == 0), stop=False)
                    ins = pe.matmul(out, k.eT[:, t.q, :], k.w1e4[:, j, :], start=False, stop=True)
                ins.then_inc(s["gathered"], 1)

            def total(t):
                if t is None:
                    return
                pe.wait_ge(s["parts"], t.n + 1)
                wait(pe, s["added"], t.n - 1)
                for j in range(t.m):
                    for i in range(PARTS):
                        ins = pe.matmul(tot(t.q)[:, j, :], k.oh[:, t.g, j, 0, :], k.msg3[:, t.q, j, i, :],
                                        start=(i == 0), stop=(i == PARTS - 1))
                ins.then_inc(s["summed"], 1)

            def step(b, r):
                for g in range(SG):
                    front(group(b, r, g))
                    gather(group(b, r, g, 1))
                    total(group(b, r, g, 2))

            looped(pe, NB, 2, step)
            last = (NB - 1, (NB - 1) % 2, SG - 1)
            gather(group(*last))
            total(group(*last, 1))
            total(group(*last))

        @block.scalar
        def _(act):
            def message(t):
                if t is None:
                    return
                act.wait_ge(s["gathered"], t.n + 1)
                wait(act, s["parts"], t.n - 1)
                act.activation(k.msg[:, t.q, 0:t.m, :].rearrange("p j f -> p (j f)"), gat(t.q)[:, 0:t.m * D], ACT.Relu
                               ).then_inc(s["message"], 1)

            def step(b, r):
                for g in range(SG):
                    t = group(b, r, g)
                    act.wait_ge(s["turned"], t.n + 1)
                    wait(act, s["gathered"], t.n - 1)
                    act.copy(k.dT[:, t.q, 0:t.m, :], d_t[:, 0:t.m, :]).then_inc(s["d_t"], 1)
                    act.wait_ge(s["a_sum"], t.n + 1)
                    wait(act, a_out[g], b * 16)
                    act.copy(k.atile[:, g, 0:t.m, :].rearrange("p j c -> p (j c)"), a_ps[:, 0:t.m * P]
                             ).then_inc(s["a_kept"], 1)
                    act.wait_ge(s["at_sum"], t.n + 1)
                    wait(act, at_out[g], b * (32 if g == SG - 1 else 16))
                    act.activation(k.attile[:, g, 0:t.m, :].rearrange("p j c -> p (j c)"), at_ps[:, 0:t.m * P],
                                   ACT.Copy, accum_out=k.degp[:, g, bass.ds(b, 1)]).then_inc(s["at_kept"], 1)
                    message(group(b, r, g, 1))

            looped(act, NB, 2, step)
            message(group(NB - 1, (NB - 1) % 2, SG - 1))

        @block.gpsimd
        def _(pool):
            def pack(t):
                if t is None:
                    return
                if t.g == 0:
                    wait_apart(pool, strip[t.r], strip_loaded(t.b, t.r))
                wait_apart(pool, s["turned"], t.n - 1)
                pool.tensor_copy(k.attr[:, t.q, 0:t.m * FE].rearrange("p (j c) -> p j c", c=FE),
                                 k.strip[:, t.r, GT * t.g:GT * t.g + t.m, 0:FE]).then_inc(s["packed"], 1)

            def split(t):
                if t is None:
                    return
                link = Chain(pool, s["e_k"], 3 * t.n)
                wait_apart(pool, s["message"], t.n + 1)
                wait_apart(pool, s["summed"], t.n - 1)
                split3(pool, link, k.msg[:, t.q, 0:t.m, :], k.msgrem[:, 0:t.m, :],
                       [k.msg3[:, t.q, 0:t.m, i, :] for i in range(PARTS)]).then_inc(s["parts"], 1)

            def step(b, r):
                for g in range(SG):
                    pack(group(b, r, g))
                    split(group(b, r, g, 1))

            looped(pool, NB, 2, step)
            split(group(NB - 1, (NB - 1) % 2, SG - 1))

        @block.vector
        def _(dve):
            def lanes(t):
                if t.g == 0:
                    dve.wait_ge(strip[t.r], strip_loaded(t.b, t.r))
                wait(dve, s["summed"], SG * (t.b - 1) + t.g + 1 if not (isinstance(t.b, int) and t.b == 0) else 0)
                val = k.strip[:, t.r, GT * t.g:GT * t.g + t.m, C_SLO:C_DLO + 1]
                dve.tensor_tensor(k.oh[:, t.g, 0:t.m, :, :],
                                  k.iota[:, :].unsqueeze(1).unsqueeze(1).to_broadcast([P, t.m, 2, P]),
                                  val.unsqueeze(3).to_broadcast([P, t.m, 2, P]), ALU.is_equal).then_inc(s["lanes"], 1)

            def keep_e(t):
                if t is None:
                    return
                dve.wait_ge(s["turned"], t.n + 1)
                wait(dve, s["gathered"], t.n - 1)
                dve.tensor_copy(k.eT[0:t.m * FE, t.q, :], e_t[0:t.m * FE, :]).then_inc(s["e_t"], 1)

            def add(t):
                if t is None:
                    return
                dve.wait_ge(s["summed"], t.n + 1)
                wait(dve, s["added"], t.n)
                if t.g < SG - 1:
                    own = k.agg0[:, GT * t.g:GT * t.g + t.m, :]
                    dve.tensor_tensor(own, tot(t.q)[:, 0:t.m, :], own, ALU.add).then_inc(s["added"], 1)
                else:
                    link = Chain(dve, s["e_c"], t.b)
                    own = k.agg0[:, GT * t.g:GT * t.g + t.m - 1, :]
                    link(dve.tensor_tensor(own, tot(t.q)[:, 0:t.m - 1, :], own, ALU.add))
                    own = block_of(k.agg0, t.b)
                    dve.tensor_tensor(own, tot(t.q)[:, t.m - 1, :], own, ALU.add).then_inc(s["added"], 1)

            def step(b, r):
                for g in range(SG):
                    lanes(group(b, r, g))
                    keep_e(group(b, r, g, 1))
                    add(group(b, r, g, 3))

            looped(dve, NB, 2, step)
            last = (NB - 1, (NB - 1) % 2, SG - 1)
            keep_e(group(*last))
            for back in (2, 1, 0):
                add(group(*last, back))



def drained(pool, sem):
    pool.wait_ge(sem, 16)
    pool.dma_reset(range(sem.num, sem.num + 1))
    pool.sem_clear(sem)


def overflow_ends(pool, k, i, sem):
    pool.dma_start(k.ovmeta[:, :], k.rows_d[bass.ds(i + OVB, 1), C_SRC:C_DST + 1].bitcast(I32)).then_inc(sem, 16)
    drained(pool, sem)
    return pool.value_load(k.ovmeta[0:1, 0:1]), pool.value_load(k.ovmeta[0:1, 1:2])


def overflow_sum(pool, k, sem, transposed):
    nov = pool.value_load(k.nov[0:1, 0:1])
    with pool.If(nov > 0):
        pool.dma_start(node_rows(k.z_d), k.zf[:, :, :]).then_inc(sem, 16)
        drained(pool, sem)
        with pool.Fori(0, nov) as i:
            src, dst = overflow_ends(pool, k, i, sem)
            frm, to = (dst, src) if transposed else (src, dst)
            pool.dma_start(k.ov_d[bass.ds(to, 1), :], k.z_d[bass.ds(frm, 1), :], accum_op=ALU.add).then_inc(sem, 16)
            drained(pool, sem)
        overflow_take(pool, k, sem)


def overflow_take(pool, k, sem):
    pool.dma_start(k.ovf[:, :, :], node_rows(k.ov_d)).then_inc(sem, 16)
    drained(pool, sem)
    pool.memset(k.h0[:, :, :], 0.0).then_inc(k.s_ovz, 1)
    pool.wait_ge(k.s_ovz, 1)
    pool.sem_clear(k.s_ovz)
    pool.dma_start(node_rows(k.ov_d), k.h0[:, :, :]).then_inc(sem, 16)
    drained(pool, sem)


def first_overflow(nc, k):
    sem, step = k.sem("ov_dma"), k.sem("ov_step")
    k.s_ovz = k.sem("ov_zero")
    with nc.Block() as block:

        @block.gpsimd
        def _(pool):
            def link(ins):
                ins.then_inc(step, 1)
                pool.wait_ge(step, 1)
                pool.sem_clear(step)

            w1e = k.arena[0:1, 0:D * FE].rearrange("p (f c) -> p f c", c=FE)
            prod = k.arena[0:1, D * FE:2 * D * FE].rearrange("p (f c) -> p f c", c=FE)
            nov = pool.value_load(k.nov[0:1, 0:1])
            with pool.If(nov > 0):
                pool.dma_start(w1e, k.inp["w1eT_in"]).then_inc(sem, 16)
                drained(pool, sem)
                pool.dma_start(node_rows(k.z_d), k.zf[:, :, :]).then_inc(sem, 16)
                drained(pool, sem)
                with pool.Fori(0, nov) as i:
                    src, dst = overflow_ends(pool, k, i, sem)
                    pool.dma_start(k.ovrow[:, :], k.rows_d[bass.ds(i + OVB, 1), 0:FE]).then_inc(sem, 16)
                    drained(pool, sem)
                    pool.dma_start(k.ovp[:, :], k.z_d[bass.ds(dst, 1), :]).then_inc(sem, 16)
                    drained(pool, sem)
                    link(pool.tensor_tensor(prod, w1e,
                                            k.ovrow[:, :].unsqueeze(1).to_broadcast([1, D, FE]), ALU.mult))
                    w = FE // 2
                    while w:
                        link(pool.tensor_tensor(prod[:, :, 0:w], prod[:, :, 0:w], prod[:, :, w:2 * w], ALU.add))
                        w //= 2
                    link(pool.tensor_tensor(k.ovmsg[:, :], prod[:, :, 0], k.ovp[:, :], ALU.add))
                    link(pool.tensor_scalar(k.ovmsg[:, :], k.ovmsg[:, :], 0.0, None, ALU.max))
                    pool.dma_start(k.ov_d[bass.ds(src, 1), :], k.ovmsg[:, :], accum_op=ALU.add).then_inc(sem, 16)
                    drained(pool, sem)
                    pool.dma_start(k.degov_d[bass.ds(dst, 1), :], k.one1[:, :], accum_op=ALU.add).then_inc(sem, 16)
                    drained(pool, sem)
                pool.dma_start(k.ovf[:, :, :], node_rows(k.ov_d)).then_inc(sem, 16)
                drained(pool, sem)
                with nc.allow_non_contiguous_dma(reason="one word per node, with overflow edges only"):
                    pool.dma_start(k.degov[:, :], k.degov_d.rearrange("(b p) f -> p (b f)", p=P)).then_inc(sem, 16)
                drained(pool, sem)
                link(pool.memset(k.zf[:, :, :], 0.0))
                pool.dma_start(node_rows(k.ov_d), k.zf[:, :, :]).then_inc(sem, 16)
                drained(pool, sem)



def node_stage(nc, k):
    s = {n: k.sem(n) for n in ("n_cat", "n_tr", "n_trs", "n_mm", "n_ln", "n_std", "n_in", "n_tr2", "n_trs2", "n_mm2",
                               "n_z", "n_split", "n_c", "n_deg", "n_root", "n_root3")}
    tr, tr2, mm, mm2 = k.bank[0], k.bank[1], k.bank[2:4], k.bank[4:6]
    w0 = k.wl[:, 0, :]

    with nc.Block() as block:

        @block.tensor
        def _(pe):
            def first(b, q):
                pe.wait_ge(s["n_cat"], b + 1)
                pe.transpose(tr[:, 0:P], k.cat[:, q, :], k.ident[:, :]).then_inc(s["n_tr"], 1)
                pe.wait_ge(s["n_trs"], b + 1)
                pe.matmul(mm[q][:, 0:D], k.catT[:, :], k.w2na[:, :], start=True, stop=True
                          ).then_inc(s["n_mm"], 1)

            def second(b, q):
                wait_apart(pe, s["n_in"], b + 1)
                pe.transpose(tr2[0:D, 0:P], k.lin_in[:, q, :], k.ident[:, :]).then_inc(s["n_tr2"], 1)
                pe.wait_ge(s["n_trs2"], b + 1)
                pe.matmul(mm2[q][:, 0:D], k.linT[:, :], w0, start=True, stop=True
                          ).then_inc(s["n_mm2"], 1)

            def step(b, q):
                first(b, q)
                if not (isinstance(b, int) and b == 0):
                    second(b - 1, 1 - q)

            looped(pe, NB, 2, step)
            second(NB - 1, (NB - 1) % 2)

        @block.scalar
        def _(act):
            act.wait_ge(s["n_deg"], 1)
            act.activation(k.dinv1[:, :], k.dtmp[:, :], ACT.Sqrt).then_inc(s["n_root"], 1)
            act.wait_ge(s["n_deg"], 2)
            act.activation(k.dinv3[:, :], k.degp[:, 0, :], ACT.Sqrt).then_inc(s["n_root"], 1)

            def first(b):
                act.wait_ge(s["n_tr"], b + 1)
                act.copy(k.catT[:, :], tr[:, 0:P]).then_inc(s["n_trs"], 1)

            def second(b):
                act.wait_ge(s["n_ln"], b + 1)
                act.activation(k.std[:, :], k.mv[:, 1:2], ACT.Sqrt, bias=k.epsc[:, :]).then_inc(s["n_std"], 1)
                act.wait_ge(s["n_tr2"], b + 1)
                act.copy(k.linT[:, :], tr2[0:D, 0:P]).then_inc(s["n_trs2"], 1)

            def step(b, q):
                first(b)
                if not (isinstance(b, int) and b == 0):
                    second(b - 1)

            looped(act, NB, 2, step)
            second(NB - 1)

        @block.vector
        def _(dve):
            link = Chain(dve, s["n_c"], 0)
            link(dve.tensor_reduce(k.deg[:, :], k.degp[:, :, :].rearrange("p g b -> p b g"), AX, ALU.add))
            link(dve.tensor_tensor(k.deg[:, :], k.deg[:, :], k.degov[:, :], ALU.add))
            dve.tensor_scalar(k.dtmp[:, :], k.deg[:, :], 1.0, None, ALU.max).then_inc(s["n_deg"], 1)
            dve.tensor_scalar(k.degp[:, 0, :], k.deg[:, :], 1.0, None, ALU.add).then_inc(s["n_deg"], 1)
            link(dve.tensor_scalar(k.deg[:, :], k.deg[:, :], 0.0, None, ALU.is_gt))
            dve.wait_ge(s["n_root"], 2)
            link(dve.reciprocal(k.dinv1[:, :], k.dinv1[:, :]))
            link(dve.tensor_tensor(k.dinv1[:, :], k.dinv1[:, :], k.deg[:, :], ALU.mult))
            link(dve.reciprocal(k.dinv3[:, :], k.dinv3[:, :]))
            start = link.n

            def gather(b, q):
                wait_apart(dve, s["n_tr"], b - 1)
                dve.tensor_copy(k.cat[:, q, 0:D], block_of(k.h0, b))
                dve.tensor_tensor(k.cat[:, q, D:2 * D], block_of(k.agg0, b), block_of(k.ovf, b), ALU.add
                                  ).then_inc(s["n_cat"], 1)

            def update(b, q):
                sub = Chain(dve, s["n_c"], start + 5 * b)
                x = block_of(k.xres, b)
                dve.wait_ge(s["n_mm"], b + 1)
                sub(dve.tensor_tensor(k.aggt[:, q, :], mm[q][:, 0:D], k.c2[:, :], ALU.add))
                sub(dve.scalar_tensor_tensor(x, k.aggt[:, q, :], 0.0, x, ALU.max, ALU.add), apart=True)
                wait_apart(dve, s["n_tr2"], b - 1)
                ins = layer_norm(dve, s["n_ln"], s["n_std"], b + 1, sub, k, x, k.lin_in[:, q, :])
                ins.then_inc(s["n_in"], 1)

            def table(b, q):
                dve.wait_ge(s["n_mm2"], b + 1)
                dve.tensor_scalar(block_of(k.zf, b), mm2[q][:, 0:D], k.dinv1[:, bass.ds(b, 1)], None,
                                  ALU.mult).then_inc(s["n_z"], 1)

            def step(b, u):
                q = u % 2
                gather(b, q)
                if not (isinstance(b, int) and b == 0):
                    update(b - 1, 1 - q)
                if not (isinstance(b, int) and b <= 1):
                    table(b - 2, q)

            looped(dve, NB, 4, step)
            update(NB - 1, (NB - 1) % 2)
            table(NB - 2, (NB - 2) % 2)
            table(NB - 1, (NB - 1) % 2)

        @block.gpsimd
        def _(pool):
            def split(b, q):
                wait_apart(pool, s["n_z"], b + 1)
                sub = Chain(pool, s["n_split"], 4 * b)
                sub(split3(pool, sub, block_of(k.zf, b), k.rem[:, :], parts_of(k.z3b, b)))

            looped(pool, NB, 2, split)



def layers(nc, k):
    gcn1 = dict(matrix="a", dinv=k.dinv1, loop=False)
    gcn3 = dict(matrix="a", dinv=k.dinv3, loop=True)
    plan = [
        dict(gcn1, bias=2, then="linear", w=k.wl[:, 1, :], out_dinv=k.dinv1),
        dict(gcn1, bias=3, then="linear", w=k.wl[:, 2, :], out_dinv=k.dinv1),
        dict(gcn1, bias=4, then="norm"),
        dict(matrix="at", dinv=None, loop=False, bias=None, then="norm linear", w=k.wl[:, 3, :], out_dinv=k.dinv3),
        dict(gcn3, bias=5, then="linear", w=k.wl[:, 4, :], out_dinv=k.dinv3),
        dict(gcn3, bias=6, then="linear", w=k.w3[:, :], out_dinv=k.dinv3),
        dict(gcn3, bias=7, then="out"),
    ]
    s = {n: k.sem("l_" + n) for n in ("ov", "sum", "ready", "tr", "trs", "mm", "z", "split", "ln", "std", "ovdma")}
    strip, out = [k.sem(f"l_strip{q}") for q in range(NS)], [k.sem(f"l_out{q}") for q in range(2)]
    linear = norms = 0
    for n, spec in enumerate(plan):
        layer(nc, k, s, strip, out, n, spec, linear * NB, norms * NB)
        linear += "linear" in spec["then"]
        norms += "norm" in spec["then"]


def layer(nc, k, s, strip, out, n, spec, lin0, ln0):
    strips = k.arena[:, 0:NS * J * P // 2].bitcast(BF16).rearrange("p (s j c) -> p s j c", s=NS, j=J)
    matrix = k.a_d if spec["matrix"] == "a" else k.at_d
    z3, z3n = (k.z3b, k.z3a) if n % 2 == 0 else (k.z3a, k.z3b)
    n0 = n * NB
    has_linear, has_norm, is_out = "linear" in spec["then"], "norm" in spec["then"], spec["then"] == "out"
    chain, splits = k.sem(f"l_c{n}"), k.sem(f"l_k{n}")
    acc, tr, mm = k.bank[0:2], k.bank[2], k.bank[3:5]

    def slot_base(q):
        return 16 * n * len(range(q, NB, NS))

    with nc.Block() as block:

        @block.sync
        def _(sp):
            def load(b, q):
                sp.dma_start(strips[:, q, :, :].rearrange("p j c -> p (j c)"),
                             matrix[bass.ds(b, 1), :, :].rearrange("o p c -> p (o c)")).then_inc(strip[q], 16)

            def step(b, q):
                sp.wait_ge(s["sum"], n0 + b + 1)
                load(b + NS, q)

            for b in range(NS):
                load(b, b)
            looped(sp, NB - NS, NS, step)

        @block.tensor
        def _(pe):
            def half(b, u, lo, hi):
                for a in range(lo, hi):
                    rhs = z3[:, a, :, :] if a < NB else z3[:, bass.ds(b, 1), :, :].rearrange("p o i f -> p (o i) f")
                    ins = pe.matmul(acc[u % 2][:, 0:ZW], strips[:, u, a, :], rhs.rearrange("p i f -> p (i f)"),
                                    start=(a == 0), stop=(a == J - 1))
                return ins

            def turn(b, q):
                wait_apart(pe, s["ready"], n0 + b + 1)
                pe.transpose(tr[0:D, 0:P], k.lin_in[:, q, :], k.ident[:, :]).then_inc(s["tr"], 1)

            def linear(b, q):
                pe.wait_ge(s["trs"], lin0 + b + 1)
                pe.matmul(mm[q][:, 0:D], k.linT[:, :], spec["w"], start=True, stop=True).then_inc(s["mm"], 1)

            def step(b, u):
                pe.wait_ge(strip[u], slot_base(u) + (16 * (b // NS) + 16 if isinstance(b, int)
                                                       else (b - u) * (16 // NS) + 16))
                wait(pe, s["ready"], n0 + b - 1 if not (isinstance(b, int) and b < 2) else 0)
                prev = has_linear and not (isinstance(b, int) and b == 0)
                half(b, u, 0, J // 2)
                if prev:
                    turn(b - 1, (u - 1) % 2)
                half(b, u, J // 2, J).then_inc(s["sum"], 1)
                if prev:
                    linear(b - 1, (u - 1) % 2)

            looped(pe, NB, NS, step)
            if has_linear:
                turn(NB - 1, (NB - 1) % 2)
                linear(NB - 1, (NB - 1) % 2)

        @block.scalar
        def _(act):
            def root(b):
                act.wait_ge(s["ln"], ln0 + b + 1)
                act.activation(k.std[:, :], k.mv[:, 1:2], ACT.Sqrt, bias=k.epsc[:, :]).then_inc(s["std"], 1)

            def keep(b):
                act.wait_ge(s["tr"], lin0 + b + 1)
                act.copy(k.linT[:, :], tr[0:D, 0:P]).then_inc(s["trs"], 1)

            def step(b, q):
                if has_norm:
                    root(b)
                if has_linear:
                    keep(b)

            def store(b, q, rows):
                act.wait_ge(s["ready"], n0 + b + 1)
                act.dma_start(k.inp["out"][bass.ds(b * P, rows), :], k.outb[0:rows, q, :]).then_inc(out[q], 16)

            if is_out:
                looped(act, NB - 1, 2, lambda b, q: store(b, q, P))
                store(NB - 1, (NB - 1) % 2, LAST)
                for q in range(2):
                    act.wait_ge(out[q], 16 * len(range(q, NB, 2)))
            elif has_norm or has_linear:
                looped(act, NB, 2, step)

        @block.vector
        def _(dve):
            LINKS = 2 + spec["loop"] + (spec["dinv"] is not None) + 4 * has_norm

            def epilogue(b, q):
                link = Chain(dve, chain, b * LINKS)
                own = bass.ds(b, 1)
                x, agg = block_of(k.xres, b), k.aggt[:, q, :]
                dve.wait_ge(s["sum"], n0 + b + 1)
                link(dve.tensor_reduce(agg, acc[q][:, 0:ZW].rearrange("p (i f) -> p f i", i=PARTS), AX, ALU.add))
                if isinstance(b, int) and b == 0:
                    dve.wait_ge(s["ov"], n + 1)
                link(dve.tensor_tensor(agg, agg, block_of(k.ovf, b), ALU.add))
                if spec["loop"]:
                    link(dve.tensor_tensor(agg, agg, block_of(k.zf, b), ALU.add))
                if spec["dinv"] is not None:
                    link(dve.scalar_tensor_tensor(agg, agg, spec["dinv"][:, own], k.bias[:, spec["bias"], :],
                                                  ALU.mult, ALU.add))
                if is_out:
                    wait(dve, out[q], 16 * (b // 2) if isinstance(b, int) else (b - q) * 8)
                    dve.tensor_tensor(k.outb[:, q, :], agg, x, ALU.add).then_inc(s["ready"], 1)
                elif not has_norm:
                    dve.tensor_scalar(k.lin_in[:, q, :], agg, 0.0, None, ALU.max).then_inc(s["ready"], 1)
                else:
                    if spec["dinv"] is not None:
                        link(dve.scalar_tensor_tensor(x, agg, 0.0, x, ALU.max, ALU.add), apart=True)
                    else:
                        link(dve.tensor_tensor(x, agg, x, ALU.add), apart=True)
                    dst = k.lin_in[:, q, :] if has_linear else block_of(k.zf, b)
                    layer_norm(dve, s["ln"], s["std"], ln0 + b + 1, link, k, x, dst).then_inc(s["ready"], 1)
                assert link.n == LINKS, (link.n, LINKS)

            def table(b, q):
                dve.wait_ge(s["mm"], lin0 + b + 1)
                dve.tensor_scalar(block_of(k.zf, b), mm[q][:, 0:D], spec["out_dinv"][:, bass.ds(b, 1)], None,
                                  ALU.mult).then_inc(s["z"], 1)

            def step(b, q):
                epilogue(b, q)
                if has_linear and not (isinstance(b, int) and b == 0):
                    table(b - 1, 1 - q)

            looped(dve, NB, 2, step)
            if has_linear:
                table(NB - 1, (NB - 1) % 2)

        @block.gpsimd
        def _(pool):
            overflow_sum(pool, k, s["ovdma"], spec["matrix"] == "at")
            pool.sem_inc(s["ov"], 1)

            def split(b, q):
                if has_linear:
                    wait_apart(pool, s["z"], lin0 + b + 1)
                else:
                    wait_apart(pool, s["ready"], n0 + b + 1)
                sub = Chain(pool, splits, 4 * b)
                sub(split3(pool, sub, block_of(k.zf, b), k.rem[:, :], parts_of(z3n, b)))

            if not is_out:
                looped(pool, NB, 2, split)


CAPO = CAP
CAPD = 2 * CAP
WLOADS = 1 + GT + 3 + 5 + 8 + 1

_INS = ["x", "L0_gnn_W1", "L0_gnn_W2", "L1_gnn_W0", "L1_gnn_W1", "L1_gnn_W2", "L3_gnn_W1", "L3_gnn_W2", "L3_gnn_W3",
        "L0_gnn_b1", "L0_gnn_b2", "L1_gnn_b0", "L1_gnn_b1", "L1_gnn_b2", "L3_gnn_b1", "L3_gnn_b2", "L3_gnn_b3"]


def kernel(**inputs):
    import numpy as np
    import concourse.bacc as bacc
    from concourse.bass_utils import run_bass_kernel_spmd

    arrays = {name: np.ascontiguousarray(inputs[name]) for name in _INS}
    for name in ("src", "dst"):
        padded = np.full((EP,), PADNODE, np.int32)
        padded[:E] = np.asarray(inputs[name])
        arrays[name] = padded.reshape(P, T)
    rows = np.zeros((EP, ROW), np.float32)
    rows[:E, :FE] = np.asarray(inputs["edge_attr_32"])
    arrays["edge_rows"] = rows.reshape(P, T, ROW)
    arrays["w1eT_in"] = np.ascontiguousarray(np.asarray(inputs["L0_gnn_W1"])[D:].T).reshape(1, D, FE)
    arrays["u0_in"] = np.ascontiguousarray(np.asarray(inputs["L0_gnn_u"])[0:1].T)

    nc = bacc.Bacc("TRN2", target_bir_lowering=False, num_devices=1)
    t = {n: nc.dram_tensor(f"in_{n}", a.shape, mybir.dt.from_np(a.dtype), kind="ExternalInput").ap()
         for n, a in arrays.items()}
    t["out"] = nc.dram_tensor("out_x", (N, D), F32, kind="ExternalOutput").ap()
    build(nc, t)
    r = run_bass_kernel_spmd(nc, [{f"in_{n}": a for n, a in arrays.items()}], core_ids=[0])
    return r.results[0]["out_x"]
```

```python
from contextlib import ExitStack

import concourse.bass as bass
from concourse import mybir

P = 128
N = 6250
E = 206250
D = 64
FE = 32
FG = 32
NB = -(-N // P)
NP = NB * P
LAST = N - (NB - 1) * P
GT = 4
UN = 4
T = -(-E // (P * GT * UN)) * GT * UN
NG = T // GT
EP = P * T
PADNODE = 8191
ROW = D + 4
C_SLO, C_DLO, C_SRC, C_DST = D, D + 1, D + 2, D + 3
CAP = P
J = NB + 1
SLOTS = NP * J
OVB = SLOTS
ROWS = SLOTS + EP
BIG = 1.0e6
PARTS = 3
ZW = PARTS * D
SG = -(-J // GT)
EU = 2
NS = 4
EPS = 1e-5

F32 = mybir.dt.float32
BF16 = mybir.dt.bfloat16
I32 = mybir.dt.int32
ALU = mybir.AluOpType
ACT = mybir.ActivationFunctionType
AX = mybir.AxisListType.X


class Names:
    pass


class Chain:

    def __init__(self, eng, sem, base):
        self.eng, self.sem, self.base, self.n = eng, sem, base, 0

    def __call__(self, ins, apart=False):
        self.n += 1
        ins.then_inc(self.sem, 1)
        (wait_apart if apart else wait)(self.eng, self.sem, self.base + self.n)


def looped(eng, count, unroll, body):
    for n in range(min(unroll, count)):
        body(n, n)
    rounds = count // unroll
    if rounds > 2:
        with eng.Fori(1, rounds) as i:
            for q in range(unroll):
                body(i * unroll + q, q)
    else:
        for n in range(unroll, rounds * unroll):
            body(n, n % unroll)
    for n in range(max(rounds, 1) * unroll, count):
        body(n, n % unroll)


def wait(eng, sem, value):
    if isinstance(value, int) and value <= 0:
        return
    eng.wait_ge(sem, value)


def wait_apart(eng, sem, value):
    if isinstance(value, int):
        return wait(eng, sem, value)
    value = eng.to_reg(value)
    eng.wait_ge(sem, 1)
    eng.wait_ge(sem, value)


def build(nc, t):
    with ExitStack() as ctx:
        k = Names()
        k.inp = t

        def sb(name, shape, dt=F32):
            return ctx.enter_context(nc.sbuf_tensor(name, shape, dt))

        k.sem = lambda name: ctx.enter_context(nc.semaphore(name))
        k.bank = [ctx.enter_context(nc.psum_tensor(f"bank{i}", [P, 512], F32)) for i in range(8)]

        k.rows_d = nc.dram_tensor("rows_d", (ROWS, ROW), F32, kind="Internal").ap()
        k.a_d = nc.dram_tensor("a_d", (NB, P, J * P), BF16, kind="Internal").ap()
        k.at_d = nc.dram_tensor("at_d", (NB, P, J * P), BF16, kind="Internal").ap()
        k.z_d = nc.dram_tensor("z_d", (NP, D), F32, kind="Internal").ap()
        k.ov_d = nc.dram_tensor("ov_d", (NP, D), F32, kind="Internal").ap()
        k.degov_d = nc.dram_tensor("degov_d", (NP, 1), F32, kind="Internal").ap()

        k.xres = sb("xres", [P, NB, D])
        k.h0 = sb("h0", [P, NB, D])
        k.agg0 = sb("agg0", [P, NB, D])
        k.zf = sb("zf", [P, NB, D])
        k.ovf = sb("ovf", [P, NB, D])
        k.z3a = sb("z3a", [P, NB, PARTS, D], BF16)
        k.z3b = sb("z3b", [P, NB, PARTS, D], BF16)
        k.deg = sb("deg", [P, NB])
        k.degov = sb("degov", [P, NB])
        k.degp = sb("degp", [P, SG, NB])
        k.dinv1 = sb("dinv1", [P, NB])
        k.dinv3 = sb("dinv3", [P, NB])
        k.dtmp = sb("dtmp", [P, NB])
        k.iota = sb("iota", [P, P])
        k.ident = sb("ident", [P, P])
        k.identb = sb("identb", [P, P], BF16)
        k.notbefore = sb("notbefore", [P, P], BF16)
        k.negfrom = sb("negfrom", [P, P], BF16)
        k.onesb = sb("onesb", [P, P], BF16)
        k.ones4 = sb("ones4", [P, GT])
        k.epsc = sb("epsc", [P, 1])
        k.minus1 = sb("minus1", [P, 1])
        k.w1n = sb("w1n", [D, D])
        k.w1e4 = sb("w1e4", [P, GT, D])
        k.w2na = sb("w2na", [P, D])
        k.w2u = sb("w2u", [FG, D])
        k.u0 = sb("u0", [FG, 1])
        k.u0b = sb("u0b", [FG, P])
        k.c2 = sb("c2", [P, D])
        k.wl = sb("wl", [D, 5, D])
        k.w3 = sb("w3", [D, D])
        k.bias = sb("bias", [P, 8, D])
        k.cat = sb("cat", [P, 2, P])
        k.catT = sb("catT", [P, P])
        k.lin_in = sb("lin_in", [P, 2, D])
        k.linT = sb("linT", [D, P])
        k.aggt = sb("aggt", [P, 2, D])
        k.st6 = sb("st6", [P, 6])
        k.mv = sb("mv", [P, 2])
        k.std = sb("std", [P, 1])
        k.rstd = sb("rstd", [P, 1])
        k.rem = sb("rem", [P, D])
        k.outb = sb("outb", [P, 2, D])
        k.nov = sb("nov", [P, 1], I32)
        k.ovmeta = sb("ovmeta", [1, 2], I32)
        k.ovrow = sb("ovrow", [1, D])
        k.ovmsg = sb("ovmsg", [1, D])
        k.ovp = sb("ovp", [1, D])
        k.one1 = sb("one1", [1, 1])
        words = max(12 * T + 80, NS * J * P // 2)
        k.arena = sb("arena", [P, words])
        k.rowbuf = sb("rowbuf", [P, UN, GT, ROW])
        k.attrT = sb("attrT", [P, UN, P])
        k.ab = sb("ab", [P, 2, GT, P], BF16)
        k.abT = sb("abT", [P, 2, GT, P], BF16)
        k.run = sb("run", [P, D], BF16)
        k.intra = sb("intra", [P, 2, GT])
        k.junk = sb("junk", [P, GT * P], BF16)
        k.pick = sb("pick", [P, GT, D])
        k.sel = sb("sel", [P, GT])
        k.rank = sb("rank", [P, GT])
        k.over = sb("over", [P, 2, GT], BF16)
        k.second = sb("second", [P, GT])
        k.pos = sb("pos", [P, 2, GT])
        k.ovseen = sb("ovseen", [P, 2, GT])
        k.ovpos = sb("ovpos", [P, GT])
        k.posi = sb("posi", [P, UN, GT], I32)
        prologue(nc, k)
        bucket_stage(nc, k)
        edge_stage(nc, k)
        first_overflow(nc, k)
        node_stage(nc, k)
        layers(nc, k)



def layer_norm(dve, act_sem, std_sem, count, link, k, src, dst):
    link(dve.bn_stats(k.st6[:, :], src), apart=True)
    dve.bn_aggr(k.mv[:, :], k.st6[:, :]).then_inc(act_sem, 1)
    dve.wait_ge(std_sem, count)
    link(dve.reciprocal(k.rstd[:, :], k.std[:, :]))
    link(dve.tensor_scalar(dst, src, k.mv[:, 0:1], k.rstd[:, 0:1], ALU.subtract, ALU.mult))
    return dve.tensor_scalar(dst, dst, 0.0, None, ALU.max)


def split3(pool, link, z, rem, parts):
    link(pool.tensor_copy(parts[0], z), apart=True)
    link(pool.tensor_tensor(rem, z, parts[0], ALU.subtract), apart=True)
    link(pool.tensor_copy(parts[1], rem), apart=True)
    return pool.tensor_tensor(parts[2], rem, parts[1], ALU.subtract)


def block_of(tile, b):
    return tile[:, bass.ds(b, 1), :].rearrange("p o f -> p (o f)")


def parts_of(tile, b):
    return [tile[:, bass.ds(b, 1), i, :].rearrange("p o f -> p (o f)") for i in range(PARTS)]


def node_rows(dram):
    return dram.rearrange("(b p) f -> p b f", p=P)



def prologue(nc, k):
    words = k.arena[:, :]
    k.ab_val = words[:, 0:2 * (T + GT)]
    o = 2 * (T + GT)
    k.meta = words[:, o:o + 4 * T]
    o += 4 * T
    k.pos0 = words[:, o:o + T]
    k.cap = words[:, o + T:o + 2 * T]
    k.hop = words[:, o + 2 * T:o + 3 * T]
    k.srci = words[:, o + 3 * T:o + 4 * T].bitcast(I32)
    k.dsti = words[:, o + 4 * T:o + 5 * T].bitcast(I32)

    k.slotrow = k.z3b[:, :, :, :].rearrange("p b i f -> p (b i f)").bitcast(F32)[:, 0:J * ROW]
    s = {n: k.sem(n) for n in ("p_x", "p_idx", "p_w", "p_clear", "p_const", "p_c", "p_k", "p_slot", "p_zero",
                               "p_ln", "p_std", "p_in", "p_tr", "p_trs", "p_mm", "p_z", "p_split", "p_u", "p_c2")}
    tr, mm, cps = k.bank[0], k.bank[1:3], k.bank[3]
    meta = k.meta.rearrange("p (t c) -> p t c", c=4)
    metai = meta.bitcast(I32)
    abv = k.ab_val.rearrange("p (t c) -> p t c", c=2)

    with nc.Block() as block:

        @block.sync
        def _(sp):
            x = k.inp["x"]
            sp.wait_ge(s["p_zero"], 1)
            sp.dma_start(k.xres[:, 0:NB - 1, :], x[0:(NB - 1) * P].rearrange("(b p) f -> p b f", p=P)
                         ).then_inc(s["p_x"], 16)
            sp.dma_start(k.xres[0:LAST, NB - 1, :], x[(NB - 1) * P:N]).then_inc(s["p_x"], 16)
            sp.dma_start(k.srci, k.inp["src"]).then_inc(s["p_idx"], 16)
            sp.dma_start(k.dsti, k.inp["dst"]).then_inc(s["p_idx"], 16)
            sp.dma_start(k.w1n[:, :], k.inp["L0_gnn_W1"][0:D]).then_inc(s["p_w"], 16)
            for j in range(GT):
                sp.dma_start(k.w1e4[FE * j:FE * (j + 1), j, :], k.inp["L0_gnn_W1"][D:D + FE]).then_inc(s["p_w"], 16)
            sp.dma_start(k.w2na[:, :], k.inp["L0_gnn_W2"][0:P]).then_inc(s["p_w"], 16)
            sp.dma_start(k.w2u[:, :], k.inp["L0_gnn_W2"][P:P + FG]).then_inc(s["p_w"], 16)
            sp.dma_start(k.u0[:, :], k.inp["u0_in"]).then_inc(s["p_w"], 16)
            for i, w in enumerate((k.inp["L1_gnn_W0"], k.inp["L1_gnn_W1"], k.inp["L1_gnn_W2"], k.inp["L3_gnn_W1"], k.inp["L3_gnn_W2"])):
                sp.dma_start(k.wl[:, i, :], w).then_inc(s["p_w"], 16)
            for i, b in enumerate((k.inp["L0_gnn_b1"], k.inp["L0_gnn_b2"], k.inp["L1_gnn_b0"], k.inp["L1_gnn_b1"], k.inp["L1_gnn_b2"],
                                   k.inp["L3_gnn_b1"], k.inp["L3_gnn_b2"], k.inp["L3_gnn_b3"])):
                sp.dma_start(k.bias[:, i, :], b.partition_broadcast(P)).then_inc(s["p_w"], 16)
            sp.dma_start(k.w3[:, :], k.inp["L3_gnn_W3"]).then_inc(s["p_w"], 16)
            sp.wait_ge(s["p_slot"], 2)
            for b in range(NB):
                sp.dma_start(k.rows_d[b * P * J:(b + 1) * P * J].rearrange("(p j) c -> p (j c)", p=P),
                             k.slotrow).then_inc(s["p_clear"], 16)
            sp.dma_start(node_rows(k.ov_d), k.ovf[:, :, :]).then_inc(s["p_clear"], 16)
            with nc.allow_non_contiguous_dma(reason="one word per node"):
                sp.dma_start(k.degov_d.rearrange("(b p) f -> p (b f)", p=P), k.degov[:, :]).then_inc(s["p_clear"], 16)
            sp.wait_ge(s["p_clear"], 16 * (NB + 2))

        @block.gpsimd
        def _(pool):
            link = Chain(pool, s["p_k"], 0)
            link(pool.iota(k.iota[:, :], [[1, P]], base=0, channel_multiplier=0, allow_small_or_imprecise_dtypes=True))
            link(pool.memset(k.ident[:, :], 0.0))
            link(pool.affine_select(out=k.ident[:, :], in_=k.ident[:, :], compare_op=ALU.not_equal, fill=1.0, base=0,
                                    pattern=[[-1, P]], channel_multiplier=1))
            pool.tensor_copy(k.identb[:, :], k.ident[:, :])
            link(pool.memset(k.notbefore[:, :], -2.0))
            link(pool.affine_select(out=k.notbefore[:, :], in_=k.notbefore[:, :], compare_op=ALU.is_ge, fill=0.0,
                                    base=0, pattern=[[1, P]], channel_multiplier=-1))
            link(pool.memset(k.negfrom[:, :], -1.0))
            link(pool.affine_select(out=k.negfrom[:, :], in_=k.negfrom[:, :], compare_op=ALU.is_ge, fill=0.0,
                                    base=0, pattern=[[-1, P]], channel_multiplier=1))
            pool.memset(k.one1[:, :], 1.0)
            pool.memset(k.onesb[:, :], 1.0).then_inc(s["p_const"], 1)

            def split(b, q):
                wait_apart(pool, s["p_z"], b + 1)
                sub = Chain(pool, s["p_split"], 4 * b)
                sub(split3(pool, sub, block_of(k.zf, b), k.rem[:, :], parts_of(k.z3a, b)))

            looped(pool, NB, 2, split)

        @block.tensor
        def _(pe):
            pe.wait_ge(s["p_const"], 1)
            pe.wait_ge(s["p_w"], 16 * WLOADS)
            pe.wait_ge(s["p_u"], 1)
            pe.matmul(cps[:, 0:D], k.u0b[:, :], k.w2u[:, :], start=True, stop=True).then_inc(s["p_c2"], 1)

            def step(b, q):
                wait_apart(pe, s["p_in"], b + 1)
                pe.transpose(tr[0:D, 0:P], k.lin_in[:, q, :], k.ident[:, :]).then_inc(s["p_tr"], 1)
                pe.wait_ge(s["p_trs"], b + 1)
                pe.matmul(mm[q][:, 0:D], k.linT[:, :], k.w1n[:, :], start=True, stop=True
                          ).then_inc(s["p_mm"], 1)

            looped(pe, NB, 2, step)

        @block.scalar
        def _(act):
            act.wait_ge(s["p_slot"], 2)
            def step(b, q):
                act.wait_ge(s["p_ln"], b + 1)
                act.activation(k.std[:, :], k.mv[:, 1:2], ACT.Sqrt, bias=k.epsc[:, :]).then_inc(s["p_std"], 1)
                act.wait_ge(s["p_tr"], b + 1)
                act.copy(k.linT[:, :], tr[0:D, 0:P]).then_inc(s["p_trs"], 1)

            looped(act, NB, 2, step)

        @block.vector
        def _(dve):
            link = Chain(dve, s["p_c"], 0)
            link(dve.memset(k.w1e4[:, :, :], 0.0))
            dve.memset(k.xres[:, NB - 1, :], 0.0).then_inc(s["p_zero"], 1)
            link(dve.memset(k.slotrow, 0.0))
            dve.memset(k.slotrow.rearrange("p (j c) -> p j c", c=ROW)[:, :, C_SLO:C_DLO + 1], -1.0
                       ).then_inc(s["p_slot"], 1)
            dve.memset(k.ovf[:, :, :], 0.0)
            dve.memset(k.epsc[:, :], EPS)
            dve.memset(k.minus1[:, :], -1.0)
            dve.memset(k.run[:, :], 0.0)
            dve.memset(k.ones4[:, :], 1.0)
            dve.memset(k.ovseen[:, :, :], 0.0)
            dve.memset(k.agg0[:, :, :], 0.0)
            dve.memset(k.degov[:, :], 0.0).then_inc(s["p_slot"], 1)
            dve.wait_ge(s["p_idx"], 32)
            link(dve.memset(k.ab_val[:, 2 * T:], 0.0))
            for c, v in ((0, k.srci), (1, k.dsti)):
                tmp = k.pos0.bitcast(I32)
                link(dve.tensor_copy(metai[:, :, 2 + c], v))
                link(dve.tensor_scalar(tmp, v, 7, None, ALU.logical_shift_right))
                link(dve.tensor_copy(abv[:, 0:T, c], tmp))
                link(dve.tensor_scalar(tmp, v, P - 1, None, ALU.bitwise_and))
                link(dve.tensor_copy(meta[:, :, c], tmp))
            a, b = abv[:, 0:T, 0], abv[:, 0:T, 1]
            link(dve.tensor_tensor(k.cap, a, b, ALU.is_equal))
            link(dve.tensor_scalar(k.cap, k.cap, float(CAPD - CAPO), float(CAPO), ALU.mult, ALU.add))
            link(dve.tensor_scalar(k.hop, a, float(NB), BIG, ALU.is_ge, ALU.mult))
            link(dve.tensor_tensor(k.cap, k.cap, k.hop, ALU.add))
            link(dve.scalar_tensor_tensor(k.pos0, b, float(P * J), k.hop, ALU.mult, ALU.add))
            link(dve.tensor_tensor(k.pos0, k.pos0, a, ALU.add))
            link(dve.tensor_scalar(k.hop, a, -1.0, float(NB - P * J), ALU.mult, ALU.add))
            dve.wait_ge(s["p_w"], 16 * WLOADS)
            dve.tensor_copy(k.u0b[:, :], k.u0[:, 0:1].to_broadcast([FG, P])).then_inc(s["p_u"], 1)
            dve.wait_ge(s["p_c2"], 1)
            link(dve.tensor_tensor(k.c2[:, :], cps[:, 0:D], k.bias[:, 1, :], ALU.add))
            dve.wait_ge(s["p_x"], 32)
            first = link.n

            def norm(b, q):
                sub = Chain(dve, s["p_c"], first + 4 * b)
                ins = layer_norm(dve, s["p_ln"], s["p_std"], b + 1, sub, k, block_of(k.xres, b), block_of(k.h0, b))
                sub(ins, apart=True)
                wait_apart(dve, s["p_tr"], b - 1)
                dve.tensor_copy(k.lin_in[:, q, :], block_of(k.h0, b)).then_inc(s["p_in"], 1)

            def table(b, q):
                dve.wait_ge(s["p_mm"], b + 1)
                dve.tensor_tensor(block_of(k.zf, b), mm[q][:, 0:D], k.bias[:, 0, :], ALU.add
                                  ).then_inc(s["p_z"], 1)

            def step(b, q):
                norm(b, q)
                if not (isinstance(b, int) and b == 0):
                    table(b - 1, 1 - q)

            looped(dve, NB, 2, step)
            table(NB - 1, (NB - 1) % 2)



def bucket_stage(nc, k):
    loaded = [k.sem(f"attr_loaded{q}") for q in range(UN)]
    scattered = [k.sem(f"row_scattered{q}") for q in range(UN)]
    s = {n: k.sem(n) for n in ("onehot", "onehot_t", "onehot_ts", "same", "intra", "counted", "run", "over", "ovcount",
                               "projected", "q_kept", "tail", "pos", "b_c", "b_f", "b_p")}
    abv = k.ab_val.rearrange("p (t c) -> p t c", c=2)
    meta = k.meta.rearrange("p (t c) -> p t c", c=4).bitcast(I32)
    LINKS, FLINKS = 5, 4

    turned = k.bank[0][:, 0:256].bitcast(BF16).rearrange("p (j e) -> p j e", j=GT)
    same = [k.bank[1][:, 0:P], k.bank[1][:, P:3 * P], k.bank[2][:, 0:3 * P], k.bank[3][:, 0:4 * P]]
    shared = 2
    ovbefore, ovtotal = k.bank[6][:, 0:GT], k.bank[6][:, GT:2 * GT]
    q_ps = k.bank[7][:, 0:GT * D]

    def picked(q):
        return k.bank[4 + q][:, 0:GT * D].rearrange("p (j f) -> p j f", j=GT)

    def counts(q):
        return k.bank[4 + q][:, GT * D:(GT + 1) * D]

    def slot_free(n, u):
        return 16 * GT * (n // UN) if isinstance(n, int) else (n - u) * (16 * GT // UN)

    with nc.Block() as block:

        @block.sync
        def _(sp):
            def load(n, u):
                wait(sp, s["projected"], n - UN + 1)
                sp.dma_start(k.attrT[:, u, :], k.inp["attr_T"][bass.ds(n, 1), :, :].rearrange("o p c -> p (o c)")
                             ).then_inc(loaded[u], 16)

            looped(sp, NG, UN, load)
            for u in range(UN):
                sp.wait_ge(scattered[u], 16 * GT * (NG // UN))

        @block.gpsimd
        def _(pool):
            limit = pool.to_reg(ROWS - 1)

            def scatter(n, u):
                wait_apart(pool, s["q_kept"], n + 1)
                wait_apart(pool, s["tail"], n + 1)
                wait_apart(pool, s["pos"], n + 1)
                for j in range(GT):
                    pool.indirect_dma_start(k.rows_d, bass.IndirectOffsetOnAxis(ap=k.posi[:, u, j:j + 1], axis=0),
                                            k.rowbuf[:, u, j, :], None, bounds_check=limit, oob_is_err=False
                                            ).then_inc(scattered[u], 16)

            looped(pool, NG, UN, scatter)

        @block.tensor
        def _(pe):
            def turn(n, q):
                pe.wait_ge(s["onehot"], n + 1)
                wait(pe, s["onehot_ts"], n)
                for j in range(GT):
                    ins = pe.transpose(turned[:, j, :], k.ab[:, q, j, :], k.identb[:, :])
                ins.then_inc(s["onehot_t"], 1)

            def project(n, u):
                pe.wait_ge(loaded[u], 16 * (n // UN) + 16 if isinstance(n, int) else (n - u) * (16 // UN) + 16)
                wait(pe, s["q_kept"], n)
                pe.matmul(q_ps, k.attrT[:, u, :], k.w1e4[:, :, :].rearrange("p j f -> p (j f)"), start=True, stop=True
                          ).then_inc(s["projected"], 1)

            def overflow(n, q):
                pe.wait_ge(s["over"], n + 1)
                wait(pe, s["pos"], n)
                pe.matmul(ovbefore, k.negfrom[:, :], k.over[:, q, :], start=True, stop=True)
                pe.matmul(ovtotal, k.onesb[:, :], k.over[:, q, :], start=True, stop=True).then_inc(s["ovcount"], 1)

            def step(n, u):
                q = u % 2
                pe.wait_ge(s["onehot_ts"], n + 1)
                for j in range(GT):
                    if j != shared - 1:
                        last = max(j + 1, shared) - GT
                        wait(pe, s["intra"], GT * n + last)
                    out = same[j]
                    pe.matmul(out, k.abT[:, q, j, :], k.abT[:, q, 0:j + 1, :].rearrange("p j e -> p (j e)"),
                              start=True, stop=False)
                    pe.matmul(out[:, j * P:(j + 1) * P], k.identb[:, :], k.notbefore[:, :], start=False, stop=True
                              ).then_inc(s["same"], 1)
                turn(n + 1, 1 - q)
                project(n, u)
                wait(pe, s["over"], n - 1)
                wait(pe, s["run"], n)
                for j in range(GT):
                    pe.matmul(picked(q)[:, j, :], k.abT[:, q, j, :], k.run[:, :], start=True, stop=True)
                for j in range(GT):
                    ins = pe.matmul(counts(q), k.ab[:, q, j, :], k.ab[:, q, j, D:2 * D],
                                    start=(j == 0), stop=(j == GT - 1))
                ins.then_inc(s["counted"], 1)
                if not (isinstance(n, int) and n == 0):
                    overflow(n - 1, 1 - q)

            turn(0, 0)
            looped(pe, NG, UN, step)
            overflow(NG - 1, (NG - 1) % 2)

        @block.scalar
        def _(act):
            def keep(n, q):
                wait(act, s["counted"], n - 1)
                act.wait_ge(s["onehot_t"], n + 1)
                act.copy(k.abT[:, q, :, :], turned).then_inc(s["onehot_ts"], 1)

            def step(n, u):
                q = u % 2
                wait(act, s["over"], n - 1)
                for j in range(GT):
                    if j:
                        act.wait_ge(s["intra"], GT * n + j)
                    act.wait_ge(s["same"], GT * n + max(j + 1, shared))
                    act.activation(k.junk[:, 0:(j + 1) * P], same[j], ACT.Relu, bias=k.minus1[:, :],
                                   accum_out=k.intra[:, q, j:j + 1]).then_inc(s["intra"], 1)
                keep(n + 1, 1 - q)
                act.wait_ge(s["projected"], n + 1)
                wait(act, scattered[u], slot_free(n, u))
                act.copy(k.rowbuf[:, u, :, 0:D], q_ps.rearrange("p (j f) -> p j f", j=GT)).then_inc(s["q_kept"], 1)

            keep(0, 0)
            looped(act, NG, UN, step)

        @block.vector
        def _(dve):
            def onehot(n, q):
                wait(dve, s["counted"], n - 1)
                val = k.ab_val[:, bass.ds(n * 2 * GT, 2 * GT)]
                dve.tensor_tensor(k.ab[:, q, :, :].rearrange("p j (c e) -> p (j c) e", c=2),
                                  k.iota[:, 0:D].unsqueeze(1).to_broadcast([P, 2 * GT, D]),
                                  val.unsqueeze(2).to_broadcast([P, 2 * GT, D]), ALU.is_equal
                                  ).then_inc(s["onehot"], 1)

            def finish(n, u):
                q = u % 2
                link = Chain(dve, s["b_f"], n * FLINKS)
                dve.wait_ge(s["ovcount"], n + 1)
                link(dve.tensor_tensor_scan(k.ovseen[:, q, :], k.ones4[:, :], ovtotal, k.ovseen[:, 1 - q, GT - 1:GT],
                                            ALU.mult, ALU.add))
                link(dve.scalar_tensor_tensor(k.ovpos[:, :], ovbefore, float(OVB), k.ovseen[:, q, :],
                                              ALU.add, ALU.add))
                dve.wait_ge(s["b_p"], n + 1)
                link(dve.tensor_tensor(k.ovpos[:, :], k.ovpos[:, :], k.pos[:, q, :], ALU.subtract))
                link(dve.tensor_tensor(k.ovpos[:, :], k.ovpos[:, :], k.over[:, q, :], ALU.mult))
                dve.tensor_tensor(k.posi[:, u, :], k.pos[:, q, :], k.ovpos[:, :], ALU.add).then_inc(s["pos"], 1)
                assert link.n == FLINKS

            def step(n, u):
                q = u % 2
                link = Chain(dve, s["b_c"], n * LINKS)
                tiles = bass.ds(n * GT, GT)
                onehot(n + 1, 1 - q)
                dve.wait_ge(s["counted"], n + 1)
                dve.tensor_tensor(k.run[0:D, :], counts(q)[0:D, :], k.run[0:D, :], ALU.add).then_inc(s["run"], 1)
                link(dve.tensor_tensor(k.pick[:, :, :], picked(q), k.ab[:, q, :, D:2 * D], ALU.mult))
                link(dve.tensor_reduce(k.sel[:, :], k.pick[:, :, :], AX, ALU.add))
                dve.wait_ge(s["intra"], GT * n + GT)
                link(dve.tensor_tensor(k.rank[:, :], k.sel[:, :], k.intra[:, q, :], ALU.add))
                dve.tensor_tensor(k.over[:, q, :], k.rank[:, :], k.cap[:, tiles], ALU.is_ge).then_inc(s["over"], 1)
                if not (isinstance(n, int) and n == 0):
                    finish(n - 1, (u - 1) % UN)
                wait(dve, scattered[u], slot_free(n, u))
                dve.tensor_copy(k.rowbuf[:, u, :, :].bitcast(I32)[:, :, C_SLO:ROW], meta[:, tiles, :]
                                ).then_inc(s["tail"], 1)
                link(dve.scalar_tensor_tensor(k.second[:, :], k.rank[:, :], float(P), k.hop[:, tiles],
                                              ALU.is_ge, ALU.mult))
                link(dve.scalar_tensor_tensor(k.pos[:, q, :], k.rank[:, :], float(J), k.pos0[:, tiles],
                                              ALU.mult, ALU.add))
                dve.tensor_tensor(k.pos[:, q, :], k.pos[:, q, :], k.second[:, :], ALU.add).then_inc(s["b_p"], 1)
                assert link.n == LINKS

            onehot(0, 0)
            looped(dve, NG, UN, step)
            finish(NG - 1, (NG - 1) % UN)
            dve.wait_ge(s["pos"], NG)
            dve.tensor_copy(k.nov[:, :], k.ovseen[:, (NG - 1) % 2, GT - 1:GT])



def edge_buffers(k):
    at = [0]

    def take(shape, dt):
        n = 1
        for d in shape:
            n *= d
        words = n if dt == F32 else n // 2
        part = k.arena[:, at[0]:at[0] + words]
        at[0] += words
        names = "abcd"[:len(shape)]
        return (part if dt == F32 else part.bitcast(dt)).rearrange(
            f"p ({' '.join(names)}) -> p {' '.join(names)}", **dict(zip(names, shape)))

    k.strip = take((EU, J, ROW), F32)
    k.oh = take((EU, GT * 2, P), BF16).rearrange("p g (j e) c -> p g j e c", e=2)
    k.ohf = take((EU, GT, P), F32)
    k.dT = take((EU, GT, P), BF16)
    k.atile = take((SG, GT, P), BF16)
    k.attile = take((SG, GT, P), BF16)
    k.presum = take((EU, GT, D), F32)
    k.msg = take((EU, GT, D), F32)


class Group:

    def __init__(self, b, r, g):
        self.b, self.r, self.g = b, r, g
        self.n, self.q, self.m = SG * b + g, (SG * r + g) % EU, min(GT, J - GT * g)


def edge_stage(nc, k):
    edge_buffers(k)
    strip = [k.sem(f"strip{q}") for q in range(EU)]
    a_out = [k.sem(f"a_out{g}") for g in range(SG)]
    at_out = [k.sem(f"at_out{g}") for g in range(SG)]
    s = {n: k.sem(n) for n in ("lanes", "lanes_f", "turned", "a_sum", "at_sum", "d_t", "a_kept", "at_kept", "gathered",
                               "presum", "message", "summed", "added", "e_c")}

    def group(b, r, g, back=0):
        if g - back < 0:
            b, r, g = b - 1, (r - 1) % EU, g + SG
        g -= back
        if isinstance(b, int) and b < 0:
            return None
        return Group(b, r, g)

    a_ps, at_ps = k.bank[0], k.bank[1]
    d_t = k.bank[2][:, 0:256].bitcast(BF16).rearrange("p (j e) -> p j e", j=GT)

    def gat(q):
        return k.bank[4 + q][:, 0:GT * D]

    def tot(q):
        return k.bank[6 + q][:, 0:GT * D].rearrange("p (j f) -> p j f", j=GT)

    cuts = [J * i // EU for i in range(EU + 1)]

    def strip_loaded(b, r):
        return 16 * EU * (b // EU) + 16 * EU if isinstance(b, int) else (b - r) * 16 + 16 * EU

    last = (NB - 1, (NB - 1) % EU, SG - 1)

    with nc.Block() as block:

        @block.sync
        def _(sp):
            def load(b, r):
                src = k.rows_d[bass.ds(b * (P * J), P * J), :] if not isinstance(b, int) else \
                    k.rows_d[b * P * J:(b + 1) * P * J]
                src = src.rearrange("(p j) c -> p j c", p=P)
                for lo, hi in zip(cuts, cuts[1:]):
                    sp.dma_start(k.strip[:, r, lo:hi, :], src[:, lo:hi, :]).then_inc(strip[r], 16)

            def step(b, r, more=True):
                for g in range(SG):
                    t = group(b, r, g)
                    sp.wait_ge(s["a_kept"], t.n + 1)
                    sp.dma_start(k.a_d[bass.ds(b, 1), :, GT * P * g:GT * P * g + t.m * P].rearrange("o p c -> p (o c)"),
                                 k.atile[:, g, 0:t.m, :].rearrange("p j c -> p (j c)")).then_inc(a_out[g], 16)
                    sp.wait_ge(s["at_kept"], t.n + 1)
                    cols = bass.ds(b * P, P)
                    own = t.m if g < SG - 1 else t.m - 1
                    sp.dma_start(k.at_d[GT * g:GT * g + own, :, cols].rearrange("a p c -> p a c"),
                                 k.attile[:, g, 0:own, :]).then_inc(at_out[g], 16)
                    if g == SG - 1:
                        sp.dma_start(k.at_d[bass.ds(b, 1), :, NB * P:J * P].rearrange("o p c -> p (o c)"),
                                     k.attile[:, g, t.m - 1, :]).then_inc(at_out[g], 16)
                if more:
                    sp.wait_ge(s["presum"], SG * b + SG)
                    load(b + EU, r)

            for b in range(EU):
                load(b, b)
            looped(sp, NB - EU, EU, step)
            for b in range(NB - EU, NB):
                step(b, b % EU, more=False)
            for g in range(SG):
                sp.wait_ge(a_out[g], 16 * NB)
                sp.wait_ge(at_out[g], 16 * NB * (2 if g == SG - 1 else 1))

        @block.tensor
        def _(pe):
            def front(t):
                wait_apart(pe, s["lanes"], t.n + 1)
                wait(pe, s["d_t"], t.n)
                for j in range(t.m):
                    ins = pe.transpose(d_t[:, j, :], k.oh[:, t.q, j, 1, :], k.identb[:, :])
                ins.then_inc(s["turned"], 1)
                wait(pe, s["a_kept"], t.n)
                for j in range(t.m):
                    ins = pe.matmul(a_ps[:, j * P:(j + 1) * P], k.oh[:, t.q, j, 0, :], k.oh[:, t.q, j, 1, :],
                                    start=True, stop=True)
                ins.then_inc(s["a_sum"], 1)
                wait(pe, s["at_kept"], t.n)
                for j in range(t.m):
                    ins = pe.matmul(at_ps[:, j * P:(j + 1) * P], k.oh[:, t.q, j, 1, :], k.oh[:, t.q, j, 0, :],
                                    start=True, stop=True)
                ins.then_inc(s["at_sum"], 1)

            def gather(t):
                if t is None:
                    return
                table = parts_of(k.z3a, t.b)
                pe.wait_ge(s["d_t"], t.n + 1)
                wait(pe, s["presum"], t.n - EU + 1)
                for j in range(t.m):
                    out = gat(t.q)[:, j * D:(j + 1) * D]
                    for i in range(PARTS):
                        ins = pe.matmul(out, k.dT[:, t.q, j, :], table[i], start=(i == 0), stop=(i == PARTS - 1))
                ins.then_inc(s["gathered"], 1)

            def total(t):
                if t is None:
                    return
                pe.wait_ge(s["lanes_f"], t.n + 1)
                pe.wait_ge(s["message"], t.n + 1)
                wait(pe, s["added"], t.n - EU + 1)
                for j in range(t.m):
                    ins = pe.matmul(tot(t.q)[:, j, :], k.ohf[:, t.q, j, :], k.msg[:, t.q, j, :], start=True, stop=True)
                ins.then_inc(s["summed"], 1)

            def step(b, r):
                for g in range(SG):
                    front(group(b, r, g))
                    gather(group(b, r, g, 1))
                    total(group(b, r, g, 2))

            looped(pe, NB, EU, step)
            gather(group(*last))
            for back in (1, 0):
                total(group(*last, back))

        @block.scalar
        def _(act):
            def step(b, r):
                for g in range(SG):
                    t = group(b, r, g)
                    act.wait_ge(s["turned"], t.n + 1)
                    wait(act, s["gathered"], t.n - EU + 1)
                    act.copy(k.dT[:, t.q, 0:t.m, :], d_t[:, 0:t.m, :]).then_inc(s["d_t"], 1)
                    act.wait_ge(s["a_sum"], t.n + 1)
                    wait(act, a_out[g], b * 16)
                    act.copy(k.atile[:, g, 0:t.m, :].rearrange("p j c -> p (j c)"), a_ps[:, 0:t.m * P]
                             ).then_inc(s["a_kept"], 1)
                    act.wait_ge(s["at_sum"], t.n + 1)
                    wait(act, at_out[g], b * (32 if g == SG - 1 else 16))
                    act.activation(k.attile[:, g, 0:t.m, :].rearrange("p j c -> p (j c)"), at_ps[:, 0:t.m * P],
                                   ACT.Copy, accum_out=k.degp[:, g, bass.ds(b, 1)]).then_inc(s["at_kept"], 1)

            looped(act, NB, EU, step)

        @block.gpsimd
        def _(pool):
            def message(t):
                if t is None:
                    return
                wait_apart(pool, s["presum"], t.n + 1)
                wait_apart(pool, s["summed"], t.n - EU + 1)
                pool.tensor_scalar(k.msg[:, t.q, 0:t.m, :], k.presum[:, t.q, 0:t.m, :], 0.0, None, ALU.max
                                   ).then_inc(s["message"], 1)

            def lanes(t):
                pool.wait_ge(s["lanes"], t.n + 1)
                wait(pool, s["summed"], t.n - EU + 1)
                own = k.oh[:, t.q, 0:t.m, 0, :]
                pool.tensor_tensor(k.ohf[:, t.q, 0:t.m, :], own, own, ALU.mult).then_inc(s["lanes_f"], 1)

            def step(b, r):
                for g in range(SG):
                    lanes(group(b, r, g))
                    message(group(b, r, g, 1))

            looped(pool, NB, EU, step)
            message(group(*last))

        @block.vector
        def _(dve):
            def lanes(t):
                if t.g == 0:
                    dve.wait_ge(strip[t.r], strip_loaded(t.b, t.r))
                wait(dve, s["at_sum"], t.n - EU + 1)
                wait(dve, s["lanes_f"], t.n - EU + 1)
                val = k.strip[:, t.r, GT * t.g:GT * t.g + t.m, C_SLO:C_DLO + 1]
                dve.tensor_tensor(k.oh[:, t.q, 0:t.m, :, :],
                                  k.iota[:, :].unsqueeze(1).unsqueeze(1).to_broadcast([P, t.m, 2, P]),
                                  val.unsqueeze(3).to_broadcast([P, t.m, 2, P]), ALU.is_equal).then_inc(s["lanes"], 1)

            def presum(t):
                if t is None:
                    return
                dve.wait_ge(s["gathered"], t.n + 1)
                wait(dve, s["message"], t.n - EU + 1)
                dve.tensor_tensor(k.presum[:, t.q, 0:t.m, :], gat(t.q)[:, 0:t.m * D].rearrange("p (j f) -> p j f", f=D),
                                  k.strip[:, t.r, GT * t.g:GT * t.g + t.m, 0:D], ALU.add).then_inc(s["presum"], 1)

            def add(t):
                if t is None:
                    return
                dve.wait_ge(s["summed"], t.n + 1)
                wait(dve, s["added"], t.n)
                if t.g < SG - 1:
                    own = k.agg0[:, GT * t.g:GT * t.g + t.m, :]
                    dve.tensor_tensor(own, tot(t.q)[:, 0:t.m, :], own, ALU.add).then_inc(s["added"], 1)
                else:
                    link = Chain(dve, s["e_c"], t.b)
                    own = k.agg0[:, GT * t.g:GT * t.g + t.m - 1, :]
                    link(dve.tensor_tensor(own, tot(t.q)[:, 0:t.m - 1, :], own, ALU.add))
                    own = block_of(k.agg0, t.b)
                    dve.tensor_tensor(own, tot(t.q)[:, t.m - 1, :], own, ALU.add).then_inc(s["added"], 1)

            def step(b, r):
                for g in range(SG):
                    lanes(group(b, r, g))
                    presum(group(b, r, g, 1))
                    add(group(b, r, g, 3))

            looped(dve, NB, EU, step)
            presum(group(*last))
            for back in (2, 1, 0):
                add(group(*last, back))



def drained(pool, sem):
    pool.wait_ge(sem, 16)
    pool.dma_reset(range(sem.num, sem.num + 1))
    pool.sem_clear(sem)


def overflow_ends(pool, k, i, sem):
    pool.dma_start(k.ovmeta[:, :], k.rows_d[bass.ds(i + OVB, 1), C_SRC:C_DST + 1].bitcast(I32)).then_inc(sem, 16)
    drained(pool, sem)
    return pool.value_load(k.ovmeta[0:1, 0:1]), pool.value_load(k.ovmeta[0:1, 1:2])


def overflow_sum(pool, k, sem, transposed):
    nov = pool.value_load(k.nov[0:1, 0:1])
    with pool.If(nov > 0):
        pool.dma_start(node_rows(k.z_d), k.zf[:, :, :]).then_inc(sem, 16)
        drained(pool, sem)
        with pool.Fori(0, nov) as i:
            src, dst = overflow_ends(pool, k, i, sem)
            frm, to = (dst, src) if transposed else (src, dst)
            pool.dma_start(k.ov_d[bass.ds(to, 1), :], k.z_d[bass.ds(frm, 1), :], accum_op=ALU.add).then_inc(sem, 16)
            drained(pool, sem)
        overflow_take(pool, k, sem)


def overflow_take(pool, k, sem):
    pool.dma_start(k.ovf[:, :, :], node_rows(k.ov_d)).then_inc(sem, 16)
    drained(pool, sem)
    pool.memset(k.h0[:, :, :], 0.0).then_inc(k.s_ovz, 1)
    pool.wait_ge(k.s_ovz, 1)
    pool.sem_clear(k.s_ovz)
    pool.dma_start(node_rows(k.ov_d), k.h0[:, :, :]).then_inc(sem, 16)
    drained(pool, sem)


def first_overflow(nc, k):
    sem, step = k.sem("ov_dma"), k.sem("ov_step")
    k.s_ovz = k.sem("ov_zero")
    with nc.Block() as block:

        @block.gpsimd
        def _(pool):
            def link(ins):
                ins.then_inc(step, 1)
                pool.wait_ge(step, 1)
                pool.sem_clear(step)

            nov = pool.value_load(k.nov[0:1, 0:1])
            with pool.If(nov > 0):
                pool.dma_start(node_rows(k.z_d), k.zf[:, :, :]).then_inc(sem, 16)
                drained(pool, sem)
                with pool.Fori(0, nov) as i:
                    src, dst = overflow_ends(pool, k, i, sem)
                    pool.dma_start(k.ovrow[:, :], k.rows_d[bass.ds(i + OVB, 1), 0:D]).then_inc(sem, 16)
                    drained(pool, sem)
                    pool.dma_start(k.ovp[:, :], k.z_d[bass.ds(dst, 1), :]).then_inc(sem, 16)
                    drained(pool, sem)
                    link(pool.tensor_tensor(k.ovmsg[:, :], k.ovrow[:, :], k.ovp[:, :], ALU.add))
                    link(pool.tensor_scalar(k.ovmsg[:, :], k.ovmsg[:, :], 0.0, None, ALU.max))
                    pool.dma_start(k.ov_d[bass.ds(src, 1), :], k.ovmsg[:, :], accum_op=ALU.add).then_inc(sem, 16)
                    drained(pool, sem)
                    pool.dma_start(k.degov_d[bass.ds(dst, 1), :], k.one1[:, :], accum_op=ALU.add).then_inc(sem, 16)
                    drained(pool, sem)
                pool.dma_start(k.ovf[:, :, :], node_rows(k.ov_d)).then_inc(sem, 16)
                drained(pool, sem)
                with nc.allow_non_contiguous_dma(reason="one word per node, with overflow edges only"):
                    pool.dma_start(k.degov[:, :], k.degov_d.rearrange("(b p) f -> p (b f)", p=P)).then_inc(sem, 16)
                drained(pool, sem)
                link(pool.memset(k.zf[:, :, :], 0.0))
                pool.dma_start(node_rows(k.ov_d), k.zf[:, :, :]).then_inc(sem, 16)
                drained(pool, sem)



def node_stage(nc, k):
    s = {n: k.sem(n) for n in ("n_cat", "n_tr", "n_trs", "n_mm", "n_ln", "n_std", "n_in", "n_tr2", "n_trs2", "n_mm2",
                               "n_z", "n_split", "n_c", "n_deg", "n_root", "n_root3")}
    tr, tr2, mm, mm2 = k.bank[0], k.bank[1], k.bank[2:4], k.bank[4:6]
    w0 = k.wl[:, 0, :]

    with nc.Block() as block:

        @block.tensor
        def _(pe):
            def first(b, q):
                pe.wait_ge(s["n_cat"], b + 1)
                pe.transpose(tr[:, 0:P], k.cat[:, q, :], k.ident[:, :]).then_inc(s["n_tr"], 1)
                pe.wait_ge(s["n_trs"], b + 1)
                pe.matmul(mm[q][:, 0:D], k.catT[:, :], k.w2na[:, :], start=True, stop=True
                          ).then_inc(s["n_mm"], 1)

            def second(b, q):
                wait_apart(pe, s["n_in"], b + 1)
                pe.transpose(tr2[0:D, 0:P], k.lin_in[:, q, :], k.ident[:, :]).then_inc(s["n_tr2"], 1)
                pe.wait_ge(s["n_trs2"], b + 1)
                pe.matmul(mm2[q][:, 0:D], k.linT[:, :], w0, start=True, stop=True
                          ).then_inc(s["n_mm2"], 1)

            def step(b, q):
                first(b, q)
                if not (isinstance(b, int) and b == 0):
                    second(b - 1, 1 - q)

            looped(pe, NB, 2, step)
            second(NB - 1, (NB - 1) % 2)

        @block.scalar
        def _(act):
            act.wait_ge(s["n_deg"], 1)
            act.activation(k.dinv1[:, :], k.dtmp[:, :], ACT.Sqrt).then_inc(s["n_root"], 1)
            act.wait_ge(s["n_deg"], 2)
            act.activation(k.dinv3[:, :], k.degp[:, 0, :], ACT.Sqrt).then_inc(s["n_root"], 1)

            def first(b):
                act.wait_ge(s["n_tr"], b + 1)
                act.copy(k.catT[:, :], tr[:, 0:P]).then_inc(s["n_trs"], 1)

            def second(b):
                act.wait_ge(s["n_ln"], b + 1)
                act.activation(k.std[:, :], k.mv[:, 1:2], ACT.Sqrt, bias=k.epsc[:, :]).then_inc(s["n_std"], 1)
                act.wait_ge(s["n_tr2"], b + 1)
                act.copy(k.linT[:, :], tr2[0:D, 0:P]).then_inc(s["n_trs2"], 1)

            def step(b, q):
                first(b)
                if not (isinstance(b, int) and b == 0):
                    second(b - 1)

            looped(act, NB, 2, step)
            second(NB - 1)

        @block.vector
        def _(dve):
            link = Chain(dve, s["n_c"], 0)
            link(dve.tensor_reduce(k.deg[:, :], k.degp[:, :, :].rearrange("p g b -> p b g"), AX, ALU.add))
            link(dve.tensor_tensor(k.deg[:, :], k.deg[:, :], k.degov[:, :], ALU.add))
            dve.tensor_scalar(k.dtmp[:, :], k.deg[:, :], 1.0, None, ALU.max).then_inc(s["n_deg"], 1)
            dve.tensor_scalar(k.degp[:, 0, :], k.deg[:, :], 1.0, None, ALU.add).then_inc(s["n_deg"], 1)
            link(dve.tensor_scalar(k.deg[:, :], k.deg[:, :], 0.0, None, ALU.is_gt))
            dve.wait_ge(s["n_root"], 2)
            link(dve.reciprocal(k.dinv1[:, :], k.dinv1[:, :]))
            link(dve.tensor_tensor(k.dinv1[:, :], k.dinv1[:, :], k.deg[:, :], ALU.mult))
            link(dve.reciprocal(k.dinv3[:, :], k.dinv3[:, :]))
            start = link.n

            def gather(b, q):
                wait_apart(dve, s["n_tr"], b - 1)
                dve.tensor_copy(k.cat[:, q, 0:D], block_of(k.h0, b))
                dve.tensor_tensor(k.cat[:, q, D:2 * D], block_of(k.agg0, b), block_of(k.ovf, b), ALU.add
                                  ).then_inc(s["n_cat"], 1)

            def update(b, q):
                sub = Chain(dve, s["n_c"], start + 5 * b)
                x = block_of(k.xres, b)
                dve.wait_ge(s["n_mm"], b + 1)
                sub(dve.tensor_tensor(k.aggt[:, q, :], mm[q][:, 0:D], k.c2[:, :], ALU.add))
                sub(dve.scalar_tensor_tensor(x, k.aggt[:, q, :], 0.0, x, ALU.max, ALU.add), apart=True)
                wait_apart(dve, s["n_tr2"], b - 1)
                ins = layer_norm(dve, s["n_ln"], s["n_std"], b + 1, sub, k, x, k.lin_in[:, q, :])
                ins.then_inc(s["n_in"], 1)

            def table(b, q):
                dve.wait_ge(s["n_mm2"], b + 1)
                dve.tensor_scalar(block_of(k.zf, b), mm2[q][:, 0:D], k.dinv1[:, bass.ds(b, 1)], None,
                                  ALU.mult).then_inc(s["n_z"], 1)

            def step(b, u):
                q = u % 2
                gather(b, q)
                if not (isinstance(b, int) and b == 0):
                    update(b - 1, 1 - q)
                if not (isinstance(b, int) and b <= 1):
                    table(b - 2, q)

            looped(dve, NB, 4, step)
            update(NB - 1, (NB - 1) % 2)
            table(NB - 2, (NB - 2) % 2)
            table(NB - 1, (NB - 1) % 2)

        @block.gpsimd
        def _(pool):
            def split(b, q):
                wait_apart(pool, s["n_z"], b + 1)
                sub = Chain(pool, s["n_split"], 4 * b)
                sub(split3(pool, sub, block_of(k.zf, b), k.rem[:, :], parts_of(k.z3b, b)))

            looped(pool, NB, 2, split)



def layers(nc, k):
    gcn1 = dict(matrix="a", dinv=k.dinv1, loop=False)
    gcn3 = dict(matrix="a", dinv=k.dinv3, loop=True)
    plan = [
        dict(gcn1, bias=2, then="linear", w=k.wl[:, 1, :], out_dinv=k.dinv1),
        dict(gcn1, bias=3, then="linear", w=k.wl[:, 2, :], out_dinv=k.dinv1),
        dict(gcn1, bias=4, then="norm"),
        dict(matrix="at", dinv=None, loop=False, bias=None, then="norm linear", w=k.wl[:, 3, :], out_dinv=k.dinv3),
        dict(gcn3, bias=5, then="linear", w=k.wl[:, 4, :], out_dinv=k.dinv3),
        dict(gcn3, bias=6, then="linear", w=k.w3[:, :], out_dinv=k.dinv3),
        dict(gcn3, bias=7, then="out"),
    ]
    s = {n: k.sem("l_" + n) for n in ("ov", "sum", "ready", "tr", "trs", "mm", "z", "split", "ln", "std", "ovdma")}
    strip, out = [k.sem(f"l_strip{q}") for q in range(NS)], [k.sem(f"l_out{q}") for q in range(2)]
    linear = norms = 0
    for n, spec in enumerate(plan):
        layer(nc, k, s, strip, out, n, spec, linear * NB, norms * NB)
        linear += "linear" in spec["then"]
        norms += "norm" in spec["then"]


def layer(nc, k, s, strip, out, n, spec, lin0, ln0):
    strips = k.arena[:, 0:NS * J * P // 2].bitcast(BF16).rearrange("p (s j c) -> p s j c", s=NS, j=J)
    matrix = k.a_d if spec["matrix"] == "a" else k.at_d
    z3, z3n = (k.z3b, k.z3a) if n % 2 == 0 else (k.z3a, k.z3b)
    n0 = n * NB
    has_linear, has_norm, is_out = "linear" in spec["then"], "norm" in spec["then"], spec["then"] == "out"
    chain, splits = k.sem(f"l_c{n}"), k.sem(f"l_k{n}")
    acc, tr, mm = k.bank[0:2], k.bank[2], k.bank[3:5]

    def slot_base(q):
        return 16 * n * len(range(q, NB, NS))

    with nc.Block() as block:

        @block.sync
        def _(sp):
            def load(b, q):
                sp.dma_start(strips[:, q, :, :].rearrange("p j c -> p (j c)"),
                             matrix[bass.ds(b, 1), :, :].rearrange("o p c -> p (o c)")).then_inc(strip[q], 16)

            def step(b, q):
                sp.wait_ge(s["sum"], n0 + b + 1)
                load(b + NS, q)

            for b in range(NS):
                load(b, b)
            looped(sp, NB - NS, NS, step)

        @block.tensor
        def _(pe):
            def half(b, u, lo, hi):
                for a in range(lo, hi):
                    rhs = z3[:, a, :, :] if a < NB else z3[:, bass.ds(b, 1), :, :].rearrange("p o i f -> p (o i) f")
                    ins = pe.matmul(acc[u % 2][:, 0:ZW], strips[:, u, a, :], rhs.rearrange("p i f -> p (i f)"),
                                    start=(a == 0), stop=(a == J - 1))
                return ins

            def turn(b, q):
                wait_apart(pe, s["ready"], n0 + b + 1)
                pe.transpose(tr[0:D, 0:P], k.lin_in[:, q, :], k.ident[:, :]).then_inc(s["tr"], 1)

            def linear(b, q):
                pe.wait_ge(s["trs"], lin0 + b + 1)
                pe.matmul(mm[q][:, 0:D], k.linT[:, :], spec["w"], start=True, stop=True).then_inc(s["mm"], 1)

            def step(b, u):
                pe.wait_ge(strip[u], slot_base(u) + (16 * (b // NS) + 16 if isinstance(b, int)
                                                       else (b - u) * (16 // NS) + 16))
                wait(pe, s["ready"], n0 + b - 1 if not (isinstance(b, int) and b < 2) else 0)
                prev = has_linear and not (isinstance(b, int) and b == 0)
                half(b, u, 0, J // 2)
                if prev:
                    turn(b - 1, (u - 1) % 2)
                half(b, u, J // 2, J).then_inc(s["sum"], 1)
                if prev:
                    linear(b - 1, (u - 1) % 2)

            looped(pe, NB, NS, step)
            if has_linear:
                turn(NB - 1, (NB - 1) % 2)
                linear(NB - 1, (NB - 1) % 2)

        @block.scalar
        def _(act):
            def root(b):
                act.wait_ge(s["ln"], ln0 + b + 1)
                act.activation(k.std[:, :], k.mv[:, 1:2], ACT.Sqrt, bias=k.epsc[:, :]).then_inc(s["std"], 1)

            def keep(b):
                act.wait_ge(s["tr"], lin0 + b + 1)
                act.copy(k.linT[:, :], tr[0:D, 0:P]).then_inc(s["trs"], 1)

            def step(b, q):
                if has_norm:
                    root(b)
                if has_linear:
                    keep(b)

            def store(b, q, rows):
                act.wait_ge(s["ready"], n0 + b + 1)
                act.dma_start(k.inp["out"][bass.ds(b * P, rows), :], k.outb[0:rows, q, :]).then_inc(out[q], 16)

            if is_out:
                looped(act, NB - 1, 2, lambda b, q: store(b, q, P))
                store(NB - 1, (NB - 1) % 2, LAST)
                for q in range(2):
                    act.wait_ge(out[q], 16 * len(range(q, NB, 2)))
            elif has_norm or has_linear:
                looped(act, NB, 2, step)

        @block.vector
        def _(dve):
            LINKS = 2 + spec["loop"] + (spec["dinv"] is not None) + 4 * has_norm

            def epilogue(b, q):
                link = Chain(dve, chain, b * LINKS)
                own = bass.ds(b, 1)
                x, agg = block_of(k.xres, b), k.aggt[:, q, :]
                dve.wait_ge(s["sum"], n0 + b + 1)
                link(dve.tensor_reduce(agg, acc[q][:, 0:ZW].rearrange("p (i f) -> p f i", i=PARTS), AX, ALU.add))
                if isinstance(b, int) and b == 0:
                    dve.wait_ge(s["ov"], n + 1)
                link(dve.tensor_tensor(agg, agg, block_of(k.ovf, b), ALU.add))
                if spec["loop"]:
                    link(dve.tensor_tensor(agg, agg, block_of(k.zf, b), ALU.add))
                if spec["dinv"] is not None:
                    link(dve.scalar_tensor_tensor(agg, agg, spec["dinv"][:, own], k.bias[:, spec["bias"], :],
                                                  ALU.mult, ALU.add))
                if is_out:
                    wait(dve, out[q], 16 * (b // 2) if isinstance(b, int) else (b - q) * 8)
                    dve.tensor_tensor(k.outb[:, q, :], agg, x, ALU.add).then_inc(s["ready"], 1)
                elif not has_norm:
                    dve.tensor_scalar(k.lin_in[:, q, :], agg, 0.0, None, ALU.max).then_inc(s["ready"], 1)
                else:
                    if spec["dinv"] is not None:
                        link(dve.scalar_tensor_tensor(x, agg, 0.0, x, ALU.max, ALU.add), apart=True)
                    else:
                        link(dve.tensor_tensor(x, agg, x, ALU.add), apart=True)
                    dst = k.lin_in[:, q, :] if has_linear else block_of(k.zf, b)
                    layer_norm(dve, s["ln"], s["std"], ln0 + b + 1, link, k, x, dst).then_inc(s["ready"], 1)
                assert link.n == LINKS, (link.n, LINKS)

            def table(b, q):
                dve.wait_ge(s["mm"], lin0 + b + 1)
                dve.tensor_scalar(block_of(k.zf, b), mm[q][:, 0:D], spec["out_dinv"][:, bass.ds(b, 1)], None,
                                  ALU.mult).then_inc(s["z"], 1)

            def step(b, q):
                epilogue(b, q)
                if has_linear and not (isinstance(b, int) and b == 0):
                    table(b - 1, 1 - q)

            looped(dve, NB, 2, step)
            if has_linear:
                table(NB - 1, (NB - 1) % 2)

        @block.gpsimd
        def _(pool):
            overflow_sum(pool, k, s["ovdma"], spec["matrix"] == "at")
            pool.sem_inc(s["ov"], 1)

            def split(b, q):
                if has_linear:
                    wait_apart(pool, s["z"], lin0 + b + 1)
                else:
                    wait_apart(pool, s["ready"], n0 + b + 1)
                sub = Chain(pool, splits, 4 * b)
                sub(split3(pool, sub, block_of(k.zf, b), k.rem[:, :], parts_of(z3n, b)))

            if not is_out:
                looped(pool, NB, 2, split)


CAPO = CAP
CAPD = 2 * CAP
WLOADS = 1 + GT + 3 + 5 + 8 + 1

_INS = ["x", "L0_gnn_W1", "L0_gnn_W2", "L1_gnn_W0", "L1_gnn_W1", "L1_gnn_W2", "L3_gnn_W1", "L3_gnn_W2", "L3_gnn_W3",
        "L0_gnn_b1", "L0_gnn_b2", "L1_gnn_b0", "L1_gnn_b1", "L1_gnn_b2", "L3_gnn_b1", "L3_gnn_b2", "L3_gnn_b3"]


def kernel(**inputs):
    import numpy as np
    import concourse.bacc as bacc
    from concourse.bass_utils import run_bass_kernel_spmd

    arrays = {name: np.ascontiguousarray(inputs[name]) for name in _INS}
    for name in ("src", "dst"):
        padded = np.full((EP,), PADNODE, np.int32)
        padded[:E] = np.asarray(inputs[name])
        arrays[name] = padded.reshape(P, T)
    attrs = np.zeros((EP, FE), np.float32)
    attrs[:E] = np.asarray(inputs["edge_attr_32"])
    attrs = attrs.reshape(P, NG, GT, FE).transpose(1, 2, 3, 0)
    arrays["attr_T"] = np.ascontiguousarray(attrs).reshape(NG, P, P)
    arrays["u0_in"] = np.ascontiguousarray(np.asarray(inputs["L0_gnn_u"])[0:1].T)

    nc = bacc.Bacc("TRN2", target_bir_lowering=False, num_devices=1)
    t = {n: nc.dram_tensor(f"in_{n}", a.shape, mybir.dt.from_np(a.dtype), kind="ExternalInput").ap()
         for n, a in arrays.items()}
    t["out"] = nc.dram_tensor("out_x", (N, D), F32, kind="ExternalOutput").ap()
    build(nc, t)
    r = run_bass_kernel_spmd(nc, [{f"in_{n}": a for n, a in arrays.items()}], core_ids=[0])
    return r.results[0]["out_x"]
```

```python
from contextlib import ExitStack

import concourse.bass as bass
from concourse import mybir

P = 128
N = 6250
E = 206250
D = 64
FE = 32
FG = 32
NB = -(-N // P)
NP = NB * P
LAST = N - (NB - 1) * P
GT = 4
UN = 4
T = -(-E // (P * GT * UN)) * GT * UN
NG = T // GT
EP = P * T
PADNODE = 8191
ROW = D + 4
C_SLO, C_DLO, C_SRC, C_DST = D, D + 1, D + 2, D + 3
CAP = P
J = NB + 1
SLOTS = NP * J
OVB = SLOTS
ROWS = SLOTS + EP
BIG = 1.0e6
PARTS = 3
ZW = PARTS * D
SG = -(-J // GT)
EU = 2
NS = 4
LATE = 3 * J // 4
BN = 7
TAIL = 3
EPS = 1e-5

F32 = mybir.dt.float32
BF16 = mybir.dt.bfloat16
I32 = mybir.dt.int32
ALU = mybir.AluOpType
ACT = mybir.ActivationFunctionType
AX = mybir.AxisListType.X


class Names:
    pass


class Chain:

    def __init__(self, eng, sem, base):
        self.eng, self.sem, self.base, self.n = eng, sem, base, 0

    def __call__(self, ins, apart=False):
        self.n += 1
        ins.then_inc(self.sem, 1)
        (wait_apart if apart else wait)(self.eng, self.sem, self.base + self.n)


def looped(eng, count, unroll, body):
    for n in range(min(unroll, count)):
        body(n, n)
    rounds = count // unroll
    if rounds > 2:
        with eng.Fori(1, rounds) as i:
            for q in range(unroll):
                body(i * unroll + q, q)
    else:
        for n in range(unroll, rounds * unroll):
            body(n, n % unroll)
    for n in range(max(rounds, 1) * unroll, count):
        body(n, n % unroll)


def wait(eng, sem, value):
    if isinstance(value, int) and value <= 0:
        return
    eng.wait_ge(sem, value)


def wait_apart(eng, sem, value):
    if isinstance(value, int):
        return wait(eng, sem, value)
    value = eng.to_reg(value)
    eng.wait_ge(sem, 1)
    eng.wait_ge(sem, value)


def build(nc, t):
    with ExitStack() as ctx:
        k = Names()
        k.inp = t

        def sb(name, shape, dt=F32):
            return ctx.enter_context(nc.sbuf_tensor(name, shape, dt))

        k.sem = lambda name: ctx.enter_context(nc.semaphore(name))
        k.bank = [ctx.enter_context(nc.psum_tensor(f"bank{i}", [P, 512], F32)) for i in range(8)]

        k.rows_d = nc.dram_tensor("rows_d", (ROWS, ROW), F32, kind="Internal").ap()
        k.a_d = nc.dram_tensor("a_d", (NB, P, J * P), BF16, kind="Internal").ap()
        k.at_d = nc.dram_tensor("at_d", (NB, P, J * P), BF16, kind="Internal").ap()
        k.z_d = nc.dram_tensor("z_d", (NP, D), F32, kind="Internal").ap()
        k.ov_d = nc.dram_tensor("ov_d", (NP, D), F32, kind="Internal").ap()
        k.degov_d = nc.dram_tensor("degov_d", (NP, 1), F32, kind="Internal").ap()

        k.xres = sb("xres", [P, NB, D])
        k.strip_h = sb("strip_h", [P, J * P], BF16)
        k.strip_agg = sb("strip_agg", [P, J * P], BF16)
        k.h0 = k.strip_h[:, :].bitcast(F32)[:, 0:NB * D].rearrange("p (b f) -> p b f", f=D)
        k.agg0 = k.strip_agg[:, :].bitcast(F32)[:, 0:NB * D].rearrange("p (b f) -> p b f", f=D)
        k.zf = sb("zf", [P, NB, D])
        k.ovf = sb("ovf", [P, NB, D])
        k.z3a = sb("z3a", [P, NB, PARTS, D], BF16)
        k.z3b = sb("z3b", [P, NB, PARTS, D], BF16)
        k.deg = sb("deg", [P, NB])
        k.degov = sb("degov", [P, NB])
        k.degp = sb("degp", [P, SG, NB])
        k.dinv1 = sb("dinv1", [P, NB])
        k.dinv3 = sb("dinv3", [P, NB])
        k.dtmp = sb("dtmp", [P, NB])
        k.iota = sb("iota", [P, P])
        k.ident = sb("ident", [P, P])
        k.identb = sb("identb", [P, P], BF16)
        k.notbefore = sb("notbefore", [P, P], BF16)
        k.negfrom = sb("negfrom", [P, P], BF16)
        k.onesb = sb("onesb", [P, P], BF16)
        k.ones4 = sb("ones4", [P, GT])
        k.epsc = sb("epsc", [P, 1])
        k.minus1 = sb("minus1", [P, 1])
        k.w1n = sb("w1n", [D, D])
        k.w1e4 = sb("w1e4", [P, GT, D])
        k.w2na = sb("w2na", [P, D])
        k.w2u = sb("w2u", [FG, D])
        k.u0 = sb("u0", [FG, 1])
        k.u0b = sb("u0b", [FG, P])
        k.c2 = sb("c2", [P, D])
        k.wl = sb("wl", [D, 5, D])
        k.w3 = sb("w3", [D, D])
        k.bias = sb("bias", [P, 8, D])
        k.lin_in = sb("lin_in", [P, 2, D])
        k.linT = sb("linT", [D, P])
        k.aggt = sb("aggt", [P, 2, D])
        k.st6 = sb("st6", [P, 6])
        k.mv = sb("mv", [P, 2])
        k.std = sb("std", [P, 1])
        k.rstd = sb("rstd", [P, 1])
        k.rem = sb("rem", [P, D])
        k.outb = sb("outb", [P, 2, D])
        k.nov = sb("nov", [P, 1], I32)
        k.ovmeta = sb("ovmeta", [1, 2], I32)
        k.ovrow = sb("ovrow", [1, D])
        k.ovmsg = sb("ovmsg", [1, D])
        k.ovp = sb("ovp", [1, D])
        k.one1 = sb("one1", [1, 1])
        k.zeros = sb("zeros", [P, D])
        words = max(11 * T + 4 * GT + UN * GT * ROW + UN * P + 2 * GT * P, EU * J * ROW + (1 + EU // 2) * SG * GT * P,
                    (2 * NS - 1) * J * P // 2)
        k.arena = sb("arena", [P, words])
        k.run = sb("run", [P, D], BF16)
        k.intra = sb("intra", [P, 2, GT])
        k.junk = sb("junk", [P, GT * P], BF16)
        k.pick = sb("pick", [P, GT, D])
        k.sel = sb("sel", [P, GT])
        k.rank = sb("rank", [P, GT])
        k.over = sb("over", [P, 2, GT], BF16)
        k.second = sb("second", [P, GT])
        k.pos = sb("pos", [P, 2, GT])
        k.ovseen = sb("ovseen", [P, 2, GT])
        k.ovpos = sb("ovpos", [P, GT])
        k.posi = sb("posi", [P, UN, GT], I32)
        prologue(nc, k)
        bucket_stage(nc, k)
        edge_stage(nc, k)
        first_overflow(nc, k)
        strip_buffers(k)
        node_stage(nc, k)
        layers(nc, k)



def layer_norm(dve, act_sem, std_sem, count, link, k, src, dst):
    link(dve.bn_stats(k.st6[:, :], src), apart=True)
    dve.bn_aggr(k.mv[:, :], k.st6[:, :]).then_inc(act_sem, 1)
    dve.wait_ge(std_sem, count)
    link(dve.reciprocal(k.rstd[:, :], k.std[:, :]))
    link(dve.tensor_scalar(dst, src, k.mv[:, 0:1], k.rstd[:, 0:1], ALU.subtract, ALU.mult))
    return dve.tensor_scalar(dst, dst, 0.0, None, ALU.max)


def split3(pool, link, z, rem, parts):
    link(pool.tensor_copy(parts[0], z), apart=True)
    link(pool.tensor_tensor(rem, z, parts[0], ALU.subtract), apart=True)
    link(pool.tensor_copy(parts[1], rem), apart=True)
    return pool.tensor_tensor(parts[2], rem, parts[1], ALU.subtract)


def block_of(tile, b):
    return tile[:, bass.ds(b, 1), :].rearrange("p o f -> p (o f)")


def parts_of(tile, b):
    return [tile[:, bass.ds(b, 1), i, :].rearrange("p o f -> p (o f)") for i in range(PARTS)]


def node_rows(dram):
    return dram.rearrange("(b p) f -> p b f", p=P)



def prologue(nc, k):
    words = k.arena[:, :]
    k.ab_val = words[:, 0:2 * (T + 2 * GT)]
    o = 2 * (T + 2 * GT)
    k.meta = words[:, o:o + 4 * T]
    o += 4 * T
    k.pos0 = words[:, o:o + T]
    k.cap = words[:, o + T:o + 2 * T]
    k.hop = words[:, o + 2 * T:o + 3 * T]
    k.srci = words[:, o + 3 * T:o + 4 * T].bitcast(I32)
    k.dsti = words[:, o + 4 * T:o + 5 * T].bitcast(I32)
    o += 5 * T
    k.rowbuf = words[:, o:o + UN * GT * ROW].rearrange("p (u j c) -> p u j c", u=UN, j=GT)
    o += UN * GT * ROW
    k.attrT = words[:, o:o + UN * P].rearrange("p (u l) -> p u l", u=UN)
    o += UN * P
    onehots = words[:, o:o + 2 * GT * P].bitcast(BF16).rearrange("p (x q j e) -> p x q j e", x=2, q=2, j=GT)
    k.ab, k.abT = onehots[:, 0, :, :, :], onehots[:, 1, :, :, :]

    k.slotrow = k.z3b[:, :, :, :].rearrange("p b i f -> p (b i f)").bitcast(F32)[:, 0:J * ROW]
    s = {n: k.sem(n) for n in ("p_x", "p_idx", "p_w", "p_clear", "p_const", "p_c", "p_k", "p_slot", "p_zero",
                               "p_ln", "p_std", "p_in", "p_tr", "p_trs", "p_mm", "p_z", "p_split", "p_u", "p_c2")}
    tr, mm, cps = k.bank[0], k.bank[1:3], k.bank[3]
    meta = k.meta.rearrange("p (t c) -> p t c", c=4)
    metai = meta.bitcast(I32)
    abv = k.ab_val.rearrange("p (t c) -> p t c", c=2)

    with nc.Block() as block:

        @block.sync
        def _(sp):
            x = k.inp["x"]
            sp.wait_ge(s["p_zero"], 1)
            sp.dma_start(k.xres[:, 0:NB - 1, :], x[0:(NB - 1) * P].rearrange("(b p) f -> p b f", p=P)
                         ).then_inc(s["p_x"], 16)
            sp.dma_start(k.xres[0:LAST, NB - 1, :], x[(NB - 1) * P:N]).then_inc(s["p_x"], 16)
            sp.dma_start(k.srci, k.inp["src"]).then_inc(s["p_idx"], 16)
            sp.dma_start(k.dsti, k.inp["dst"]).then_inc(s["p_idx"], 16)
            sp.dma_start(k.w1n[:, :], k.inp["L0_gnn_W1"][0:D]).then_inc(s["p_w"], 16)
            for j in range(GT):
                sp.dma_start(k.w1e4[FE * j:FE * (j + 1), j, :], k.inp["L0_gnn_W1"][D:D + FE]).then_inc(s["p_w"], 16)
            sp.dma_start(k.w2na[:, :], k.inp["L0_gnn_W2"][0:P]).then_inc(s["p_w"], 16)
            sp.dma_start(k.w2u[:, :], k.inp["L0_gnn_W2"][P:P + FG]).then_inc(s["p_w"], 16)
            sp.dma_start(k.u0[:, :], k.inp["u0_in"]).then_inc(s["p_w"], 16)
            for i, w in enumerate((k.inp["L1_gnn_W0"], k.inp["L1_gnn_W1"], k.inp["L1_gnn_W2"], k.inp["L3_gnn_W1"], k.inp["L3_gnn_W2"])):
                sp.dma_start(k.wl[:, i, :], w).then_inc(s["p_w"], 16)
            for i, b in enumerate((k.inp["L0_gnn_b1"], k.inp["L0_gnn_b2"], k.inp["L1_gnn_b0"], k.inp["L1_gnn_b1"], k.inp["L1_gnn_b2"],
                                   k.inp["L3_gnn_b1"], k.inp["L3_gnn_b2"], k.inp["L3_gnn_b3"])):
                sp.dma_start(k.bias[:, i, :], b.partition_broadcast(P)).then_inc(s["p_w"], 16)
            sp.dma_start(k.w3[:, :], k.inp["L3_gnn_W3"]).then_inc(s["p_w"], 16)
            sp.wait_ge(s["p_slot"], 1)
            for b in range(NB):
                sp.dma_start(k.rows_d[b * P * J:(b + 1) * P * J].rearrange("(p j) c -> p (j c)", p=P),
                             k.slotrow).then_inc(s["p_clear"], 16)
            sp.wait_ge(s["p_slot"], 2)
            sp.dma_start(node_rows(k.ov_d), k.ovf[:, :, :]).then_inc(s["p_clear"], 16)
            with nc.allow_non_contiguous_dma(reason="one word per node"):
                sp.dma_start(k.degov_d.rearrange("(b p) f -> p (b f)", p=P), k.degov[:, :]).then_inc(s["p_clear"], 16)
            sp.wait_ge(s["p_clear"], 16 * (NB + 2))

        @block.gpsimd
        def _(pool):
            link = Chain(pool, s["p_k"], 0)
            link(pool.iota(k.iota[:, :], [[1, P]], base=0, channel_multiplier=0, allow_small_or_imprecise_dtypes=True))
            link(pool.memset(k.ident[:, :], 0.0))
            link(pool.affine_select(out=k.ident[:, :], in_=k.ident[:, :], compare_op=ALU.not_equal, fill=1.0, base=0,
                                    pattern=[[-1, P]], channel_multiplier=1))
            pool.tensor_copy(k.identb[:, :], k.ident[:, :])
            link(pool.memset(k.notbefore[:, :], -2.0))
            link(pool.affine_select(out=k.notbefore[:, :], in_=k.notbefore[:, :], compare_op=ALU.is_ge, fill=0.0,
                                    base=0, pattern=[[1, P]], channel_multiplier=-1))
            link(pool.memset(k.negfrom[:, :], -1.0))
            link(pool.affine_select(out=k.negfrom[:, :], in_=k.negfrom[:, :], compare_op=ALU.is_ge, fill=0.0,
                                    base=0, pattern=[[-1, P]], channel_multiplier=1))
            pool.memset(k.one1[:, :], 1.0)
            pool.memset(k.onesb[:, :], 1.0).then_inc(s["p_const"], 1)

            def split(b, q):
                wait_apart(pool, s["p_z"], b + 1)
                sub = Chain(pool, s["p_split"], 4 * b)
                sub(split3(pool, sub, block_of(k.zf, b), k.rem[:, :], parts_of(k.z3a, b)))

            looped(pool, NB, 2, split)

        @block.tensor
        def _(pe):
            pe.wait_ge(s["p_const"], 1)
            pe.wait_ge(s["p_w"], 16 * WLOADS)
            pe.wait_ge(s["p_u"], 1)
            pe.matmul(cps[:, 0:D], k.u0b[:, :], k.w2u[:, :], start=True, stop=True).then_inc(s["p_c2"], 1)

            def step(b, q):
                wait_apart(pe, s["p_in"], b + 1)
                pe.transpose(tr[0:D, 0:P], k.lin_in[:, q, :], k.ident[:, :]).then_inc(s["p_tr"], 1)
                pe.wait_ge(s["p_trs"], b + 1)
                pe.matmul(mm[q][:, 0:D], k.linT[:, :], k.w1n[:, :], start=True, stop=True
                          ).then_inc(s["p_mm"], 1)

            looped(pe, NB, 2, step)

        @block.scalar
        def _(act):
            def step(b, q):
                act.wait_ge(s["p_ln"], b + 1)
                act.activation(k.std[:, :], k.mv[:, 1:2], ACT.Sqrt, bias=k.epsc[:, :]).then_inc(s["p_std"], 1)
                act.wait_ge(s["p_tr"], b + 1)
                act.copy(k.linT[:, :], tr[0:D, 0:P]).then_inc(s["p_trs"], 1)

            looped(act, NB, 2, step)

        @block.vector
        def _(dve):
            link = Chain(dve, s["p_c"], 0)
            link(dve.memset(k.slotrow, 0.0))
            dve.memset(k.slotrow.rearrange("p (j c) -> p j c", c=ROW)[:, :, C_SLO:C_DLO + 1], -1.0
                       ).then_inc(s["p_slot"], 1)
            link(dve.memset(k.w1e4[:, :, :], 0.0))
            dve.memset(k.xres[:, NB - 1, :], 0.0).then_inc(s["p_zero"], 1)
            dve.memset(k.ovf[:, :, :], 0.0)
            dve.memset(k.epsc[:, :], EPS)
            dve.memset(k.zeros[:, :], 0.0)
            dve.memset(k.minus1[:, :], -1.0)
            dve.memset(k.run[:, :], 0.0)
            dve.memset(k.ones4[:, :], 1.0)
            dve.memset(k.ovseen[:, :, :], 0.0)
            dve.memset(k.agg0[:, :, :], 0.0)
            dve.memset(k.degov[:, :], 0.0).then_inc(s["p_slot"], 1)
            dve.wait_ge(s["p_idx"], 32)
            link(dve.memset(k.ab_val[:, 2 * T:], 0.0))
            for c, v in ((0, k.srci), (1, k.dsti)):
                tmp = k.pos0.bitcast(I32)
                link(dve.tensor_copy(metai[:, :, 2 + c], v))
                link(dve.tensor_scalar(tmp, v, 7, None, ALU.logical_shift_right))
                link(dve.tensor_copy(abv[:, 0:T, c], tmp))
                link(dve.tensor_scalar(tmp, v, P - 1, None, ALU.bitwise_and))
                link(dve.tensor_copy(meta[:, :, c], tmp))
            a, b = abv[:, 0:T, 0], abv[:, 0:T, 1]
            link(dve.tensor_tensor(k.cap, a, b, ALU.is_equal))
            link(dve.tensor_scalar(k.cap, k.cap, float(CAPD - CAPO), float(CAPO), ALU.mult, ALU.add))
            link(dve.tensor_scalar(k.hop, a, float(NB), BIG, ALU.is_ge, ALU.mult))
            link(dve.tensor_tensor(k.cap, k.cap, k.hop, ALU.add))
            link(dve.scalar_tensor_tensor(k.pos0, b, float(P * J), k.hop, ALU.mult, ALU.add))
            link(dve.tensor_tensor(k.pos0, k.pos0, a, ALU.add))
            link(dve.tensor_scalar(k.hop, a, -1.0, float(NB - P * J), ALU.mult, ALU.add))
            dve.wait_ge(s["p_w"], 16 * WLOADS)
            dve.tensor_copy(k.u0b[:, :], k.u0[:, 0:1].to_broadcast([FG, P])).then_inc(s["p_u"], 1)
            dve.wait_ge(s["p_c2"], 1)
            link(dve.tensor_tensor(k.c2[:, :], cps[:, 0:D], k.bias[:, 1, :], ALU.add))
            dve.wait_ge(s["p_x"], 32)
            first = link.n

            def norm(b, q):
                sub = Chain(dve, s["p_c"], first + 4 * b)
                ins = layer_norm(dve, s["p_ln"], s["p_std"], b + 1, sub, k, block_of(k.xres, b), block_of(k.h0, b))
                sub(ins, apart=True)
                wait_apart(dve, s["p_tr"], b - 1)
                dve.tensor_copy(k.lin_in[:, q, :], block_of(k.h0, b)).then_inc(s["p_in"], 1)

            def table(b, q):
                dve.wait_ge(s["p_mm"], b + 1)
                dve.tensor_tensor(block_of(k.zf, b), mm[q][:, 0:D], k.bias[:, 0, :], ALU.add
                                  ).then_inc(s["p_z"], 1)

            def step(b, q):
                norm(b, q)
                if not (isinstance(b, int) and b == 0):
                    table(b - 1, 1 - q)

            looped(dve, NB, 2, step)
            table(NB - 1, (NB - 1) % 2)



def bucket_stage(nc, k):
    loaded = [k.sem(f"attr_loaded{q}") for q in range(UN)]
    scattered = [k.sem(f"row_scattered{q}") for q in range(UN)]
    s = {n: k.sem(n) for n in ("onehot", "onehot_t", "onehot_ts", "same", "intra", "counted", "run", "over", "ovcount",
                               "projected", "q_kept", "tail", "pos", "b_c", "b_f")}
    meta = k.meta.rearrange("p (t c) -> p t c", c=4).bitcast(I32)
    LINKS, FLINKS = 5, 4

    turned = k.bank[0][:, 0:256].bitcast(BF16).rearrange("p (j e) -> p j e", j=GT)
    same = [k.bank[1][:, 0:P], k.bank[1][:, P:3 * P], k.bank[2][:, 0:3 * P], k.bank[3][:, 0:4 * P]]
    shared = 2
    ovbefore, ovtotal = k.bank[6][:, 0:GT], k.bank[6][:, GT:2 * GT]
    q_ps = k.bank[7][:, 0:GT * D]

    def picked(q):
        return k.bank[4 + q][:, 0:GT * D].rearrange("p (j f) -> p j f", j=GT)

    def counts(q):
        return k.bank[4 + q][:, GT * D:(GT + 1) * D]

    def slot_free(n, u):
        return 16 * GT * (n // UN) if isinstance(n, int) else (n - u) * (16 * GT // UN)

    with nc.Block() as block:

        @block.sync
        def _(sp):
            def load(n, u):
                wait(sp, s["projected"], n - UN + 1)
                sp.dma_start(k.attrT[:, u, :], k.inp["attr_T"][bass.ds(n, 1), :, :].rearrange("o p c -> p (o c)")
                             ).then_inc(loaded[u], 16)

            looped(sp, NG, UN, load)
            for u in range(UN):
                sp.wait_ge(scattered[u], 16 * GT * (NG // UN))

        @block.gpsimd
        def _(pool):
            limit = pool.to_reg(ROWS - 1)

            def scatter(n, u):
                wait_apart(pool, s["q_kept"], n + 1)
                wait_apart(pool, s["tail"], n + 1)
                wait_apart(pool, s["pos"], n + 1)
                for j in range(GT):
                    pool.indirect_dma_start(k.rows_d, bass.IndirectOffsetOnAxis(ap=k.posi[:, u, j:j + 1], axis=0),
                                            k.rowbuf[:, u, j, :], None, bounds_check=limit, oob_is_err=False
                                            ).then_inc(scattered[u], 16)

            looped(pool, NG, UN, scatter)

        @block.tensor
        def _(pe):
            def turn(n, q):
                pe.wait_ge(s["onehot"], n + 1)
                wait(pe, s["onehot_ts"], n)
                for j in range(GT):
                    ins = pe.transpose(turned[:, j, :], k.ab[:, q, j, :], k.identb[:, :])
                ins.then_inc(s["onehot_t"], 1)

            def project(n, u):
                pe.wait_ge(loaded[u], 16 * (n // UN) + 16 if isinstance(n, int) else (n - u) * (16 // UN) + 16)
                wait(pe, s["q_kept"], n)
                pe.matmul(q_ps, k.attrT[:, u, :], k.w1e4[:, :, :].rearrange("p j f -> p (j f)"), start=True, stop=True
                          ).then_inc(s["projected"], 1)

            def overflow(n, q):
                pe.wait_ge(s["over"], n + 1)
                wait(pe, s["pos"], n)
                pe.matmul(ovbefore, k.negfrom[:, :], k.over[:, q, :], start=True, stop=True)
                pe.matmul(ovtotal, k.onesb[:, :], k.over[:, q, :], start=True, stop=True).then_inc(s["ovcount"], 1)

            def step(n, u):
                q = u % 2
                pe.wait_ge(s["onehot_ts"], n + 1)
                for j in range(GT):
                    if j != shared - 1:
                        last = max(j + 1, shared) - GT
                        wait(pe, s["intra"], GT * n + last)
                    out = same[j]
                    pe.matmul(out, k.abT[:, q, j, :], k.abT[:, q, 0:j + 1, :].rearrange("p j e -> p (j e)"),
                              start=True, stop=False)
                    pe.matmul(out[:, j * P:(j + 1) * P], k.identb[:, :], k.notbefore[:, :], start=False, stop=True
                              ).then_inc(s["same"], 1)
                turn(n + 1, 1 - q)
                project(n, u)
                wait(pe, s["over"], n - 1)
                wait(pe, s["run"], n)
                for j in range(GT):
                    pe.matmul(picked(q)[:, j, :], k.abT[:, q, j, :], k.run[:, :], start=True, stop=True)
                for j in range(GT):
                    ins = pe.matmul(counts(q), k.ab[:, q, j, :], k.ab[:, q, j, D:2 * D],
                                    start=(j == 0), stop=(j == GT - 1))
                ins.then_inc(s["counted"], 1)
                if not (isinstance(n, int) and n == 0):
                    overflow(n - 1, 1 - q)

            turn(0, 0)
            looped(pe, NG, UN, step)
            overflow(NG - 1, (NG - 1) % 2)

        @block.scalar
        def _(act):
            def keep(n, q):
                wait(act, s["counted"], n - 1)
                act.wait_ge(s["onehot_t"], n + 1)
                act.copy(k.abT[:, q, :, :], turned).then_inc(s["onehot_ts"], 1)

            def step(n, u):
                q = u % 2
                wait(act, s["over"], n - 1)
                for j in range(GT):
                    if j:
                        act.wait_ge(s["intra"], GT * n + j)
                    act.wait_ge(s["same"], GT * n + max(j + 1, shared))
                    act.activation(k.junk[:, 0:(j + 1) * P], same[j], ACT.Relu, bias=k.minus1[:, :],
                                   accum_out=k.intra[:, q, j:j + 1]).then_inc(s["intra"], 1)
                keep(n + 1, 1 - q)
                act.wait_ge(s["projected"], n + 1)
                wait(act, scattered[u], slot_free(n, u))
                act.copy(k.rowbuf[:, u, :, 0:D], q_ps.rearrange("p (j f) -> p j f", j=GT)).then_inc(s["q_kept"], 1)

            keep(0, 0)
            looped(act, NG, UN, step)

        @block.vector
        def _(dve):
            def onehot(n, q):
                wait(dve, s["counted"], n - 1)
                val = k.ab_val[:, bass.ds(n * 2 * GT, 2 * GT)]
                dve.tensor_tensor(k.ab[:, q, :, :].rearrange("p j (c e) -> p (j c) e", c=2),
                                  k.iota[:, 0:D].unsqueeze(1).to_broadcast([P, 2 * GT, D]),
                                  val.unsqueeze(2).to_broadcast([P, 2 * GT, D]), ALU.is_equal
                                  ).then_inc(s["onehot"], 1)

            def step(n, u, now=True, prev=True):
                q, w, v = u % 2, 1 - u % 2, (u - 1) % UN
                tiles = bass.ds(n * GT, GT)

                def link(ins):
                    ins.then_inc(s["b_c"], 1)

                def after(i):
                    dve.wait_ge(s["b_c"], n * LINKS + i)

                def flink(ins):
                    ins.then_inc(s["b_f"], 1)

                def fafter(i):
                    dve.wait_ge(s["b_f"], (n - 1) * FLINKS + i)

                if now:
                    dve.wait_ge(s["counted"], n + 1)
                    dve.tensor_tensor(k.run[0:D, :], counts(q)[0:D, :], k.run[0:D, :], ALU.add).then_inc(s["run"], 1)
                    link(dve.tensor_tensor(k.pick[:, :, :], picked(q), k.ab[:, q, :, D:2 * D], ALU.mult))
                if prev:
                    dve.wait_ge(s["ovcount"], n)
                    flink(dve.tensor_tensor_scan(k.ovseen[:, w, :], k.ones4[:, :], ovtotal, k.ovseen[:, q, GT - 1:GT],
                                                 ALU.mult, ALU.add))
                if now:
                    after(1)
                    link(dve.tensor_reduce(k.sel[:, :], k.pick[:, :, :], AX, ALU.add))
                    onehot(n + 2, q)
                if prev:
                    fafter(1)
                    flink(dve.scalar_tensor_tensor(k.ovpos[:, :], ovbefore, float(OVB), k.ovseen[:, w, :],
                                                   ALU.add, ALU.add))
                if now:
                    dve.wait_ge(s["intra"], GT * n + GT)
                    after(2)
                    link(dve.tensor_tensor(k.rank[:, :], k.sel[:, :], k.intra[:, q, :], ALU.add))
                if prev:
                    fafter(2)
                    flink(dve.tensor_tensor(k.ovpos[:, :], k.ovpos[:, :], k.pos[:, w, :], ALU.subtract))
                if now:
                    after(3)
                    dve.tensor_tensor(k.over[:, q, :], k.rank[:, :], k.cap[:, tiles], ALU.is_ge).then_inc(s["over"], 1)
                    dve.scalar_tensor_tensor(k.second[:, :], k.rank[:, :], float(P), k.hop[:, tiles],
                                             ALU.is_ge, ALU.mult)
                    link(dve.scalar_tensor_tensor(k.pos[:, q, :], k.rank[:, :], float(J), k.pos0[:, tiles],
                                                  ALU.mult, ALU.add))
                if prev:
                    fafter(3)
                    flink(dve.tensor_tensor(k.ovpos[:, :], k.ovpos[:, :], k.over[:, w, :], ALU.mult))
                if now:
                    wait(dve, scattered[u], slot_free(n, u))
                    dve.tensor_copy(k.rowbuf[:, u, :, :].bitcast(I32)[:, :, C_SLO:ROW], meta[:, tiles, :]
                                    ).then_inc(s["tail"], 1)
                    after(4)
                    link(dve.tensor_tensor(k.pos[:, q, :], k.pos[:, q, :], k.second[:, :], ALU.add))
                if prev:
                    fafter(4)
                    dve.tensor_tensor(k.posi[:, v, :], k.pos[:, w, :], k.ovpos[:, :], ALU.add).then_inc(s["pos"], 1)
                if now:
                    after(LINKS)

            onehot(0, 0)
            onehot(1, 1)
            looped(dve, NG, UN, lambda n, u: step(n, u, prev=not isinstance(n, int) or n > 0))
            step(NG, NG % UN, now=False)
            dve.wait_ge(s["pos"], NG)
            dve.tensor_copy(k.nov[:, :], k.ovseen[:, (NG - 1) % 2, GT - 1:GT])



def edge_buffers(k):
    table = k.z3b[:, :, :, :].rearrange("p b i f -> p (b i f)").bitcast(F32)

    def taker(space):
        at = [0]

        def take(shape, dt):
            n = 1
            for d in shape:
                n *= d
            words = n if dt == F32 else n // 2
            part = space[:, at[0]:at[0] + words]
            at[0] += words
            names = "abcd"[:len(shape)]
            return (part if dt == F32 else part.bitcast(dt)).rearrange(
                f"p ({' '.join(names)}) -> p {' '.join(names)}", **dict(zip(names, shape)))
        return take

    take, take_table = taker(k.arena), taker(table)
    k.strip = take((EU, J, ROW), F32)
    k.oh = take((SG, GT * 2, P), BF16).rearrange("p g (j e) c -> p g j e c", e=2)
    k.attile = take((SG, GT * EU, P), BF16).rearrange("p g (j r) c -> p g j r c", r=EU)
    k.ohf = take_table((EU, GT, P), F32)
    k.dT = take_table((EU, GT, P), BF16)
    k.presum = take_table((EU, GT, D), F32)
    k.msg = take_table((EU, GT, D), F32)
    some = k.ovf[:, :, :].rearrange("p b f -> p (b f)").bitcast(BF16)
    k.atile = [some[:, g * GT * P:(g + 1) * GT * P].rearrange("p (j c) -> p j c", c=P) for g in range(SG - 1)]
    k.atile.append(take_table((GT, P), BF16))


class Group:

    def __init__(self, b, r, g):
        self.b, self.r, self.g = b, r, g
        self.n, self.q, self.m = SG * b + g, (SG * r + g) % EU, min(GT, J - GT * g)


def edge_stage(nc, k):
    edge_buffers(k)
    strip = [k.sem(f"strip{q}") for q in range(EU)]
    a_out = [k.sem(f"a_out{g}") for g in range(SG)]
    at_out = [k.sem(f"at_out{g}") for g in range(SG)]
    s = {n: k.sem(n) for n in ("lanes", "lanes_f", "turned", "a_sum", "at_sum", "d_t", "a_kept", "at_kept", "gathered",
                               "presum", "message", "summed", "added", "e_c")}

    def group(b, r, g, back=0):
        if g - back < 0:
            b, r, g = b - 1, (r - 1) % EU, g + SG
        elif g - back >= SG:
            b, r, g = b + 1, (r + 1) % EU, g - SG
        g -= back
        if isinstance(b, int) and not 0 <= b < NB:
            return None
        return Group(b, r, g)

    a_ps, at_ps = k.bank[0], k.bank[1]
    d_t = k.bank[2][:, 0:256].bitcast(BF16).rearrange("p (j e) -> p j e", j=GT)

    def gat(q):
        return k.bank[4 + q][:, 0:GT * D]

    def tot(q):
        return k.bank[6 + q][:, 0:GT * D].rearrange("p (j f) -> p j f", j=GT)

    cuts = [J * i // EU for i in range(EU + 1)]

    def strip_loaded(b, r):
        return 16 * EU * (b // EU) + 16 * EU if isinstance(b, int) else (b - r) * 16 + 16 * EU

    last = (NB - 1, (NB - 1) % EU, SG - 1)

    with nc.Block() as block:

        @block.sync
        def _(sp):
            def load(b, r):
                src = k.rows_d[bass.ds(b * (P * J), P * J), :] if not isinstance(b, int) else \
                    k.rows_d[b * P * J:(b + 1) * P * J]
                src = src.rearrange("(p j) c -> p j c", p=P)
                for lo, hi in zip(cuts, cuts[1:]):
                    sp.dma_start(k.strip[:, r, lo:hi, :], src[:, lo:hi, :]).then_inc(strip[r], 16)

            def step(b, r, more=True):
                for g in range(SG):
                    t = group(b, r, g)
                    sp.wait_ge(s["a_kept"], t.n + 1)
                    sp.dma_start(k.a_d[bass.ds(b, 1), :, GT * P * g:GT * P * g + t.m * P].rearrange("o p c -> p (o c)"),
                                 k.atile[g][:, 0:t.m, :].rearrange("p j c -> p (j c)")).then_inc(a_out[g], 16)
                    own = t.m if g < SG - 1 else t.m - 1
                    rows = k.at_d[GT * g:GT * g + own]
                    if r == EU - 1 or g == SG - 1 or (isinstance(b, int) and b == NB - 1):
                        sp.wait_ge(s["at_kept"], t.n + 1)
                    if r == EU - 1:
                        sp.dma_start(rows[:, :, bass.ds((b - r) * P, EU * P)].rearrange("a p c -> p a c"),
                                     k.attile[:, g, 0:own, :, :].rearrange("p j r c -> p j (r c)")
                                     ).then_inc(at_out[g], 16)
                    elif isinstance(b, int) and b == NB - 1:
                        sp.dma_start(rows[:, :, b * P:NB * P].rearrange("a p c -> p a c"), k.attile[:, g, 0:own, r, :]
                                     ).then_inc(at_out[g], 16)
                    if g == SG - 1:
                        sp.dma_start(k.at_d[bass.ds(b, 1), :, NB * P:J * P].rearrange("o p c -> p (o c)"),
                                     k.attile[:, g, t.m - 1, r, :]).then_inc(at_out[g], 16)
                if more:
                    sp.wait_ge(s["presum"], SG * b + SG)
                    load(b + EU, r)

            for b in range(EU):
                load(b, b)
            looped(sp, NB - EU, EU, step)
            for b in range(NB - EU, NB):
                step(b, b % EU, more=False)
            for g in range(SG):
                sp.wait_ge(a_out[g], 16 * NB)
                sp.wait_ge(at_out[g], 16 * (NB // EU + 1 + (NB if g == SG - 1 else 0)))

        @block.tensor
        def _(pe):
            def front(t):
                wait_apart(pe, s["lanes"], t.n + 1)
                wait(pe, s["d_t"], t.n)
                for j in range(t.m):
                    ins = pe.transpose(d_t[:, j, :], k.oh[:, t.g, j, 1, :], k.identb[:, :])
                ins.then_inc(s["turned"], 1)
                wait(pe, s["a_kept"], t.n)
                for j in range(t.m):
                    ins = pe.matmul(a_ps[:, j * P:(j + 1) * P], k.oh[:, t.g, j, 0, :], k.oh[:, t.g, j, 1, :],
                                    start=True, stop=True)
                ins.then_inc(s["a_sum"], 1)
                wait(pe, s["at_kept"], t.n)
                for j in range(t.m):
                    ins = pe.matmul(at_ps[:, j * P:(j + 1) * P], k.oh[:, t.g, j, 1, :], k.oh[:, t.g, j, 0, :],
                                    start=True, stop=True)
                ins.then_inc(s["at_sum"], 1)

            def gather(t):
                if t is None:
                    return
                table = parts_of(k.z3a, t.b)
                pe.wait_ge(s["d_t"], t.n + 1)
                wait(pe, s["presum"], t.n - EU + 1)
                for j in range(t.m):
                    out = gat(t.q)[:, j * D:(j + 1) * D]
                    for i in range(PARTS):
                        ins = pe.matmul(out, k.dT[:, t.q, j, :], table[i], start=(i == 0), stop=(i == PARTS - 1))
                ins.then_inc(s["gathered"], 1)

            def total(t):
                if t is None:
                    return
                pe.wait_ge(s["lanes_f"], t.n + 1)
                pe.wait_ge(s["message"], t.n + 1)
                wait(pe, s["added"], t.n - EU + 1)
                for j in range(t.m):
                    ins = pe.matmul(tot(t.q)[:, j, :], k.ohf[:, t.q, j, :], k.msg[:, t.q, j, :], start=True, stop=True)
                ins.then_inc(s["summed"], 1)

            def step(b, r):
                for g in range(SG):
                    front(group(b, r, g))
                    gather(group(b, r, g, 1))
                    total(group(b, r, g, 2))

            looped(pe, NB, EU, step)
            gather(group(*last))
            for back in (1, 0):
                total(group(*last, back))

        @block.scalar
        def _(act):
            def message(t):
                if t is None:
                    return
                act.wait_ge(s["presum"], t.n + 1)
                wait(act, s["summed"], t.n - EU + 1)
                act.activation(k.msg[:, t.q, 0:t.m, :], k.presum[:, t.q, 0:t.m, :], ACT.Relu
                               ).then_inc(s["message"], 1)

            def step(b, r):
                for g in range(SG):
                    t = group(b, r, g)
                    act.wait_ge(s["turned"], t.n + 1)
                    wait(act, s["gathered"], t.n - EU + 1)
                    act.copy(k.dT[:, t.q, 0:t.m, :], d_t[:, 0:t.m, :]).then_inc(s["d_t"], 1)
                    act.wait_ge(s["a_sum"], t.n + 1)
                    wait(act, a_out[g], b * 16)
                    act.copy(k.atile[g][:, 0:t.m, :].rearrange("p j c -> p (j c)"), a_ps[:, 0:t.m * P]
                             ).then_inc(s["a_kept"], 1)
                    act.wait_ge(s["at_sum"], t.n + 1)
                    if r == 0:
                        wait(act, at_out[g], b * (16 // EU + (16 if g == SG - 1 else 0)))
                    act.activation(k.attile[:, g, 0:t.m, r, :], at_ps[:, 0:t.m * P].rearrange("p (j c) -> p j c", c=P),
                                   ACT.Copy, accum_out=k.degp[:, g, bass.ds(b, 1)]).then_inc(s["at_kept"], 1)
                    message(group(b, r, g, 1))

            looped(act, NB, EU, step)
            message(group(*last))

        @block.gpsimd
        def _(pool):
            def lanes(t):
                pool.wait_ge(s["lanes"], t.n + 1)
                wait(pool, s["summed"], t.n - EU + 1)
                own = k.oh[:, t.g, 0:t.m, 0, :]
                pool.tensor_tensor(k.ohf[:, t.q, 0:t.m, :], own, own, ALU.mult).then_inc(s["lanes_f"], 1)

            def step(b, r):
                for g in range(SG):
                    lanes(group(b, r, g))

            looped(pool, NB, EU, step)

        @block.vector
        def _(dve):
            def lanes(t):
                if t is None:
                    return
                if t.g == 0:
                    dve.wait_ge(strip[t.r], strip_loaded(t.b, t.r))
                wait(dve, s["at_sum"], t.n - SG + 1)
                wait(dve, s["lanes_f"], t.n - SG + 1)
                val = k.strip[:, t.r, GT * t.g:GT * t.g + t.m, C_SLO:C_DLO + 1]
                dve.tensor_tensor(k.oh[:, t.g, 0:t.m, :, :],
                                  k.iota[:, :].unsqueeze(1).unsqueeze(1).to_broadcast([P, t.m, 2, P]),
                                  val.unsqueeze(3).to_broadcast([P, t.m, 2, P]), ALU.is_equal).then_inc(s["lanes"], 1)

            def presum(t):
                if t is None:
                    return
                dve.wait_ge(s["gathered"], t.n + 1)
                wait(dve, s["message"], t.n - EU + 1)
                dve.tensor_tensor(k.presum[:, t.q, 0:t.m, :], gat(t.q)[:, 0:t.m * D].rearrange("p (j f) -> p j f", f=D),
                                  k.strip[:, t.r, GT * t.g:GT * t.g + t.m, 0:D], ALU.add).then_inc(s["presum"], 1)

            def add(t):
                if t is None:
                    return
                dve.wait_ge(s["summed"], t.n + 1)
                wait(dve, s["added"], t.n)
                if t.g < SG - 1:
                    own = k.agg0[:, GT * t.g:GT * t.g + t.m, :]
                    dve.tensor_tensor(own, tot(t.q)[:, 0:t.m, :], own, ALU.add).then_inc(s["added"], 1)
                else:
                    link = Chain(dve, s["e_c"], t.b)
                    own = k.agg0[:, GT * t.g:GT * t.g + t.m - 1, :]
                    link(dve.tensor_tensor(own, tot(t.q)[:, 0:t.m - 1, :], own, ALU.add))
                    own = block_of(k.agg0, t.b)
                    dve.tensor_tensor(own, tot(t.q)[:, t.m - 1, :], own, ALU.add).then_inc(s["added"], 1)

            def step(b, r):
                for g in range(SG):
                    lanes(group(b, r, g, -1))
                    presum(group(b, r, g, 1))
                    add(group(b, r, g, 3))

            lanes(group(0, 0, 0))
            looped(dve, NB, EU, step)
            presum(group(*last))
            for back in (2, 1, 0):
                add(group(*last, back))
            for g in range(SG - 1):
                dve.wait_ge(a_out[g], 16 * NB)
                dve.memset(k.atile[g], 0.0)



def drained(pool, sem):
    pool.wait_ge(sem, 16)
    pool.dma_reset(range(sem.num, sem.num + 1))
    pool.sem_clear(sem)


def overflow_ends(pool, k, i, sem):
    pool.dma_start(k.ovmeta[:, :], k.rows_d[bass.ds(i + OVB, 1), C_SRC:C_DST + 1].bitcast(I32)).then_inc(sem, 16)
    drained(pool, sem)
    return pool.value_load(k.ovmeta[0:1, 0:1]), pool.value_load(k.ovmeta[0:1, 1:2])


def overflow_sum(pool, k, sem, transposed):
    nov = pool.value_load(k.nov[0:1, 0:1])
    with pool.If(nov > 0):
        pool.dma_start(node_rows(k.z_d), k.zf[:, :, :]).then_inc(sem, 16)
        drained(pool, sem)
        with pool.Fori(0, nov) as i:
            src, dst = overflow_ends(pool, k, i, sem)
            frm, to = (dst, src) if transposed else (src, dst)
            pool.dma_start(k.ov_d[bass.ds(to, 1), :], k.z_d[bass.ds(frm, 1), :], accum_op=ALU.add).then_inc(sem, 16)
            drained(pool, sem)
        overflow_take(pool, k, sem)


def overflow_take(pool, k, sem):
    pool.dma_start(k.ovf[:, :, :], node_rows(k.ov_d)).then_inc(sem, 16)
    drained(pool, sem)
    pool.dma_start(node_rows(k.ov_d), k.zeros[:, :].unsqueeze(1).to_broadcast([P, NB, D])).then_inc(sem, 16)
    drained(pool, sem)


def first_overflow(nc, k):
    sem, step = k.sem("ov_dma"), k.sem("ov_step")
    with nc.Block() as block:

        @block.gpsimd
        def _(pool):
            def link(ins):
                ins.then_inc(step, 1)
                pool.wait_ge(step, 1)
                pool.sem_clear(step)

            nov = pool.value_load(k.nov[0:1, 0:1])
            with pool.If(nov > 0):
                pool.dma_start(node_rows(k.z_d), k.zf[:, :, :]).then_inc(sem, 16)
                drained(pool, sem)
                with pool.Fori(0, nov) as i:
                    src, dst = overflow_ends(pool, k, i, sem)
                    pool.dma_start(k.ovrow[:, :], k.rows_d[bass.ds(i + OVB, 1), 0:D]).then_inc(sem, 16)
                    drained(pool, sem)
                    pool.dma_start(k.ovp[:, :], k.z_d[bass.ds(dst, 1), :]).then_inc(sem, 16)
                    drained(pool, sem)
                    link(pool.tensor_tensor(k.ovmsg[:, :], k.ovrow[:, :], k.ovp[:, :], ALU.add))
                    link(pool.tensor_scalar(k.ovmsg[:, :], k.ovmsg[:, :], 0.0, None, ALU.max))
                    pool.dma_start(k.ov_d[bass.ds(src, 1), :], k.ovmsg[:, :], accum_op=ALU.add).then_inc(sem, 16)
                    drained(pool, sem)
                    pool.dma_start(k.degov_d[bass.ds(dst, 1), :], k.one1[:, :], accum_op=ALU.add).then_inc(sem, 16)
                    drained(pool, sem)
                pool.dma_start(k.ovf[:, :, :], node_rows(k.ov_d)).then_inc(sem, 16)
                drained(pool, sem)
                with nc.allow_non_contiguous_dma(reason="one word per node, with overflow edges only"):
                    pool.dma_start(k.degov[:, :], k.degov_d.rearrange("(b p) f -> p (b f)", p=P)).then_inc(sem, 16)
                drained(pool, sem)
                link(pool.memset(k.zf[:, :, :], 0.0))
                pool.dma_start(node_rows(k.ov_d), k.zf[:, :, :]).then_inc(sem, 16)
                drained(pool, sem)



def strip_buffers(k):
    k.loaded = [k.sem(f"l_strip{q}") for q in range(NS)]
    k.kept = {b: k.sem(f"l_kept{b}") for b in (*range(NS), NB - 1)}
    arena = k.arena[:, 0:(2 * NS - 1) * J * P // 2].bitcast(BF16).rearrange("p (s j) -> p s j", s=2 * NS - 1)
    k.stream = [arena[:, q, :] for q in range(NS)]
    k.stay = dict(zip(k.kept, (arena[:, NS, :], k.strip_h[:, :], k.strip_agg[:, :], arena[:, NS + 1, :], arena[:, NS + 2, :])))
    k.early = [0]
    assert NS + NS * ((NB - 1 - NS) // NS) == NB - 1


def load_strip(sp, matrix, b, to, sem):
    sp.dma_start(to, matrix[bass.ds(b, 1), :, :].rearrange("o p c -> p (o c)")).then_inc(sem, 16)


def node_stage(nc, k):
    s = {n: k.sem(n) for n in ("n_cat", "n_tr", "n_trs", "n_mm", "n_ln", "n_std", "n_in", "n_tr2", "n_trs2", "n_mm2",
                               "n_z", "n_split", "n_c", "n_u", "n_deg", "n_root")}
    steps = NB // BN
    assert steps * BN == NB
    halves = [(0, BN // 2 + 1), (BN // 2 + 1, BN)]
    tr, tr2, mm, mm2 = k.bank[0:2], k.bank[2:4], k.bank[4:6], k.bank[6]
    at = [(NS + 1) * J * P // 2]

    def take(*shape):
        n = shape[0] * (shape[1] if len(shape) > 1 else 1)
        part = k.arena[:, at[0]:at[0] + n]
        at[0] += n
        return part.rearrange("p (b f) -> p b f", b=BN) if len(shape) > 1 else part

    cat, catT, lin, linT = take(BN, P), take(BN, P), take(BN, D), take(BN, P)
    agg, rem, st6, mv, std, rstd = take(BN, D), take(BN, D), take(BN, 6), take(BN, 2), take(BN), take(BN)
    w0 = k.wl[:, 0, :]

    def own(i):
        return bass.ds(i * BN, BN)

    def by_block(bank):
        return bank[:, 0:BN * D].rearrange("p (b f) -> p b f", f=D)

    with nc.Block() as block:

        @block.sync
        def _(sp):
            for b in k.early:
                load_strip(sp, k.a_d, b, k.stay[b], k.kept[b])
            for q in range(NS):
                load_strip(sp, k.a_d, NS + q, k.stream[q], k.loaded[q])

        @block.tensor
        def _(pe):
            def first(i, q):
                pe.wait_ge(s["n_cat"], i + 1)
                wait(pe, s["n_trs"], 2 * i)
                for x, (lo, hi) in enumerate(halves):
                    for b in range(lo, hi):
                        ins = pe.transpose(tr[x][:, (b - lo) * P:(b - lo + 1) * P], cat[:, b, :], k.ident[:, :])
                    ins.then_inc(s["n_tr"], 1)
                for x, (lo, hi) in enumerate(halves):
                    pe.wait_ge(s["n_trs"], 2 * i + x + 1)
                    for b in range(lo, hi):
                        ins = pe.matmul(mm[q][:, D * b:D * (b + 1)], catT[:, b, :], k.w2na[:, :], start=True, stop=True)
                ins.then_inc(s["n_mm"], 1)

            def second(i, q):
                wait_apart(pe, s["n_in"], i + 1)
                for x, (lo, hi) in enumerate(halves):
                    for b in range(lo, hi):
                        ins = pe.transpose(tr2[x][0:D, (b - lo) * P:(b - lo + 1) * P], lin[:, b, :], k.ident[:, :])
                    ins.then_inc(s["n_tr2"], 1)
                for x, (lo, hi) in enumerate(halves):
                    pe.wait_ge(s["n_trs2"], 2 * i + x + 1)
                    for b in range(lo, hi):
                        ins = pe.matmul(mm2[:, D * b:D * (b + 1)], linT[0:D, b, :], w0, start=True, stop=True)
                ins.then_inc(s["n_mm2"], 1)

            def step(i, q):
                first(i + 1, 1 - q)
                second(i, q)

            first(0, 0)
            looped(pe, steps - 1, 2, step)
            second(steps - 1, (steps - 1) % 2)

        @block.scalar
        def _(act):
            act.wait_ge(s["n_deg"], 1)
            act.activation(k.dinv1[:, :], k.dtmp[:, :], ACT.Sqrt).then_inc(s["n_root"], 1)
            act.wait_ge(s["n_deg"], 2)
            act.activation(k.dinv3[:, :], k.degp[:, 0, :], ACT.Sqrt).then_inc(s["n_root"], 1)

            def first(i):
                for x, (lo, hi) in enumerate(halves):
                    act.wait_ge(s["n_tr"], 2 * i + x + 1)
                    if x == 0:
                        wait(act, s["n_mm"], i)
                    act.copy(catT[:, lo:hi, :].rearrange("p b c -> p (b c)"), tr[x][:, 0:(hi - lo) * P]
                             ).then_inc(s["n_trs"], 1)

            def second(i):
                act.wait_ge(s["n_ln"], i + 1)
                act.activation(std, mv[:, :, 1], ACT.Sqrt, bias=k.epsc[:, :]).then_inc(s["n_std"], 1)
                for x, (lo, hi) in enumerate(halves):
                    act.wait_ge(s["n_tr2"], 2 * i + x + 1)
                    act.copy(linT[0:D, lo:hi, :].rearrange("p b c -> p (b c)"), tr2[x][0:D, 0:(hi - lo) * P]
                             ).then_inc(s["n_trs2"], 1)

            def step(i, q):
                first(i + 1)
                second(i)

            first(0)
            looped(act, steps - 1, 2, step)
            second(steps - 1)

        @block.vector
        def _(dve):
            def gather(i):
                wait_apart(dve, s["n_tr"], 2 * i)
                dve.tensor_scalar(cat[:, :, 0:D], k.h0[:, own(i), :], 1.0, None, ALU.mult)
                dve.tensor_tensor(cat[:, :, D:2 * D], k.agg0[:, own(i), :], k.ovf[:, own(i), :], ALU.add
                                  ).then_inc(s["n_cat"], 1)

            def update(i, q):
                link = Chain(dve, s["n_u"], UL * i)
                x = k.xres[:, own(i), :]
                dve.wait_ge(s["n_mm"], i + 1)
                link(dve.tensor_tensor(agg, by_block(mm[q]), k.c2[:, :].unsqueeze(1).to_broadcast([P, BN, D]), ALU.add))
                link(dve.scalar_tensor_tensor(x, agg, 0.0, x, ALU.max, ALU.add), apart=True)
                for b in range(BN):
                    ins = dve.bn_stats(st6[:, b, :], block_of(k.xres, i * BN + b))
                link(ins, apart=True)
                for b in range(BN):
                    ins = dve.bn_aggr(mv[:, b, :], st6[:, b, :])
                ins.then_inc(s["n_ln"], 1)
                link(dve.tensor_scalar(agg, x, 1.0, None, ALU.mult))
                dve.wait_ge(s["n_ln"], i + 1)
                link(dve.tensor_tensor(agg, agg, mv[:, :, 0:1].to_broadcast([P, BN, D]), ALU.subtract))
                dve.wait_ge(s["n_std"], i + 1)
                link(dve.reciprocal(rstd, std))
                link(dve.tensor_tensor(agg, agg, rstd.unsqueeze(2).to_broadcast([P, BN, D]), ALU.mult))
                wait(dve, s["n_tr2"], 2 * i)
                dve.tensor_scalar(lin, agg, 0.0, None, ALU.max).then_inc(s["n_in"], 1)
                assert link.n == UL

            def table(i):
                dve.wait_ge(s["n_mm2"], i + 1)
                dve.tensor_tensor(k.zf[:, own(i), :], by_block(mm2),
                                  k.dinv1[:, own(i)].unsqueeze(2).to_broadcast([P, BN, D]), ALU.mult
                                  ).then_inc(s["n_z"], 1)

            def step(i, q):
                gather(i + 1)
                if not (isinstance(i, int) and i == 0):
                    table(i - 1)
                update(i, q)

            UL = 7
            gather(0)
            link = Chain(dve, s["n_c"], 0)
            link(dve.tensor_reduce(k.deg[:, :], k.degp[:, :, :].rearrange("p g b -> p b g"), AX, ALU.add))
            link(dve.tensor_tensor(k.deg[:, :], k.deg[:, :], k.degov[:, :], ALU.add))
            dve.tensor_scalar(k.dtmp[:, :], k.deg[:, :], 1.0, None, ALU.max).then_inc(s["n_deg"], 1)
            dve.tensor_scalar(k.degp[:, 0, :], k.deg[:, :], 1.0, None, ALU.add).then_inc(s["n_deg"], 1)
            link(dve.tensor_scalar(k.deg[:, :], k.deg[:, :], 0.0, None, ALU.is_gt))
            dve.wait_ge(s["n_root"], 2)
            link(dve.reciprocal(k.dinv1[:, :], k.dinv1[:, :]))
            link(dve.tensor_tensor(k.dinv1[:, :], k.dinv1[:, :], k.deg[:, :], ALU.mult))
            link(dve.reciprocal(k.dinv3[:, :], k.dinv3[:, :]))
            looped(dve, steps - 1, 2, step)
            table(steps - 2)
            update(steps - 1, (steps - 1) % 2)
            table(steps - 1)

        @block.gpsimd
        def _(pool):
            def split(i, q):
                wait_apart(pool, s["n_z"], i + 1)
                sub = Chain(pool, s["n_split"], 4 * i)
                sub(split3(pool, sub, k.zf[:, own(i), :], rem, [k.z3b[:, own(i), x, :] for x in range(PARTS)]))

            looped(pool, steps, 2, split)



def layers(nc, k):
    gcn1 = dict(matrix="a", dinv=k.dinv1, loop=False)
    gcn3 = dict(matrix="a", dinv=k.dinv3, loop=True)
    plan = [
        dict(gcn1, bias=2, then="linear", w=k.wl[:, 1, :], out_dinv=k.dinv1),
        dict(gcn1, bias=3, then="linear", w=k.wl[:, 2, :], out_dinv=k.dinv1),
        dict(gcn1, bias=4, then="norm"),
        dict(matrix="at", dinv=None, loop=False, bias=None, then="norm linear", w=k.wl[:, 3, :], out_dinv=k.dinv3),
        dict(gcn3, bias=5, then="linear", w=k.wl[:, 4, :], out_dinv=k.dinv3),
        dict(gcn3, bias=6, then="linear", w=k.w3[:, :], out_dinv=k.dinv3),
        dict(gcn3, bias=7, then="out"),
    ]
    linear = norms = resident_loads = 0
    for n, spec in enumerate(plan):
        spec["n"], spec["n0"], spec["lin0"], spec["ln0"] = n, n * NB, linear * NB, norms * NB
        spec["has_linear"], spec["has_norm"], spec["is_out"] = (x in spec["then"] for x in ("linear", "norm", "out"))
        spec["fresh"] = n == 0 or spec["matrix"] != plan[n - 1]["matrix"]
        resident_loads += spec["fresh"]
        spec["resident_loads"] = resident_loads
        linear += spec["has_linear"]
        norms += spec["has_norm"]
    s = {n: k.sem("l_" + n) for n in ("ov", "sum", "ready", "tr", "trs", "mm", "z", "ln", "std", "ovdma")}
    out = [k.sem(f"l_out{q}") for q in range(2)]
    chain, splits = [k.sem(f"l_c{n}") for n in range(len(plan))], [k.sem(f"l_k{n}") for n in range(len(plan))]

    stream, stay, loaded, kept, streamed = k.stream, k.stay, k.loaded, k.kept, (NB - 1 - NS) // NS
    acc, tr, mm = k.bank[0:4] + k.bank[7:8], k.bank[4], k.bank[5:7]

    def acc_of(b, u):
        return acc[4 if isinstance(b, int) and b == NB - 1 else u][:, 0:ZW]

    with nc.Block() as block:

        @block.sync
        def _(sp):
            for spec in plan:
                n0 = spec["n0"]
                matrix = k.a_d if spec["matrix"] == "a" else k.at_d

                if spec["fresh"]:
                    for b in range(NS):
                        wait(sp, s["sum"], n0 - NB + b + 1)
                        if n0 or b not in k.early:
                            load_strip(sp, matrix, b, stay[b], kept[b])
                for q in range(NS if n0 else 0):
                    wait(sp, s["sum"], n0 - NS + q)
                    load_strip(sp, matrix, NS + q, stream[q], loaded[q])
                if spec["fresh"]:
                    wait(sp, s["sum"], n0)
                    load_strip(sp, matrix, NB - 1, stay[NB - 1], kept[NB - 1])

                def step(b, q):
                    sp.wait_ge(s["sum"], n0 + b + NS + 1)
                    load_strip(sp, matrix, b + 2 * NS, stream[q], loaded[q])

                looped(sp, NB - 1 - 2 * NS, NS, step)

        @block.tensor
        def _(pe):
            for spec in plan:
                n, n0, lin0 = spec["n"], spec["n0"], spec["lin0"]
                z3 = k.z3b if n % 2 == 0 else k.z3a

                def part(b, u, lo, hi):
                    strip = stay[b] if isinstance(b, int) and b in stay else stream[u]
                    for a in range(lo, hi):
                        rhs = z3[:, a, :, :] if a < NB else z3[:, bass.ds(b, 1), :, :].rearrange("p o i f -> p (o i) f")
                        ins = pe.matmul(acc_of(b, u), strip[:, a * P:(a + 1) * P], rhs.rearrange("p i f -> p (i f)"),
                                        start=(a == 0), stop=(a == J - 1))
                    return ins

                def turn(b, q):
                    if spec["has_linear"]:
                        wait_apart(pe, s["ready"], n0 + b + 1)
                        pe.transpose(tr[0:D, 0:P], k.lin_in[:, q, :], k.ident[:, :]).then_inc(s["tr"], 1)

                def linear(b, q):
                    if spec["has_linear"]:
                        pe.wait_ge(s["trs"], lin0 + b + 1)
                        pe.matmul(mm[q][:, 0:D], k.linT[:, :], spec["w"], start=True, stop=True).then_inc(s["mm"], 1)

                def strip_there(b, u):
                    if isinstance(b, int) and b in stay:
                        pe.wait_ge(kept[b], 16 * spec["resident_loads"])
                    else:
                        pe.wait_ge(loaded[u], 16 * n * streamed + (16 * (b // NS) if isinstance(b, int)
                                                                      else (b - u) * (16 // NS)))

                def step(b, u):
                    if isinstance(b, int) and b < 2:
                        return
                    strip_there(b, u)
                    if not (isinstance(b, int) and b < NS):
                        pe.wait_ge(s["ready"], n0 + b - NS + 1)
                    if isinstance(b, int) and b == 2:
                        part(b, u, 0, J // 4)
                        turn(0, 0)
                        part(b, u, J // 4, J // 2)
                        linear(0, 0)
                        part(b, u, J // 2, LATE)
                    else:
                        part(b, u, 0, LATE)
                    turn(b - 1, (u - 1) % 2)
                    part(b, u, LATE, J).then_inc(s["sum"], 1)
                    linear(b - 1, (u - 1) % 2)

                wait(pe, splits[n - 1], 4 * (NB - TAIL) if n else 0)
                for b in (0, 1):
                    strip_there(b, b)
                    part(b, b, 0, NB - TAIL)
                wait(pe, splits[n - 1], 4 * NB if n else 0)
                for b in (0, 1):
                    part(b, b, NB - TAIL, J).then_inc(s["sum"], 1)
                looped(pe, NB, NS, step)
                turn(NB - 1, (NB - 1) % 2)
                linear(NB - 1, (NB - 1) % 2)

        @block.scalar
        def _(act):
            for spec in plan:
                n0, lin0, ln0 = spec["n0"], spec["lin0"], spec["ln0"]

                def step(b, q):
                    if spec["has_norm"]:
                        act.wait_ge(s["ln"], ln0 + b + 1)
                        act.activation(k.std[:, :], k.mv[:, 1:2], ACT.Sqrt, bias=k.epsc[:, :]).then_inc(s["std"], 1)
                    if spec["has_linear"]:
                        act.wait_ge(s["tr"], lin0 + b + 1)
                        act.copy(k.linT[:, :], tr[0:D, 0:P]).then_inc(s["trs"], 1)

                def store(b, q, rows):
                    act.wait_ge(s["ready"], n0 + b + 1)
                    act.dma_start(k.inp["out"][bass.ds(b * P, rows), :], k.outb[0:rows, q, :]).then_inc(out[q], 16)

                if spec["is_out"]:
                    looped(act, NB - 1, 2, lambda b, q: store(b, q, P))
                    store(NB - 1, (NB - 1) % 2, LAST)
                    for q in range(2):
                        act.wait_ge(out[q], 16 * len(range(q, NB, 2)))
                else:
                    looped(act, NB, 2, step)

        @block.vector
        def _(dve):
            for spec in plan:
                n, n0, lin0, ln0 = spec["n"], spec["n0"], spec["lin0"], spec["ln0"]
                links = 2 + spec["loop"] + (spec["dinv"] is not None) + 4 * spec["has_norm"]

                def epilogue(b, u):
                    q = u % 2
                    link = Chain(dve, chain[n], b * links)
                    own = bass.ds(b, 1)
                    x, agg = block_of(k.xres, b), k.aggt[:, q, :]
                    dve.wait_ge(s["sum"], n0 + b + 1)
                    link(dve.tensor_reduce(agg, acc_of(b, u).rearrange("p (i f) -> p f i", i=PARTS), AX, ALU.add))
                    if isinstance(b, int) and b == 0:
                        dve.wait_ge(s["ov"], n + 1)
                    link(dve.tensor_tensor(agg, agg, block_of(k.ovf, b), ALU.add))
                    if spec["loop"]:
                        link(dve.tensor_tensor(agg, agg, block_of(k.zf, b), ALU.add))
                    if spec["dinv"] is not None:
                        link(dve.scalar_tensor_tensor(agg, agg, spec["dinv"][:, own], k.bias[:, spec["bias"], :],
                                                      ALU.mult, ALU.add))
                    if spec["is_out"]:
                        wait(dve, out[q], 16 * (b // 2) if isinstance(b, int) else (b - q) * 8)
                        dve.tensor_tensor(k.outb[:, q, :], agg, x, ALU.add).then_inc(s["ready"], 1)
                    elif not spec["has_norm"]:
                        dve.tensor_scalar(k.lin_in[:, q, :], agg, 0.0, None, ALU.max).then_inc(s["ready"], 1)
                    else:
                        if spec["dinv"] is not None:
                            link(dve.scalar_tensor_tensor(x, agg, 0.0, x, ALU.max, ALU.add), apart=True)
                        else:
                            link(dve.tensor_tensor(x, agg, x, ALU.add), apart=True)
                        dst = k.lin_in[:, q, :] if spec["has_linear"] else block_of(k.zf, b)
                        layer_norm(dve, s["ln"], s["std"], ln0 + b + 1, link, k, x, dst).then_inc(s["ready"], 1)
                    assert link.n == links, (link.n, links)

                def table(b, q):
                    if spec["has_linear"]:
                        dve.wait_ge(s["mm"], lin0 + b + 1)
                        dve.tensor_scalar(block_of(k.zf, b), mm[q][:, 0:D], spec["out_dinv"][:, bass.ds(b, 1)], None,
                                          ALU.mult).then_inc(s["z"], 1)

                def step(b, u):
                    if isinstance(b, int) and b == 2:
                        table(0, 0)
                    epilogue(b, u)
                    if not (isinstance(b, int) and b < 2):
                        table(b - 1, (u - 1) % 2)

                looped(dve, NB, NS, step)
                table(NB - 1, (NB - 1) % 2)

        @block.gpsimd
        def _(pool):
            for spec in plan:
                n, z3n = spec["n"], k.z3a if spec["n"] % 2 == 0 else k.z3b
                overflow_sum(pool, k, s["ovdma"], spec["matrix"] == "at")
                pool.sem_inc(s["ov"], 1)

                def split(b, q):
                    if spec["has_linear"]:
                        wait_apart(pool, s["z"], spec["lin0"] + b + 1)
                    else:
                        wait_apart(pool, s["ready"], spec["n0"] + b + 1)
                    sub = Chain(pool, splits[n], 4 * b)
                    sub(split3(pool, sub, block_of(k.zf, b), k.rem[:, :], parts_of(z3n, b)))

                if not spec["is_out"]:
                    looped(pool, NB, 2, split)


CAPO = CAP
CAPD = 2 * CAP
WLOADS = 1 + GT + 3 + 5 + 8 + 1

_INS = ["x", "L0_gnn_W1", "L0_gnn_W2", "L1_gnn_W0", "L1_gnn_W1", "L1_gnn_W2", "L3_gnn_W1", "L3_gnn_W2", "L3_gnn_W3",
        "L0_gnn_b1", "L0_gnn_b2", "L1_gnn_b0", "L1_gnn_b1", "L1_gnn_b2", "L3_gnn_b1", "L3_gnn_b2", "L3_gnn_b3"]


def kernel(**inputs):
    import numpy as np
    import concourse.bacc as bacc
    from concourse.bass_utils import run_bass_kernel_spmd

    arrays = {name: np.ascontiguousarray(inputs[name]) for name in _INS}
    for name in ("src", "dst"):
        padded = np.full((EP,), PADNODE, np.int32)
        padded[:E] = np.asarray(inputs[name])
        arrays[name] = padded.reshape(P, T)
    attrs = np.zeros((EP, FE), np.float32)
    attrs[:E] = np.asarray(inputs["edge_attr_32"])
    attrs = attrs.reshape(P, NG, GT, FE).transpose(1, 2, 3, 0)
    arrays["attr_T"] = np.ascontiguousarray(attrs).reshape(NG, P, P)
    arrays["u0_in"] = np.ascontiguousarray(np.asarray(inputs["L0_gnn_u"])[0:1].T)

    nc = bacc.Bacc("TRN2", target_bir_lowering=False, num_devices=1)
    t = {n: nc.dram_tensor(f"in_{n}", a.shape, mybir.dt.from_np(a.dtype), kind="ExternalInput").ap()
         for n, a in arrays.items()}
    t["out"] = nc.dram_tensor("out_x", (N, D), F32, kind="ExternalOutput").ap()
    build(nc, t)
    r = run_bass_kernel_spmd(nc, [{f"in_{n}": a for n, a in arrays.items()}], core_ids=[0])
    return r.results[0]["out_x"]
```
